# Optimizing a Trainium2 kernel written in Bass

```python
import numpy as np
import jax
import jax.numpy as jnp

def _softmax(x, axis=-1):
    return jax.nn.softmax(x, axis=axis)

def _gelu(x):
    return jax.nn.gelu(x, approximate=True)

def _silu(x):
    return jax.nn.silu(x)

def _sigmoid(x):
    return jax.nn.sigmoid(x)

def _layernorm(x, axis=-1, eps=1e-05):
    m = jnp.mean(x, axis=axis, keepdims=True)
    v = jnp.var(x, axis=axis, keepdims=True)
    return (x - m) / jnp.sqrt(v + eps)

def _scatter_add(tgt, idx, src, axis=0):
    return tgt.at[idx].add(src)

def _segment_sum(src, seg, n):
    return jax.ops.segment_sum(src, seg, n)
kernel_name = 'mk_decoder_preln_d1_seqx_r4_0d772a'

def setup_inputs(seed: int=0):
    np.random.seed(seed)
    _w = jnp.asarray

    def _rec_inputs():
        import jax
        import jax.numpy as jnp
        _rk = jax.random.key(seed)
        x = -0.0002928 + 1 * jax.random.normal(jax.random.fold_in(_rk, 1), (8, 512, 256), jnp.float32)
        _lenS = 512 - jax.random.randint(jax.random.fold_in(_rk, 7), (8,), 0, max(1, 512 // 4) + 1, jnp.int32)
        _lenS2 = 512 - jax.random.randint(jax.random.fold_in(_rk, 8), (8,), 0, max(1, 512 // 4) + 1, jnp.int32)
        _ctx_1024P = jax.random.normal(jax.random.fold_in(_rk, 11), (8, 16, 256), jnp.float32)
        _ctx_1024c = jax.random.dirichlet(jax.random.fold_in(_rk, 511), 0.3 * jnp.ones((16,), jnp.float32), (8, 512))
        _ctx_1024t = jnp.einsum('bsk,bkd->bsd', _ctx_1024c, _ctx_1024P)
        _ctx_1024t = _ctx_1024t * jax.lax.rsqrt(jnp.mean(jnp.square(_ctx_1024t)) + 1e-12) * 0.953939
        ctx_1024 = -1.39393e-06 + 0.999914 * (_ctx_1024t + 0.3 * jax.random.normal(jax.random.fold_in(_rk, 611), (8, 512, 256), jnp.float32))
        return (x, ctx_1024)
    x, ctx_1024 = _rec_inputs()

    def _L0_attn_setup():
        import jax, jax.numpy as jnp
        import numpy as np
        from jax import lax
        EPS = 1e-05

        def _rmsnorm(x, w):
            return x * lax.rsqrt(jnp.mean(x * x, axis=-1, keepdims=True) + EPS) * w

        def _mamba_block(u, W_in, conv_w, conv_b, W_x, W_dt, b_dt, A_log, Dp, W_out):
            ED, K = conv_w.shape
            R = W_dt.shape[0]
            N = A_log.shape[1]
            L = u.shape[1]
            xz = u @ W_in
            xs, z = (xz[..., :ED], xz[..., ED:])
            xc = lax.conv_general_dilated(xs.transpose(0, 2, 1), conv_w[:, None, :], window_strides=(1,), padding=[(K - 1, 0)], feature_group_count=ED) + conv_b[None, :, None]
            xc = jax.nn.silu(xc).transpose(0, 2, 1)
            dbc = xc @ W_x
            dt, Bm, Cm = (dbc[..., :R], dbc[..., R:R + N], dbc[..., R + N:])
            delta = jax.nn.softplus(dt @ W_dt + b_dt)
            A = -jnp.exp(A_log)
            dA = jnp.exp(delta[..., None] * A)
            dBx = delta[..., None] * Bm[:, :, None, :] * xc[..., None]

            def comb(c1, c2):
                a1, b1 = c1
                a2, b2 = c2
                return (a1 * a2, a2 * b1 + b2)
            _, h = lax.associative_scan(comb, (dA, dBx), axis=1)
            y = jnp.einsum('blen,bln->ble', h, Cm) + Dp * xc
            y = y * jax.nn.silu(z)
            return y @ W_out
        key = jax.random.key(seed)
        B, L, D = (1, 256, 256)
        ED, N, R, K = (2 * D, 16, 64, 4)
        ks = jax.random.split(key, 8)
        s = 0.02
        return {'x': jax.random.normal(ks[0], (B, L, D), dtype=jnp.float32), 'rms_w': jnp.ones((D,), jnp.float32), 'W_in': jax.random.normal(ks[1], (D, 2 * ED), jnp.float32) * s, 'conv_w': jax.random.normal(ks[2], (ED, K), jnp.float32) * s, 'conv_b': jnp.zeros((ED,), jnp.float32), 'W_x': jax.random.normal(ks[3], (ED, R + 2 * N), jnp.float32) * s, 'W_dt': jax.random.normal(ks[4], (R, ED), jnp.float32) * s, 'b_dt': jax.random.normal(ks[5], (ED,), jnp.float32) * 0.1, 'A_log': jnp.broadcast_to(jnp.log(jnp.arange(1, N + 1, dtype=jnp.float32)), (ED, N)).copy(), 'Dp': jnp.ones((ED,), jnp.float32), 'W_out': jax.random.normal(ks[6], (ED, D), jnp.float32) * s, 'ln_w': jnp.ones((D,), jnp.float32), 'ln_b': jnp.zeros((D,), jnp.float32)}
    _L0_attn_all = _L0_attn_setup()
    _L0_attn_in = {k: v for k, v in _L0_attn_all.items() if k in ('rms_w', 'W_in', 'conv_w', 'conv_b', 'W_x', 'W_dt', 'b_dt', 'A_log', 'Dp', 'W_out', 'ln_w', 'ln_b')}
    del _L0_attn_all

    def _L0_xattn_setup():
        import jax, jax.numpy as jnp
        import numpy as np
        B, S, H, NH = (2, 512, 256, 4)
        DH = H // NH
        EPS_BACKEND = 1e-06
        EPS_LN = 1e-06

        def _mlstm_parallel_stabilized(q, k, v, igate_preact, fgate_preact):
            b, nh, s, dh = q.shape
            log_fg = jax.nn.log_sigmoid(fgate_preact)
            cs = jnp.concatenate([jnp.zeros((b, nh, 1), q.dtype), jnp.cumsum(log_fg[..., 0], axis=2)], axis=2)
            fg_matrix = cs[:, :, :, None] - cs[:, :, None, :]
            fg_matrix = fg_matrix[:, :, 1:, 1:]
            causal = jnp.tril(jnp.ones((s, s), dtype=bool))
            log_fg_matrix = jnp.where(causal, fg_matrix, -jnp.inf)
            log_D = log_fg_matrix + jnp.swapaxes(igate_preact, -2, -1)
            max_log_D = jnp.max(log_D, axis=-1, keepdims=True)
            D = jnp.exp(log_D - max_log_D)
            qk = jnp.einsum('bhsd,bhtd->bhst', q, k) / jnp.sqrt(jnp.asarray(dh, q.dtype))
            C = qk * D
            normalizer = jnp.maximum(jnp.abs(jnp.sum(C, axis=-1, keepdims=True)), jnp.exp(-max_log_D))
            C_norm = C / (normalizer + EPS_BACKEND)
            return jnp.einsum('bhst,bhtd->bhsd', C_norm, v)

        def _multihead_layernorm(x, scale):
            mean = jnp.mean(x, axis=-1, keepdims=True)
            var = jnp.var(x, axis=-1, keepdims=True)
            xn = (x - mean) * jax.lax.rsqrt(var + EPS_LN)
            return xn * scale.reshape(NH, 1, DH)
        key = jax.random.key(seed)
        kq, kk, kv, kib = jax.random.split(key, 4)
        q = jax.random.normal(kq, (B, S, H), dtype=jnp.float32)
        k = jax.random.normal(kk, (B, S, H), dtype=jnp.float32)
        v = jax.random.normal(kv, (B, S, H), dtype=jnp.float32)
        igate_kernel = jnp.zeros((3 * H, NH), dtype=jnp.float32)
        igate_bias = 0.1 * jax.random.normal(kib, (NH,), dtype=jnp.float32)
        fgate_kernel = jnp.zeros((3 * H, NH), dtype=jnp.float32)
        fgate_bias = jnp.linspace(3.0, 6.0, NH, dtype=jnp.float32)
        outnorm_scale = jnp.ones((H,), dtype=jnp.float32)
        return {'q': q, 'k': k, 'v': v, 'igate_kernel': igate_kernel, 'igate_bias': igate_bias, 'fgate_kernel': fgate_kernel, 'fgate_bias': fgate_bias, 'outnorm_scale': outnorm_scale}
    _L0_xattn_all = _L0_xattn_setup()
    _L0_xattn_in = {k: v for k, v in _L0_xattn_all.items() if k in ('igate_kernel', 'igate_bias', 'fgate_kernel', 'fgate_bias', 'outnorm_scale')}
    del _L0_xattn_all

    def _L0_ffn_setup():
        import jax, jax.numpy as jnp
        import numpy as np
        DIM = 256
        HIDDEN = 768
        SCALE = 1.0 / 127.0

        def _dequant(w_int, dtype):
            return w_int.astype(dtype) * jnp.asarray(SCALE, dtype)
        key = jax.random.key(seed)
        k_x, k_g, k_u, k_d = jax.random.split(key, 4)
        x = jax.random.normal(k_x, (4, 512, DIM), dtype=jnp.float32)
        w_gate = jax.random.randint(k_g, (HIDDEN, DIM), -127, 128, dtype=jnp.int32)
        w_up = jax.random.randint(k_u, (HIDDEN, DIM), -127, 128, dtype=jnp.int32)
        w_down = jax.random.randint(k_d, (DIM, HIDDEN), -127, 128, dtype=jnp.int32)
        return {'x': x, 'w_gate': w_gate, 'w_up': w_up, 'w_down': w_down}
    _L0_ffn_all = _L0_ffn_setup()
    _L0_ffn_in = {k: v for k, v in _L0_ffn_all.items() if k in ('w_gate', 'w_up', 'w_down')}
    del _L0_ffn_all
    return {'x': x, 'ctx_1024': ctx_1024, 'L0_attn_rms_w': _L0_attn_in['rms_w'], 'L0_attn_W_in': _L0_attn_in['W_in'], 'L0_attn_conv_w': _L0_attn_in['conv_w'], 'L0_attn_conv_b': _L0_attn_in['conv_b'], 'L0_attn_W_x': _L0_attn_in['W_x'], 'L0_attn_W_dt': _L0_attn_in['W_dt'], 'L0_attn_b_dt': _L0_attn_in['b_dt'], 'L0_attn_A_log': _L0_attn_in['A_log'], 'L0_attn_Dp': _L0_attn_in['Dp'], 'L0_attn_W_out': _L0_attn_in['W_out'], 'L0_attn_ln_w': _L0_attn_in['ln_w'], 'L0_attn_ln_b': _L0_attn_in['ln_b'], 'L0_xattn_igate_kernel': _L0_xattn_in['igate_kernel'], 'L0_xattn_igate_bias': _L0_xattn_in['igate_bias'], 'L0_xattn_fgate_kernel': _L0_xattn_in['fgate_kernel'], 'L0_xattn_fgate_bias': _L0_xattn_in['fgate_bias'], 'L0_xattn_outnorm_scale': _L0_xattn_in['outnorm_scale'], 'L0_ffn_w_gate': _L0_ffn_in['w_gate'], 'L0_ffn_w_up': _L0_ffn_in['w_up'], 'L0_ffn_w_down': _L0_ffn_in['w_down']}

def reference(x, ctx_1024, L0_attn_rms_w, L0_attn_W_in, L0_attn_conv_w, L0_attn_conv_b, L0_attn_W_x, L0_attn_W_dt, L0_attn_b_dt, L0_attn_A_log, L0_attn_Dp, L0_attn_W_out, L0_attn_ln_w, L0_attn_ln_b, L0_xattn_igate_kernel, L0_xattn_igate_bias, L0_xattn_fgate_kernel, L0_xattn_fgate_bias, L0_xattn_outnorm_scale, L0_ffn_w_gate, L0_ffn_w_up, L0_ffn_w_down):
    import jax
    import jax.numpy as jnp

    def _L0_attn_ref(x, rms_w, W_in, conv_w, conv_b, W_x, W_dt, b_dt, A_log, Dp, W_out, ln_w, ln_b):
        import jax, jax.numpy as jnp
        import numpy as np
        from jax import lax
        EPS = 1e-05

        def _rmsnorm(x, w):
            return x * lax.rsqrt(jnp.mean(x * x, axis=-1, keepdims=True) + EPS) * w

        def _mamba_block(u, W_in, conv_w, conv_b, W_x, W_dt, b_dt, A_log, Dp, W_out):
            ED, K = conv_w.shape
            R = W_dt.shape[0]
            N = A_log.shape[1]
            L = u.shape[1]
            xz = u @ W_in
            xs, z = (xz[..., :ED], xz[..., ED:])
            xc = lax.conv_general_dilated(xs.transpose(0, 2, 1), conv_w[:, None, :], window_strides=(1,), padding=[(K - 1, 0)], feature_group_count=ED) + conv_b[None, :, None]
            xc = jax.nn.silu(xc).transpose(0, 2, 1)
            dbc = xc @ W_x
            dt, Bm, Cm = (dbc[..., :R], dbc[..., R:R + N], dbc[..., R + N:])
            delta = jax.nn.softplus(dt @ W_dt + b_dt)
            A = -jnp.exp(A_log)
            dA = jnp.exp(delta[..., None] * A)
            dBx = delta[..., None] * Bm[:, :, None, :] * xc[..., None]

            def comb(c1, c2):
                a1, b1 = c1
                a2, b2 = c2
                return (a1 * a2, a2 * b1 + b2)
            _, h = lax.associative_scan(comb, (dA, dBx), axis=1)
            y = jnp.einsum('blen,bln->ble', h, Cm) + Dp * xc
            y = y * jax.nn.silu(z)
            return y @ W_out
        depth = 6
        for _ in range(depth):
            inner = _mamba_block(_rmsnorm(x, rms_w), W_in, conv_w, conv_b, W_x, W_dt, b_dt, A_log, Dp, W_out) + x
            x = inner + x
        mu = jnp.mean(x, axis=-1, keepdims=True)
        var = jnp.mean((x - mu) ** 2, axis=-1, keepdims=True)
        return (x - mu) * lax.rsqrt(var + EPS) * ln_w + ln_b

    def _L0_xattn_ref(q, k, v, igate_kernel, igate_bias, fgate_kernel, fgate_bias, outnorm_scale):
        import jax, jax.numpy as jnp
        import numpy as np
        B, S, H, NH = (2, 512, 256, 4)
        DH = H // NH
        EPS_BACKEND = 1e-06
        EPS_LN = 1e-06

        def _mlstm_parallel_stabilized(q, k, v, igate_preact, fgate_preact):
            b, nh, s, dh = q.shape
            log_fg = jax.nn.log_sigmoid(fgate_preact)
            cs = jnp.concatenate([jnp.zeros((b, nh, 1), q.dtype), jnp.cumsum(log_fg[..., 0], axis=2)], axis=2)
            fg_matrix = cs[:, :, :, None] - cs[:, :, None, :]
            fg_matrix = fg_matrix[:, :, 1:, 1:]
            causal = jnp.tril(jnp.ones((s, s), dtype=bool))
            log_fg_matrix = jnp.where(causal, fg_matrix, -jnp.inf)
            log_D = log_fg_matrix + jnp.swapaxes(igate_preact, -2, -1)
            max_log_D = jnp.max(log_D, axis=-1, keepdims=True)
            D = jnp.exp(log_D - max_log_D)
            qk = jnp.einsum('bhsd,bhtd->bhst', q, k) / jnp.sqrt(jnp.asarray(dh, q.dtype))
            C = qk * D
            normalizer = jnp.maximum(jnp.abs(jnp.sum(C, axis=-1, keepdims=True)), jnp.exp(-max_log_D))
            C_norm = C / (normalizer + EPS_BACKEND)
            return jnp.einsum('bhst,bhtd->bhsd', C_norm, v)

        def _multihead_layernorm(x, scale):
            mean = jnp.mean(x, axis=-1, keepdims=True)
            var = jnp.var(x, axis=-1, keepdims=True)
            xn = (x - mean) * jax.lax.rsqrt(var + EPS_LN)
            return xn * scale.reshape(NH, 1, DH)
        b, s, h = q.shape
        gate_in = jnp.concatenate([q, k, v], axis=-1)
        ig = gate_in @ igate_kernel + igate_bias
        fg = gate_in @ fgate_kernel + fgate_bias
        ig = jnp.transpose(ig, (0, 2, 1))[..., None]
        fg = jnp.transpose(fg, (0, 2, 1))[..., None]
        qh = jnp.transpose(q.reshape(b, s, NH, DH), (0, 2, 1, 3))
        kh = jnp.transpose(k.reshape(b, s, NH, DH), (0, 2, 1, 3))
        vh = jnp.transpose(v.reshape(b, s, NH, DH), (0, 2, 1, 3))
        hs = _mlstm_parallel_stabilized(qh, kh, vh, ig, fg)
        hn = _multihead_layernorm(hs, outnorm_scale)
        return jnp.transpose(hn, (0, 2, 1, 3)).reshape(b, s, h)

    def _L0_ffn_ref(x, w_gate, w_up, w_down):
        import jax, jax.numpy as jnp
        import numpy as np
        DIM = 256
        HIDDEN = 768
        SCALE = 1.0 / 127.0

        def _dequant(w_int, dtype):
            return w_int.astype(dtype) * jnp.asarray(SCALE, dtype)
        wg = _dequant(w_gate, x.dtype)
        wu = _dequant(w_up, x.dtype)
        wd = _dequant(w_down, x.dtype)
        gate = jnp.einsum('bsd,hd->bsh', x, wg)
        up = jnp.einsum('bsd,hd->bsh', x, wu)
        h = jax.nn.silu(gate) * up
        return jnp.einsum('bsh,dh->bsd', h, wd)
    x = x + _L0_attn_ref(_layernorm(x, axis=-1), L0_attn_rms_w, L0_attn_W_in, L0_attn_conv_w, L0_attn_conv_b, L0_attn_W_x, L0_attn_W_dt, L0_attn_b_dt, L0_attn_A_log, L0_attn_Dp, L0_attn_W_out, L0_attn_ln_w, L0_attn_ln_b)
    x = x + _L0_xattn_ref(_layernorm(x, axis=-1), ctx_1024, ctx_1024, L0_xattn_igate_kernel, L0_xattn_igate_bias, L0_xattn_fgate_kernel, L0_xattn_fgate_bias, L0_xattn_outnorm_scale)
    x = x + _L0_ffn_ref(_layernorm(x, axis=-1), L0_ffn_w_gate, L0_ffn_w_up, L0_ffn_w_down)
    return x

_drawn_inputs = setup_inputs


def setup_inputs(seed=0):
    import zlib

    import numpy as np

    out = dict(_drawn_inputs(seed))
    spreads = {'L0_attn_rms_w': (1.0, 0.6),
     'L0_attn_conv_b': (0.0, 0.8),
     'L0_attn_Dp': (1.0, 0.6),
     'L0_attn_ln_w': (1.0, 0.2),
     'L0_attn_ln_b': (0.0, 0.1),
     'L0_xattn_igate_kernel': (0.0, 0.1),
     'L0_xattn_fgate_kernel': (0.0, 0.1),
     'L0_xattn_outnorm_scale': (1.0, 0.2)}
    factors = {'L0_attn_W_in': 8.0,
     'L0_attn_conv_w': 8.0,
     'L0_attn_W_x': 8.0,
     'L0_attn_W_dt': 8.0,
     'L0_attn_b_dt': 8.0,
     'L0_attn_A_log': 8.0,
     'L0_attn_W_out': 8.0,
     'L0_xattn_igate_bias': 200.0}
    for name, (base, spread) in spreads.items():
        noise = np.random.default_rng([zlib.crc32(name.encode()), seed]).standard_normal(out[name].shape)
        drawn = base * np.exp(spread * noise) if base else spread * noise
        out[name] = jnp.asarray(drawn.astype(out[name].dtype))
    for name, factor in factors.items():
        out[name] = (out[name] * factor).astype(out[name].dtype)
    return out
```

```python
def build(nc, x, ctx_1024, rms_w, W_in, conv_w, conv_b, W_x, W_dt, b_dt, A_log, Dp, W_out, ln_w, ln_b,
          igate_kernel, igate_bias, fgate_kernel, fgate_bias, outnorm_scale, w_gate, w_up, w_down, out):
    import concourse.bass as bass
    from concourse import mybir
    from contextlib import ExitStack

    F32 = mybir.dt.float32
    I32 = mybir.dt.int32
    ACT = mybir.ActivationFunctionType
    ALU = mybir.AluOpType
    ds = bass.ds

    P = 128
    NB, L, D = x.shape
    ED, KC = conv_w.shape
    R = W_dt.shape[0]
    N = A_log.shape[1]
    NH = igate_bias.shape[0]
    DH = D // NH
    HID = w_gate.shape[0]
    DC, EC, LC, HC = D // P, ED // P, L // P, HID // P
    DEPTH = 6
    STAGES = DEPTH * NB
    EPS, EPS_MLSTM, FFN_SCALE = 1e-5, 1e-6, 1.0 / 127.0
    SIG_MIN = -40.0
    DBC = R + 2 * N

    SLOTS = [
        [("z", 0), ("z", 1), ("ms", 0)],
        [("z", 2), ("z", 3)],
        [("xs", 0), ("xs", 1)],
        [("cv", 0), ("y", 0), ("y", 1)],
        [("xs", 2), ("cv", 1), ("y", 2)],
        [("xs", 3), ("cv", 2), ("y", 3)],
        [("cv", 3)],
        [("o", 0)],
        [("o", 1)],
        [("bc", 0)],
        [("dl", 0), ("dl", 1)],
        [("dl", 2), ("dl", 3), ("cl", 0)],
        [("dx", 0), ("dx", 1)],
        [("dx", 2), ("dx", 3)],
        [],
        [],
    ]
    BACK, GATE = ("y", "o"), ("z",)

    def steps(n, back, gate, front):
        return [k for k in SLOTS[n] if (back if k[0] in BACK else gate if k[0] in GATE else front)]

    N_BACK = sum(k[0] in BACK for s in SLOTS for k in s)
    N_GATE = sum(k[0] in GATE for s in SLOTS for k in s)
    N_FRONT = sum(len(s) for s in SLOTS) - N_BACK - N_GATE
    N_ALL = N_BACK + N_GATE + N_FRONT

    NHB = 3

    def hb_of(n):
        return n % NHB if n < N - 1 else 1

    def hb_age(n):
        m = n - 1
        while hb_of(m % N) != hb_of(n):
            m -= 1
        return n - m

    top = ExitStack()
    with top:
        def sem(name):
            return top.enter_context(nc.semaphore(name))

        def sb(stack, name, shape, dt=F32):
            return stack.enter_context(nc.sbuf_tensor(name, shape, dt))

        def pb(stack, name, shape):
            return stack.enter_context(nc.psum_tensor(name, shape, F32))

        xT = sb(top, "xT", [P, NB, DC, L])
        ident = sb(top, "ident", [P, P])
        eps = sb(top, "eps", [P, 2])

        mamba = ExitStack()
        with mamba:
            w_in = sb(mamba, "w_in", [P, DC, 2 * ED])
            w_x = sb(mamba, "w_x", [P, EC, DBC])
            w_dt = sb(mamba, "w_dt", [R, ED])
            w_out = sb(mamba, "w_out", [P, EC, D])
            conv_diag = sb(mamba, "conv_diag", [P, EC, KC, P])
            d_diag = sb(mamba, "d_diag", [P, EC, P])
            mean_mat = sb(mamba, "mean_mat", [P, P])
            neg_a = sb(mamba, "neg_a", [P, EC, N])
            cb = sb(mamba, "cb", [P, EC])
            bdt = sb(mamba, "bdt", [P, EC])

            w_loaded, x_loaded = sem("w_loaded"), sem("x_loaded")
            const_set, weights_set, a_exp = sem("const_set"), sem("weights_set"), sem("a_exp")
            ln_stats, ln_mv, ln_log, ln_rstd, ln_out = (sem("ln_stats"), sem("ln_mv"), sem("ln_log"),
                                                        sem("ln_rstd"), sem("ln_out"))
            ln_tr = sem("ln_tr")
            x_ready = sem("x_ready")

            with ExitStack() as s1:
                x_nat = sb(s1, "x_nat", [P, NB, LC, D])
                rmsw = sb(s1, "rmsw", [P, DC])
                cw = sb(s1, "cw", [P, EC, KC])
                dcol = sb(s1, "dcol", [P, EC])
                stats = sb(s1, "stats", [P, LC, 6])
                mv = sb(s1, "mv", [P, LC, 2])
                lnv = sb(s1, "lnv", [P, LC])
                xn = sb(s1, "xn", [P, LC, D])
                carrier1 = sb(s1, "carrier1", [P, 1])
                pt = pb(s1, "pt", [P, DC, L])
                N_LOADS = 10
                with nc.Block() as block:
                    @block.sync
                    def _(sp):
                        sp.dma_start(x_nat[:, 0], x[0].rearrange("(j p) d -> p j d", p=P)).then_inc(x_loaded, 16)
                        sp.dma_start(x_nat[:, 1:NB], x[1:NB].rearrange("b (j p) d -> p b j d", p=P)).then_inc(x_loaded, 16)
                        sp.dma_start(w_in[:], W_in.rearrange("(k p) e -> p k e", p=P)).then_inc(w_loaded, 16)
                        sp.dma_start(w_x[:], W_x.rearrange("(c p) m -> p c m", p=P)).then_inc(w_loaded, 16)
                        sp.dma_start(w_dt[:], W_dt).then_inc(w_loaded, 16)
                        sp.dma_start(w_out[:], W_out.rearrange("(c p) d -> p c d", p=P)).then_inc(w_loaded, 16)

                    @block.gpsimd
                    def _(pool):
                        pool.memset(ident[:], 0.0).then_inc(const_set, 1)
                        pool.wait_ge(const_set, 1)
                        pool.affine_select(out=ident[:], in_=ident[:], compare_op=ALU.not_equal, fill=1.0,
                                           base=0, pattern=[[-1, P]], channel_multiplier=1).then_inc(const_set, 1)
                        pool.memset(mean_mat[:], 1.0 / D).then_inc(weights_set, 1)
                        pool.memset(eps[:, 0:1], EPS).then_inc(const_set, 1)
                        pool.memset(eps[:, 1:2], EPS_MLSTM).then_inc(const_set, 1)
                        pool.wait_ge(const_set, 2)
                        pool.wait_ge(w_loaded, 16 * N_LOADS)
                        for c in range(EC):
                            for k in range(KC):
                                pool.tensor_scalar(conv_diag[:, c, k, :], ident[:], cw[:, c, k:k + 1], None,
                                                   ALU.mult).then_inc(weights_set, 1)
                            pool.tensor_scalar(d_diag[:, c, :], ident[:], dcol[:, c:c + 1], None,
                                               ALU.mult).then_inc(weights_set, 1)
                        for k in range(DC):
                            pool.tensor_scalar(w_in[:, k, :], w_in[:, k, :], rmsw[:, k:k + 1], None,
                                               ALU.mult).then_inc(weights_set, 1)
                        pool.wait_ge(a_exp, 1)
                        pool.tensor_scalar(neg_a[:], neg_a[:], -1.0, None, ALU.mult).then_inc(weights_set, 1)

                    @block.scalar
                    def _(act):
                        act.dma_start(cw[:], conv_w.rearrange("(c p) k -> p c k", p=P)).then_inc(w_loaded, 16)
                        act.dma_start(neg_a[:], A_log.rearrange("(c p) n -> p c n", p=P)).then_inc(w_loaded, 16)
                        for dst, src in ((rmsw, rms_w), (cb, conv_b), (bdt, b_dt), (dcol, Dp)):
                            act.dma_start(dst[:], src.rearrange("(c p) -> p c", p=P),
                                          allow_slow_non_contiguous=True).then_inc(w_loaded, 16)
                        act.preload_act_table_set("natural_log_exp_and_others")
                        act.wait_ge(w_loaded, 16 * N_LOADS)
                        act.activation(neg_a[:], neg_a[:], ACT.Exp).then_inc(a_exp, 1)
                        act.wait_ge(const_set, 4)
                        with act.Fori(0, NB) as b:
                            act.wait_ge(ln_mv, b + 1)
                            act.activation(lnv[:], mv[:, :, 1], ACT.Ln, bias=eps[:, 0:1]).then_inc(ln_log, 1)
                            act.wait_ge(ln_log, b + 1)
                            act.activation(lnv[:], lnv[:], ACT.Exp, scale=-0.5).then_inc(ln_rstd, 1)
                            act.wait_ge(ln_tr, b + 1)
                            act.activation(xT[:, ds(b, 1), :, :], pt[:], ACT.Copy).then_inc(x_ready, 1)

                    @block.vector
                    def _(dve):
                        dve.wait_ge(x_loaded, 32)
                        with dve.Fori(0, NB) as b:
                            for j in range(LC):
                                dve.bn_stats(stats[:, j, :], x_nat[:, ds(b, 1), j, :]).then_inc(ln_stats, 1)
                            dve.wait_ge(ln_stats, (b + 1) * LC)
                            dve.memset(carrier1[:], 0.0)
                            for j in range(LC):
                                last = dve.bn_aggr(mv[:, j, :], stats[:, j, :])
                            last.then_inc(ln_mv, 1)
                            dve.wait_ge(ln_rstd, b + 1)
                            for j in range(LC):
                                last = dve.tensor_scalar(xn[:, j, :], x_nat[:, ds(b, 1), j, :], mv[:, j, 0:1],
                                                         lnv[:, j:j + 1], ALU.subtract, ALU.mult)
                            last.then_inc(ln_out, 1)
                            dve.wait_ge(ln_tr, b + 1)

                    @block.tensor
                    def _(pe):
                        pe.wait_ge(const_set, 2)
                        with pe.Fori(0, NB) as b:
                            pe.wait_ge(ln_out, b + 1)
                            for k in range(DC):
                                for j in range(LC):
                                    last = pe.transpose(pt[:, k, j * P:(j + 1) * P], xn[:, j, k * P:(k + 1) * P],
                                                        ident[:])
                            last.then_inc(ln_tr, 1)
                            pe.wait_ge(x_ready, b + 1)

            with ExitStack() as s2:
                sq = sb(s2, "sq", [P, DC, L])
                rstd = sb(s2, "rstd", [P, L])
                u = sb(s2, "u", [P, DC, L])
                PAD = KC - 1
                xs = sb(s2, "xs", [P, 2, L + PAD])
                xc = sb(s2, "xc", [P, EC, L])
                sg = sb(s2, "sg", [P, 2, L])
                dbc = sb(s2, "dbc", [DBC, 2, L])
                c_tok = sb(s2, "c_tok", [P, 2, LC, N])
                delta = sb(s2, "delta", [P, 2, EC, L])
                dx = sb(s2, "dx", [P, 2, EC, L])
                pos = sb(s2, "pos", [P, 2, L])
                zl = sb(s2, "zl", [P, LC, ED])
                g = sb(s2, "g", [P, LC, ED])
                acc = sb(s2, "acc", [P, 2, LC, ED])
                da = sb(s2, "da", [P, 2, EC, L])
                hb = sb(s2, "hb", [P, NHB, EC, L])
                b_all = sb(s2, "b_all", [P, 2, L])
                ht = pb(s2, "ht", [P, LC, ED])
                bb = pb(s2, "bb", [P, 2, L])
                fr = pb(s2, "fr", [P, 2, L])

                pads = sem("pads")
                front_full, front_free = sem("front_full"), sem("front_free")
                sq_ready, rms_log, rstd_ready, u_ready = (sem("sq_ready"), sem("rms_log"), sem("rstd_ready"),
                                                          sem("u_ready"))
                v_ready, v_clamped, v_exp, v_log, v_sig, xc_ready = (
                    sem("v_ready"), sem("v_clamped"), sem("v_exp"), sem("v_log"), sem("v_sig"), sem("xc_ready"))
                z_ready, z_clamped, z_exp, z_log, z_sig, g_ready = (
                    sem("z_ready"), sem("z_clamped"), sem("z_exp"), sem("z_log"), sem("z_sig"), sem("g_ready"))
                p_abs, p_pos, p_exp, p_log, delta_ready, dx_ready = (
                    sem("p_abs"), sem("p_pos"), sem("p_exp"), sem("p_log"), sem("delta_ready"), sem("dx_ready"))
                xs_ready, dbc_ready, c_ready, acc_set = sem("xs_ready"), sem("dbc_ready"), sem("c_ready"), sem("acc_set")
                yg_ready, yt_ready, o_ready = sem("yg_ready"), sem("yt_ready"), sem("o_ready")
                b_bcast, b_ready = sem("b_bcast"), sem("b_ready")
                da_ready, dbx_ready, scanned, h_tr, y_added = (sem("da_ready"), sem("dbx_ready"), sem("scanned"),
                                                               sem("h_tr"), sem("y_added"))

                class Stage:

                    def __init__(self, s, par, base, phase):
                        self.s, self.par, self.base, self.phase = s, par, base, phase

                    def bank(self, k):
                        return (self.phase + k) % 2

                def emit_act_step(act, st, k, kind, i):
                    s, nx = st.s, st.s + 1
                    q = 1 - st.par
                    bank = fr[:, st.bank(k), :]
                    act.wait_ge(front_full, st.base + k + 1)
                    if kind == "z":
                        if not st.is_first:
                            act.wait_ge(g_ready, LC * s)
                        act.activation(zl[:, i, :], bank, ACT.Copy).then_inc(front_free, 1)
                    elif kind == "ms":
                        act.activation(rstd[:], bank, ACT.Ln, bias=eps[:, 0:1]).then_inc(front_free, 1)
                        act.wait_ge(front_free, st.base + k + 1)
                        act.activation(rstd[:], rstd[:], ACT.Exp, scale=-0.5).then_inc(rstd_ready, 1)
                    elif kind == "xs":
                        act.activation(xs[:, i % 2, PAD:], bank, ACT.Copy).then_inc(front_free, 1)
                    elif kind == "cv":
                        if i == 0 and not st.is_prelude:
                            act.wait_ge(dx_ready, EC * nx)
                        act.activation(xc[:, i, :], bank, ACT.Identity, bias=cb[:, i:i + 1]).then_inc(front_free, 1)
                    elif kind == "y":
                        act.activation(delta[:, q, i, :], bank, ACT.Copy).then_inc(front_free, 1)
                    elif kind == "o":
                        act.activation(sq[:, i, :], bank, ACT.Copy).then_inc(front_free, 1)
                    elif kind == "bc":
                        act.activation(dbc[:, q, :], fr[0:DBC, st.bank(k), :], ACT.Copy).then_inc(front_free, 1)
                    elif kind == "cl":
                        if not (st.is_prelude or st.is_first):
                            act.wait_ge(y_added, LC * N * s)
                        act.activation(c_tok[:, q], bank[:, 0:LC * N].rearrange("p (j n) -> p j n", n=N),
                                       ACT.Copy).then_inc(front_free, 1)
                    elif kind == "dx":
                        act.activation(acc[:, q, i, :], bank, ACT.Copy).then_inc(front_free, 1)
                    elif kind == "dl":
                        act.activation(delta[:, q, i, :], bank, ACT.Abs, bias=bdt[:, i:i + 1]).then_inc(p_abs, 1)
                        if i < 2:
                            if not st.is_prelude:
                                act.wait_ge(delta_ready, EC * nx)
                        else:
                            act.wait_ge(delta_ready, EC * nx + i - 1)
                        act.activation(pos[:, i % 2, :], bank, ACT.Relu, bias=bdt[:, i:i + 1]).then_inc(front_free, 1)
                        act.wait_ge(p_abs, EC * nx + i + 1)
                        act.activation(delta[:, q, i, :], delta[:, q, i, :], ACT.Exp, scale=-1.0).then_inc(p_exp, 1)
                        act.wait_ge(p_exp, EC * nx + i + 1)
                        act.activation(delta[:, q, i, :], delta[:, q, i, :], ACT.Ln, bias=1.0).then_inc(p_log, 1)

                def emit_act_sigmoid(act, buf, clamped, e, l, sig, count):
                    act.wait_ge(clamped, count)
                    act.activation(buf, buf, ACT.Exp, scale=-1.0).then_inc(e, 1)
                    act.wait_ge(e, count)
                    act.activation(buf, buf, ACT.Ln, bias=1.0).then_inc(l, 1)
                    act.wait_ge(l, count)
                    act.activation(buf, buf, ACT.Exp, scale=-1.0).then_inc(sig, 1)

                def emit_act_squares(act, nx, b):
                    act.wait_ge(x_ready, nx + 1)
                    act.wait_ge(x_ready, nx + (NB - 2))
                    act.activation(sq[:], xT[:, ds(b, 1), :, :], ACT.Square).then_inc(sq_ready, 1)

                def emit_act_decay(act, s, par, n, warm):
                    if n == 0:
                        act.wait_ge(delta_ready, EC * s + EC)
                    if warm:
                        act.wait_ge(scanned, N * s + n - 1)
                    for c in range(EC):
                        last = act.activation(da[:, n % 2, c, 1:L], delta[:, par, c, 1:L], ACT.Exp,
                                              scale=neg_a[:, c, n:n + 1])
                    last.then_inc(da_ready, 1)

                def emit_act_b(act, s, n, warm):
                    act.wait_ge(b_bcast, N * s + n + 1)
                    if warm:
                        act.wait_ge(dbx_ready, N * s + n - 1)
                    act.activation(b_all[:, n % 2, :], bb[:, n % 2, :], ACT.Copy).then_inc(b_ready, 1)

                def act_stage(act, st, back, gate, front, scan, next_scan, first=False):
                    s, k = st.s, 0
                    for n in range(N):
                        if scan:
                            if n + 1 < N:
                                emit_act_decay(act, s, st.par, n + 1, not first or n + 1 >= 2)
                            elif next_scan:
                                emit_act_decay(act, s + 1, 1 - st.par, 0, True)
                        if n == 0 and front:
                            emit_act_squares(act, s + 1, (s + 1) % NB)
                        for kind, i in steps(n, back, gate, front):
                            emit_act_step(act, st, k, kind, i)
                            k += 1
                        if scan:
                            if n + 2 < N:
                                emit_act_b(act, s, n + 2, True)
                            elif next_scan:
                                emit_act_b(act, s + 1, n + 2 - N, True)
                        if front and 4 <= n < 8:
                            emit_act_sigmoid(act, sg[:, (n - 4) % 2, :], v_clamped, v_exp, v_log, v_sig,
                                             EC * (s + 1) + n - 3)
                        if gate and n in (8, 9, 10, 11):
                            emit_act_sigmoid(act, g[:, n - 8, :], z_clamped, z_exp, z_log, z_sig, LC * s + n - 7)

                def emit_pe_step(pe, st, k, kind, i):
                    s, nx = st.s, st.s + 1
                    q = 1 - st.par
                    b_ = st.bank(k)
                    bank = fr[:, b_, :]
                    if not (st.is_prelude and k < 2):
                        pe.wait_ge(front_free, st.base + k - 1)

                    if kind == "z":
                        pe.wait_ge(u_ready, s + 1)
                        for d in range(DC):
                            last = pe.matmul(bank, u[:, d, i * P:(i + 1) * P], w_in[:, d, ED:2 * ED],
                                             start=d == 0, stop=d == DC - 1)
                    elif kind == "ms":
                        pe.wait_ge(sq_ready, nx + 1)
                        for d in range(DC):
                            last = pe.matmul(bank, mean_mat[:], sq[:, d, :], start=d == 0, stop=d == DC - 1)
                    elif kind == "xs":
                        pe.wait_ge(u_ready, nx + 1)
                        for d in range(DC):
                            last = pe.matmul(bank, w_in[:, d, i * P:(i + 1) * P], u[:, d, :],
                                             start=d == 0, stop=d == DC - 1)
                    elif kind == "cv":
                        pe.wait_ge(front_free, st.base + xs_step(st, i) + 1)
                        for t in range(KC):
                            last = pe.matmul(bank, conv_diag[:, i, t, :], xs[:, i % 2, t:t + L],
                                             start=t == 0, stop=t == KC - 1)
                    elif kind == "y":
                        pe.wait_ge(yg_ready, LC * s)
                        for j in range(LC):
                            last = pe.transpose(bank[:, j * P:(j + 1) * P], acc[:, q, j, i * P:(i + 1) * P], ident[:])
                    elif kind == "o":
                        pe.wait_ge(front_free, st.base + k_of(st, "y", EC - 1) + 1)
                        for c in range(EC):
                            last = pe.matmul(bank, w_out[:, c, i * P:(i + 1) * P], delta[:, q, c, :],
                                             start=c == 0, stop=c == EC - 1)
                    elif kind == "bc":
                        pe.wait_ge(xc_ready, EC * nx + EC)
                        for c in range(EC):
                            last = pe.matmul(fr[0:DBC, b_, :], w_x[:, c, :], xc[:, c, :], start=c == 0, stop=c == EC - 1)
                    elif kind == "dl":
                        pe.wait_ge(front_free, st.base + k_of(st, "bc", 0) + 1)
                        last = pe.matmul(bank, w_dt[:, i * P:(i + 1) * P], dbc[0:R, q, :], start=True, stop=True)
                    elif kind == "cl":
                        for j in range(LC):
                            for c in range(EC):
                                last = pe.matmul(bank[:, j * N:(j + 1) * N], xc[:, c, j * P:(j + 1) * P],
                                                 w_x[:, c, R + N:DBC], start=c == 0, stop=c == EC - 1)
                    elif kind == "dx":
                        for c in range(EC):
                            last = pe.matmul(bank[:, c * P:(c + 1) * P], xc[:, c, i * P:(i + 1) * P],
                                             d_diag[:, c, :], start=True, stop=True)
                    last.then_inc(front_full, 1)

                def k_of(st, kind, i):
                    return st.order.index((kind, i))

                def xs_step(st, i):
                    return k_of(st, "xs", i)

                def emit_pe_b(pe, s, par, n, warm):
                    if warm:
                        pe.wait_ge(b_ready, N * s + n - 1)
                    pe.matmul(bb[:, n % 2, :], ident[R:R + N, R + n:R + n + 1].broadcast_to([N, P]),
                              dbc[R:R + N, par, :], start=True, stop=True).then_inc(b_bcast, 1)

                def emit_pe_transposes(pe, s, n, warm):
                    pe.wait_ge(scanned, N * s + n + 1)
                    for j in range(LC):
                        if warm:
                            pe.wait_ge(y_added, LC * (N * s + n - 1) + j + 1)
                        for c in range(EC):
                            last = pe.transpose(ht[:, j, c * P:(c + 1) * P], hb[:, hb_of(n), c, j * P:(j + 1) * P],
                                                ident[:])
                        last.then_inc(h_tr, 1)

                def pe_stage(pe, st, back, gate, front, scan, next_scan, first=False):
                    s, k = st.s, 0
                    for n in range(N):
                        for kind, i in steps(n, back, gate, front):
                            emit_pe_step(pe, st, k, kind, i)
                            k += 1
                        if scan:
                            if n + 2 < N:
                                emit_pe_b(pe, s, st.par, n + 2, True)
                            elif next_scan:
                                emit_pe_b(pe, s + 1, 1 - st.par, n + 2 - N, True)
                            emit_pe_transposes(pe, s, n, not first or n > 0)

                def emit_pool_dbx(pool, s, par, n, warm):
                    pool.wait_ge(b_ready, N * s + n + 1)
                    if n == 0:
                        pool.wait_ge(dx_ready, EC * s + EC)
                    if warm:
                        pool.wait_ge(h_tr, LC * (N * s + n - hb_age(n) + 1))
                    pool.tensor_tensor(hb[:, hb_of(n)], dx[:, par],
                                       b_all[:, n % 2:n % 2 + 1, :].broadcast_to([P, EC, L]),
                                       ALU.mult).then_inc(dbx_ready, 1)

                def emit_pool_rms(pool, nx, b):
                    pool.wait_ge(rstd_ready, nx + 1)
                    pool.tensor_tensor(u[:], xT[:, ds(b, 1), :, :], rstd[:].unsqueeze(1).broadcast_to([P, DC, L]),
                                       ALU.mult).then_inc(u_ready, 1)

                def emit_pool_xc(pool, nx, i):
                    pool.wait_ge(v_sig, EC * nx + i + 1)
                    pool.tensor_tensor(xc[:, i, :], xc[:, i, :], sg[:, i % 2, :], ALU.mult).then_inc(xc_ready, 1)

                def emit_pool_delta(pool, nx, q, i):
                    pool.wait_ge(p_log, EC * nx + i + 1)
                    pool.tensor_tensor(delta[:, q, i, :], delta[:, q, i, :], pos[:, i % 2, :],
                                       ALU.add).then_inc(delta_ready, 1)
                    pool.wait_ge(delta_ready, EC * nx + i + 1)
                    pool.tensor_tensor(dx[:, q, i, :], delta[:, q, i, :], xc[:, i, :], ALU.mult).then_inc(dx_ready, 1)

                def emit_pool_gate(pool, s, i):
                    pool.wait_ge(z_sig, LC * s + i + 1)
                    pool.tensor_tensor(g[:, i, :], g[:, i, :], zl[:, i, :], ALU.mult).then_inc(g_ready, 1)

                def emit_pool_yg(pool, s, q, j):
                    pool.wait_ge(y_added, LC * N * s - LC + j + 1)
                    pool.wait_ge(g_ready, LC * (s - 1) + j + 1)
                    pool.tensor_tensor(acc[:, q, j, :], acc[:, q, j, :], g[:, j, :], ALU.mult).then_inc(yg_ready, 1)

                def pool_stage(pool, st, back, gate, front, scan, next_scan, first=False):
                    s, q = st.s, 1 - st.par
                    for n in range(N):
                        if scan:
                            if n + 1 < N:
                                emit_pool_dbx(pool, s, st.par, n + 1, not first or n + 1 >= NHB)
                            elif next_scan:
                                emit_pool_dbx(pool, s + 1, q, 0, True)
                        if front:
                            if n == 1:
                                if gate:
                                    pool.wait_ge(front_free, st.base + k_of(st, "z", LC - 1) + 1)
                                emit_pool_rms(pool, s + 1, (s + 1) % NB)
                            if 4 <= n < 8:
                                emit_pool_xc(pool, s + 1, n - 4)
                        if back and n in (2, 3):
                            for j in (2 * n - 4, 2 * n - 3):
                                emit_pool_yg(pool, s, q, j)
                        if gate and n in (9, 10, 14, 15):
                            emit_pool_gate(pool, s, (9, 10, 14, 15).index(n))
                        if front and 10 <= n < 14:
                            emit_pool_delta(pool, s + 1, q, n - 10)

                def emit_dve_scan(dve, s, n):
                    dve.wait_ge(da_ready, N * s + n + 1)
                    dve.wait_ge(dbx_ready, N * s + n + 1)
                    h = hb[:, hb_of(n)].rearrange("p c l -> p (c l)")
                    dve.tensor_tensor_scan(h, da[:, n % 2].rearrange("p c l -> p (c l)"), h, 0.0,
                                           ALU.mult, ALU.add).then_inc(scanned, 1)

                def emit_dve_y(dve, s, par, n, st=None):
                    for j in range(LC):
                        dve.wait_ge(h_tr, LC * (N * s + n) + j + 1)
                        if n > 0:
                            dve.wait_ge(y_added, LC * (N * s + n - 1) + j + 1)
                        dve.scalar_tensor_tensor(acc[:, par, j, :], ht[:, j, :], c_tok[:, par, j, n:n + 1],
                                                 acc[:, par, j, :], ALU.mult, ALU.add).then_inc(y_added, 1)

                def emit_dve_residual(dve, st, s, b):
                    dve.wait_ge(front_free, st.base + k_of(st, "o", DC - 1) + 1)
                    dve.scalar_tensor_tensor(xT[:, ds(b, 1), :, :].rearrange("p b k l -> p (b k l)"),
                                             xT[:, ds(b, 1), :, :].rearrange("p b k l -> p (b k l)"), 2.0,
                                             sq[:].rearrange("p k l -> p (k l)"), ALU.mult, ALU.add).then_inc(x_ready, 1)

                def emit_dve_clamp_v(dve, st, nx, i):
                    dve.wait_ge(front_free, st.base + k_of(st, "cv", i) + 1)
                    if i >= 2:
                        dve.wait_ge(xc_ready, EC * nx + i - 1)
                    dve.tensor_scalar(sg[:, i % 2, :], xc[:, i, :], SIG_MIN, None, ALU.max).then_inc(v_clamped, 1)

                def emit_dve_clamp_z(dve, st, s, i):
                    dve.wait_ge(front_free, st.base + k_of(st, "z", i) + 1)
                    dve.tensor_scalar(g[:, i, :], zl[:, i, :], SIG_MIN, None, ALU.max).then_inc(z_clamped, 1)

                def dve_stage(dve, st, back, gate, front, scan, next_scan, first=False, acc_base=None):
                    s = st.s
                    for n in range(N):
                        if scan:
                            emit_dve_scan(dve, s, n)
                            if n == 0:
                                if back:
                                    emit_dve_y(dve, s - 1, 1 - st.par, N - 1)
                            else:
                                if n == 1:
                                    dve.wait_ge(front_free, st.base)
                                emit_dve_y(dve, s, st.par, n - 1)
                        if front and 3 <= n < 7:
                            emit_dve_clamp_v(dve, st, s + 1, n - 3)
                        if gate and n in (7, 8):
                            if n == 7 and back:
                                dve.wait_ge(yg_ready, LC * s)
                            for j in (2 * n - 14, 2 * n - 13):
                                emit_dve_clamp_z(dve, st, s, j)
                        if back and n == 9:
                            emit_dve_residual(dve, st, s, (s - 1 + NB) % NB)

                def order_of(back, gate, front):
                    return [k for n in range(N) for k in steps(n, back, gate, front)]

                def make(s, par, base, phase, back, gate, front):
                    st = Stage(s, par, base, phase % 2)
                    st.order = order_of(back, gate, front)
                    st.is_prelude, st.is_first = front and not gate, gate and front and not back
                    return st

                PAIRS = (STAGES - 2) // 2
                BASE1 = 2 * N_FRONT + N_GATE

                def drive(eng, stage_fn, prelude, flush):
                    st = make(-1, 1, 0, 0, False, False, True)
                    stage_fn(eng, st, False, False, True, False, False, first=True)
                    prelude(eng)
                    st = make(0, 0, N_FRONT, N_FRONT, False, True, True)
                    stage_fn(eng, st, False, True, True, True, True, first=True)
                    with eng.Fori(0, PAIRS) as t:
                        for half in (0, 1):
                            st = make(t * 2 + (1 + half), (1 + half) % 2, t * (2 * N_ALL) + (BASE1 + half * N_ALL),
                                      BASE1 + half * N_ALL, True, True, True)
                            stage_fn(eng, st, True, True, True, True, True)
                    last = STAGES - 1
                    base = BASE1 + (STAGES - 2) * N_ALL
                    st = make(last, last % 2, base, base, True, True, False)
                    stage_fn(eng, st, True, True, False, True, False)
                    flush(eng)
                    base += N_BACK + N_GATE
                    st = make(STAGES, STAGES % 2, base, base, True, False, False)
                    stage_fn(eng, st, True, False, False, False, False)

                nothing = lambda eng: None

                with nc.Block() as block:
                    @block.scalar
                    def _(act):
                        act.wait_ge(pads, 2)

                        def prelude(act):
                            emit_act_decay(act, 0, 0, 0, False)
                            emit_act_b(act, 0, 0, False)
                            emit_act_b(act, 0, 1, False)
                        drive(act, act_stage, prelude, nothing)

                    @block.tensor
                    def _(pe):
                        def prelude(pe):
                            pe.wait_ge(front_free, N_FRONT)
                            emit_pe_b(pe, 0, 0, 0, False)
                            emit_pe_b(pe, 0, 0, 1, False)
                        drive(pe, pe_stage, prelude, nothing)

                    @block.gpsimd
                    def _(pool):
                        def prelude(pool):
                            emit_pool_dbx(pool, 0, 0, 0, False)
                        drive(pool, pool_stage, prelude, nothing)

                    @block.vector
                    def _(dve):
                        dve.memset(da[:], 0.0).then_inc(pads, 1)
                        dve.memset(xs[:], 0.0).then_inc(pads, 1)
                        drive(dve, dve_stage, nothing,
                              lambda dve: emit_dve_y(dve, STAGES - 1, (STAGES - 1) % 2, N - 1))

        with ExitStack() as s3:
            GK = 3 * DC
            lnw = sb(s3, "lnw", [P, D])
            lnb = sb(s3, "lnb", [P, D])
            onorm = sb(s3, "onorm", [P, D])
            igk = sb(s3, "igk", [P, GK, NH])
            fgk = sb(s3, "fgk", [P, GK, NH])
            gate_bias = sb(s3, "gate_bias", [NH, 3])
            ones = sb(s3, "ones", [NH, L])
            neg_sel = sb(s3, "neg_sel", [NH, NH])
            wg = sb(s3, "wg", [P, DC, HID])
            wu = sb(s3, "wu", [P, DC, HID])
            wd = sb(s3, "wd", [P, HC, D])
            w_int = sb(s3, "w_int", [P, HC * D], I32)
            w_f = sb(s3, "w_f", [P, HC * D])
            xin = sb(s3, "xin", [P, LC, D])
            cx = sb(s3, "cx", [P, LC, D])
            xm = sb(s3, "xm", [P, DC, L])
            t_a = sb(s3, "t_a", [P, LC, D])
            x1 = sb(s3, "x1", [P, LC, D])
            x2 = sb(s3, "x2", [P, LC, D])
            nrm = sb(s3, "nrm", [P, LC, D])
            qt = sb(s3, "qt", [P, DC, L])
            ct = sb(s3, "ct", [P, DC, L])
            x2t = sb(s3, "x2t", [P, DC, L])
            v1 = sb(s3, "v1", [P, LC, NH, DH + 1])
            stats3 = sb(s3, "stats3", [P, 4 * LC, 6])
            mv3 = sb(s3, "mv3", [P, 4 * LC, 2])
            lnv3 = sb(s3, "lnv3", [P, 4 * LC])
            carrier = sb(s3, "carrier", [P, 1])
            carrier_p = sb(s3, "carrier_p", [P, 1])
            fa = sb(s3, "fa", [NH, L])
            fr_ = sb(s3, "fr_", [NH, L])
            ncs = sb(s3, "ncs", [NH, L])
            ga = sb(s3, "ga", [NH, L])
            gm = sb(s3, "gm", [NH, L])
            ge = sb(s3, "ge", [NH, L])
            ae = sb(s3, "ae", [P, LC, 2 * NH])
            dm = sb(s3, "dm", [P, 2, LC, L])
            osb = sb(s3, "osb", [P, LC, NH, DH + 1])
            den = sb(s3, "den", [P, LC, NH])
            kk = sb(s3, "kk", [P, LC, NH])
            gl = sb(s3, "gl", [P, 2, L])
            gs = sb(s3, "gs", [P, 2, L])
            hid = sb(s3, "hid", [P, HC, L])
            o_sb = sb(s3, "o_sb", [P, LC, D])
            ps_a = pb(s3, "ps_a", [P, 2, L])
            ps_b = pb(s3, "ps_b", [P, 2, L])
            ps_s = pb(s3, "ps_s", [P, 4, L])

            S = {k: sem("e_" + k) for k in (
                "consts", "w_in", "w_scaled", "w_tr", "w_evac", "x_in", "c_in", "out_free", "out_ready", "set", "act_set",
                "xm_ready", "x_tok", "stats", "mv", "log", "rstd", "normed", "lnm_w", "lnm_b", "x1_ready",
                "c_tr", "c_t_ready", "v_ready", "q_tr", "q_t_ready", "gates", "f_abs", "f_relu", "f_exp", "f_log",
                "i_ready", "f_sum", "cs_ready", "ga_ready", "gm_ready", "ge_diff", "ge_ready", "ae_tr", "ae_ready",
                "m_bc", "d_arg", "qk", "d_exp", "d_masked", "c_ready", "av", "h_stats", "h_mv", "h_neg", "h_den", "h_rec", "o_evac",
                "h_t1", "h_t2", "h_log", "h_rs", "h_k", "h_sub", "h_mul", "h_scaled", "x2_ready", "x2_tr",
                "x2t_ready", "ffn_g", "ffn_u", "gl_ready", "g_cl", "g_exp", "g_log", "g_sig", "g_silu", "hid_ready",
                "down")}

            def three(ap, k):
                return ap.rearrange("p (k f) -> p k f", k=k)

            oh = [ps_a[:, 0], ps_a[:, 1], ps_b[:, 0], ps_b[:, 1]]

            def oh_heads(j):
                return oh[j][:, 0:NH * (DH + 1)].rearrange("p (h d) -> p h d", h=NH)

            N_CONST = 7
            with nc.Block() as block:
                @block.sync
                def _(sp):
                    for dst, src in ((lnw, ln_w), (lnb, ln_b), (onorm, outnorm_scale)):
                        sp.dma_start(dst[:], src.partition_broadcast(P)).then_inc(S["consts"], 16)
                    sp.dma_start(igk[:], igate_kernel.rearrange("(k p) h -> p k h", p=P)).then_inc(S["consts"], 16)
                    sp.dma_start(fgk[:], fgate_kernel.rearrange("(k p) h -> p k h", p=P)).then_inc(S["consts"], 16)
                    sp.dma_start(gate_bias[:, 0:1], igate_bias.rearrange("(h a) -> h a", a=1),
                                 allow_slow_non_contiguous=True).then_inc(S["consts"], 16)
                    sp.dma_start(gate_bias[:, 1:2], fgate_bias.rearrange("(h a) -> h a", a=1),
                                 allow_slow_non_contiguous=True).then_inc(S["consts"], 16)
                    sp.sem_inc(S["out_free"], 16)
                    for m, w in enumerate((w_gate, w_up)):
                        if m:
                            sp.wait_ge(S["w_scaled"], m)
                        sp.dma_start(three(w_int[:], HC), w.rearrange("(c p) d -> p c d", p=P)).then_inc(S["w_in"], 16)
                    sp.wait_ge(S["w_scaled"], 2)
                    sp.dma_start(three(w_int[:], DC), w_down.rearrange("(k p) h -> p k h", p=P)).then_inc(S["w_in"], 16)

                    def load(b):
                        sp.dma_start(xin[:], x[ds(b, 1)].rearrange("b (j p) d -> p (b j) d", p=P)).then_inc(S["x_in"], 16)
                        sp.dma_start(cx[:], ctx_1024[ds(b, 1)].rearrange("b (j p) d -> p (b j) d", p=P)).then_inc(S["c_in"], 16)

                    def store(b):
                        sp.wait_ge(S["out_ready"], (b + 1) * LC)
                        sp.dma_start(out[ds(b, 1)].rearrange("b (j p) d -> p (b j) d", p=P), o_sb[:]).then_inc(S["out_free"], 16)

                    load(0)
                    with sp.Fori(0, NB - 1) as b:
                        sp.wait_ge(S["x1_ready"], b + 1)
                        sp.wait_ge(S["c_t_ready"], b + 1)
                        sp.wait_ge(S["v_ready"], b + 1)
                        load(b + 1)
                        store(b)
                    store(NB - 1)
                    sp.wait_ge(S["out_free"], 16 * (NB + 1))

                @block.scalar
                def _(act):
                    def evac(out_, in_, full, count, done):
                        act.wait_ge(S[full], count)
                        act.activation(out_, in_, ACT.Copy).then_inc(S[done], 1)

                    def rsqrt(out_, in_, ready, count, log, done, e, lead=1.0):
                        act.wait_ge(S[ready], count)
                        act.activation(out_, in_, ACT.Ln, bias=e).then_inc(S[log], 1)
                        act.wait_ge(S[log], count)
                        act.activation(out_, out_, ACT.Exp, scale=-0.5).then_inc(S[done], 1)

                    act.wait_ge(S["consts"], 16 * N_CONST)
                    act.activation(gate_bias[:, 2:3], gate_bias[:, 1:2], ACT.Copy, scale=-1.0).then_inc(S["act_set"], 1)
                    act.activation(neg_sel[:], ident[0:NH, 0:NH], ACT.Copy, scale=-1.0).then_inc(S["act_set"], 1)
                    act.wait_ge(S["act_set"], 2)
                    for m, w in enumerate((wg, wu)):
                        for k in range(DC):
                            act.wait_ge(S["w_tr"], m * DC + k + 1)
                            act.activation(w[:, k, 0:L], ps_s[:, 2 * k, :], ACT.Copy)
                            act.activation(w[:, k, L:HID], ps_s[:, 2 * k + 1, 0:HID - L], ACT.Copy).then_inc(S["w_evac"], 1)
                    act.wait_ge(S["w_tr"], 2 * DC + 1)
                    act.activation(wd[:, 0:4, :], ps_s[:, 0:2, :].rearrange("p a l -> p (a l)").rearrange("p (c d) -> p c d", d=D), ACT.Copy)
                    act.activation(wd[:, 4:6, :], three(ps_s[:, 2, :], 2), ACT.Copy).then_inc(S["w_evac"], 1)
                    with act.Fori(0, NB) as b:
                        act.wait_ge(S["w_evac"], 2 * DC + 1)
                        act.activation(xm[:], xT[:, ds(b, 1), :, :], ACT.Copy).then_inc(S["xm_ready"], 1)
                        act.wait_ge(S["set"], 2)
                        act.wait_ge(S["c_in"], 16 * (b + 1))
                        for i in range(LC):
                            last = act.activation(v1[:, i, :, 0:DH], cx[:, i, :].rearrange("p (h d) -> p h d", h=NH), ACT.Copy)
                        last.then_inc(S["v_ready"], 1)
                        rsqrt(lnv3[:, 0:LC], mv3[:, 0:LC, 1], "mv", 3 * b + 1, "log", "rstd", eps[:, 0:1])
                        evac(ct[:], ps_b[:], "c_tr", b + 1, "c_t_ready")
                        rsqrt(lnv3[:, 0:LC], mv3[:, 0:LC, 1], "mv", 3 * b + 2, "log", "rstd", eps[:, 0:1])
                        evac(qt[:], ps_a[:], "q_tr", b + 1, "q_t_ready")
                        act.wait_ge(S["gates"], b + 1)
                        act.activation(ga[:], ps_s[0:NH, 0, :], ACT.Identity, bias=gate_bias[:, 0:1]).then_inc(S["i_ready"], 1)
                        act.activation(fa[:], ps_s[0:NH, 1, :], ACT.Abs, bias=gate_bias[:, 1:2]).then_inc(S["f_abs"], 1)
                        act.activation(fr_[:], ps_s[0:NH, 1, :], ACT.Relu, scale=-1.0, bias=gate_bias[:, 2:3]).then_inc(S["f_relu"], 1)
                        act.wait_ge(S["f_abs"], b + 1)
                        act.activation(fa[:], fa[:], ACT.Exp, scale=-1.0).then_inc(S["f_exp"], 1)
                        act.wait_ge(S["f_exp"], b + 1)
                        act.activation(fa[:], fa[:], ACT.Ln, bias=1.0).then_inc(S["f_log"], 1)
                        act.wait_ge(S["ge_diff"], b + 1)
                        act.activation(ge[:], ge[:], ACT.Exp).then_inc(S["ge_ready"], 1)
                        evac(ae[:], ps_s[:, 2, 0:LC * 2 * NH].rearrange("p (j g) -> p j g", j=LC), "ae_tr", b + 1, "ae_ready")
                        act.wait_ge(S["ae_ready"], b + 1)
                        for h in range(NH):
                            for i in range(LC):
                                blk = dm[:, h % 2, i, i * P:L]
                                act.wait_ge(S["d_arg"], (b * NH + h) * LC + i + 1)
                                act.activation(blk, blk, ACT.Exp).then_inc(S["d_exp"], 1)
                        act.wait_ge(S["av"], (b + 1) * NH)
                        for j in range(LC):
                            act.activation(osb[:, j], oh_heads(j), ACT.Copy).then_inc(S["o_evac"], 1)
                        rsqrt(kk[:], kk[:], "h_t2", b + 1, "h_log", "h_rs", eps[:, 1:2])
                        rsqrt(lnv3[:, 0:LC], mv3[:, 0:LC, 1], "mv", 3 * b + 3, "log", "rstd", eps[:, 0:1])
                        evac(x2t[:], ps_a[:], "x2_tr", b + 1, "x2t_ready")
                        for c in range(HC):
                            n_ = b * HC + c + 1
                            if c >= 2:
                                act.wait_ge(S["g_silu"], n_ - 2)
                            evac(gl[:, c % 2, :], ps_s[:, c % 2, :], "ffn_g", n_, "gl_ready")
                            buf = gs[:, c % 2, :]
                            act.wait_ge(S["g_cl"], n_)
                            act.activation(buf, buf, ACT.Exp, scale=-1.0).then_inc(S["g_exp"], 1)
                            act.wait_ge(S["g_exp"], n_)
                            act.activation(buf, buf, ACT.Ln, bias=1.0).then_inc(S["g_log"], 1)
                            act.wait_ge(S["g_log"], n_)
                            act.activation(buf, buf, ACT.Exp, scale=-1.0).then_inc(S["g_sig"], 1)

                @block.tensor
                def _(pe):
                    for m, w in enumerate((wg, wu)):
                        pe.wait_ge(S["w_scaled"], m + 1)
                        if m:
                            pe.wait_ge(S["w_evac"], m * DC)
                        wf = three(w_f[:], HC)
                        for k in range(DC):
                            for c in range(HC):
                                dst = ps_s[:, 2 * k + c // 4, (c % 4) * P:(c % 4 + 1) * P]
                                last = pe.transpose(dst, wf[:, c, k * P:(k + 1) * P], ident[:])
                            last.then_inc(S["w_tr"], 1)
                    pe.wait_ge(S["w_scaled"], 3)
                    pe.wait_ge(S["w_evac"], 2 * DC)
                    wf = three(w_f[:], DC)
                    for c in range(HC):
                        for k in range(DC):
                            at = c * D + k * P
                            last = pe.transpose(ps_s[:, at // L, at % L:at % L + P], wf[:, k, c * P:(c + 1) * P], ident[:])
                    last.then_inc(S["w_tr"], 1)

                    def to_channels(dst, src, done):
                        for k in range(DC):
                            for j in range(LC):
                                last = pe.transpose(dst[:, k, j * P:(j + 1) * P], src[:, j, k * P:(k + 1) * P], ident[:])
                        last.then_inc(S[done], 1)

                    with pe.Fori(0, NB) as b:
                        pe.wait_ge(S["xm_ready"], b + 1)
                        for j in range(LC):
                            for k in range(DC):
                                last = pe.transpose(ps_a[:, j // 2, (j % 2) * D + k * P:(j % 2) * D + (k + 1) * P],
                                                    xm[:, k, j * P:(j + 1) * P], ident[:])
                        last.then_inc(S["x_tok"], 1)
                        pe.wait_ge(S["c_in"], 16 * (b + 1))
                        pe.wait_ge(S["normed"], 3 * b + 1)
                        to_channels(ps_b, cx, "c_tr")
                        pe.wait_ge(S["normed"], 3 * b + 2)
                        to_channels(ps_a, nrm, "q_tr")
                        pe.wait_ge(S["q_t_ready"], b + 1)
                        pe.wait_ge(S["c_t_ready"], b + 1)
                        for m, w in enumerate((igk, fgk)):
                            for k in range(GK):
                                src = qt[:, k, :] if k < DC else ct[:, k % DC, :]
                                last = pe.matmul(ps_s[0:NH, m, :], w[:, k, :], src, start=k == 0, stop=k == GK - 1)
                        last.then_inc(S["gates"], 1)
                        pe.wait_ge(S["ga_ready"], b + 1)
                        pe.wait_ge(S["ge_ready"], b + 1)
                        for j in range(LC):
                            for m, src in enumerate((ga, ge)):
                                last = pe.matmul(ps_s[:, 2, (2 * j + m) * NH:(2 * j + m + 1) * NH],
                                                 src[:, j * P:(j + 1) * P], ident[0:NH, 0:NH], start=True, stop=True)
                        last.then_inc(S["ae_tr"], 1)
                        pe.wait_ge(S["v_ready"], b + 1)
                        pe.wait_ge(S["ae_ready"], b + 1)

                        def attend(h):
                            pe.wait_ge(S["c_ready"], (b * NH + h + 1) * LC)
                            for j in range(LC):
                                for i in range(j + 1):
                                    last = pe.matmul(oh[j][:, h * (DH + 1):(h + 1) * (DH + 1)],
                                                     dm[:, h % 2, i, j * P:(j + 1) * P], v1[:, i, h, :],
                                                     start=i == 0, stop=i == j)
                            last.then_inc(S["av"], 1)

                        for h in range(NH):
                            at = (h % 2) * DH
                            if h:
                                pe.wait_ge(S["d_arg"], (b * NH + h) * LC)
                            pe.matmul(ps_s[:, 0, :], neg_sel[:, h:h + 1].broadcast_to([NH, P]), gm[:],
                                      start=True, stop=True).then_inc(S["m_bc"], 1)
                            for i in range(LC):
                                if i == 0 and h:
                                    pe.wait_ge(S["c_ready"], (b * NH + h) * LC)
                                if i == 3:
                                    pe.wait_ge(S["c_ready"], (b * NH + h) * LC + 1)
                                pe.matmul(ps_s[:, 1 + i % 3, i * P:L], ct[at:at + DH, h // 2, i * P:(i + 1) * P],
                                          qt[at:at + DH, h // 2, i * P:L], start=True, stop=True).then_inc(S["qk"], 1)
                            if h:
                                attend(h - 1)
                        attend(NH - 1)
                        pe.wait_ge(S["normed"], 3 * b + 3)
                        to_channels(ps_a, nrm, "x2_tr")
                        pe.wait_ge(S["x2t_ready"], b + 1)
                        for c in range(HC):
                            if c >= 2:
                                pe.wait_ge(S["gl_ready"], b * HC + c - 1)
                                pe.wait_ge(S["hid_ready"], b * HC + c - 1)
                            for w, bank, done in ((wg, c % 2, "ffn_g"), (wu, 2 + c % 2, "ffn_u")):
                                for k in range(DC):
                                    last = pe.matmul(ps_s[:, bank, :], w[:, k, c * P:(c + 1) * P], x2t[:, k, :],
                                                     start=k == 0, stop=k == DC - 1)
                                last.then_inc(S[done], 1)
                        pe.wait_ge(S["hid_ready"], (b + 1) * HC)
                        for j in range(LC):
                            for c in range(HC):
                                last = pe.matmul(ps_b[:, j // 2, (j % 2) * D:(j % 2 + 1) * D],
                                                 hid[:, c, j * P:(j + 1) * P], wd[:, c, :], start=c == 0, stop=c == HC - 1)
                            last.then_inc(S["down"], 1)

                @block.gpsimd
                def _(pool):
                    pool.memset(ones[:], 1.0).then_inc(S["set"], 1)
                    pool.memset(v1[:], 1.0).then_inc(S["set"], 1)
                    pool.wait_ge(S["set"], 2)
                    with pool.Fori(0, NB) as b:
                        def bc(w, reps):
                            return w[:].unsqueeze(1).broadcast_to([P, reps, D])
                        pool.wait_ge(S["normed"], 3 * b + 1)
                        pool.tensor_tensor(t_a[:], nrm[:], bc(lnw, LC), ALU.mult).then_inc(S["lnm_w"], 1)
                        pool.wait_ge(S["lnm_w"], b + 1)
                        pool.tensor_tensor(t_a[:], t_a[:], bc(lnb, LC), ALU.add).then_inc(S["lnm_b"], 1)
                        pool.wait_ge(S["lnm_b"], b + 1)
                        pool.wait_ge(S["x_in"], 16 * (b + 1))
                        pool.tensor_tensor(x1[:], t_a[:], xin[:], ALU.add).then_inc(S["x1_ready"], 1)
                        for h in range(NH):
                            pool.wait_ge(S["d_exp"], (b * NH + h + 1) * LC)
                            pool.tensor_tensor(carrier_p[:], eps[:, 0:1], eps[:, 0:1], ALU.add)
                            for i in range(LC):
                                blk = dm[:, h % 2, i, i * P:(i + 1) * P]
                                pool.affine_select(out=blk, in_=blk, compare_op=ALU.is_ge, fill=0.0, base=0,
                                                   pattern=[[1, P]], channel_multiplier=-1).then_inc(S["d_masked"], 1)
                        flat = osb[:].rearrange("p j h d -> p (j h) d")[:, :, 0:DH]
                        pool.wait_ge(S["o_evac"], (b + 1) * LC)
                        pool.wait_ge(S["h_mv"], b + 1)
                        pool.tensor_tensor(flat, flat, mv3[:, :, 0:1].broadcast_to([P, LC * NH, DH]),
                                           ALU.subtract).then_inc(S["h_sub"], 1)
                        pool.wait_ge(S["h_sub"], b + 1)
                        pool.wait_ge(S["h_k"], b + 1)
                        pool.tensor_tensor(flat, flat, kk[:].rearrange("p j h -> p (j h)").unsqueeze(2)
                                           .broadcast_to([P, LC * NH, DH]), ALU.mult).then_inc(S["h_mul"], 1)
                        pool.wait_ge(S["h_mul"], b + 1)
                        pool.tensor_tensor(t_a[:].rearrange("p j (h d) -> p j h d", h=NH), osb[:, :, :, 0:DH],
                                           onorm[:].rearrange("p (h d) -> p h d", h=NH).unsqueeze(1)
                                           .broadcast_to([P, LC, NH, DH]), ALU.mult).then_inc(S["h_scaled"], 1)
                        for c in range(HC):
                            n_ = b * HC + c + 1
                            pool.wait_ge(S["g_sig"], n_)
                            pool.tensor_tensor(gs[:, c % 2, :], gs[:, c % 2, :], gl[:, c % 2, :], ALU.mult).then_inc(S["g_silu"], 1)

                @block.vector
                def _(dve):
                    for m in range(3):
                        dve.wait_ge(S["w_in"], 16 * (m + 1))
                        if m:
                            dve.wait_ge(S["w_tr"], m * DC)
                        dve.tensor_scalar(w_f[:], w_int[:], FFN_SCALE, None, ALU.mult).then_inc(S["w_scaled"], 1)

                    def stats_of(parts, wait, count, stat, done, times):
                        dve.wait_ge(S[wait], count)
                        for m, part in enumerate(parts):
                            dve.bn_stats(stats3[:, m, :], part).then_inc(S[stat], 1)
                        dve.wait_ge(S[stat], times * len(parts))
                        dve.memset(carrier[:], 0.0)
                        for m in range(len(parts)):
                            last = dve.bn_aggr(mv3[:, m, :], stats3[:, m, :])
                        last.then_inc(S[done], 1)

                    def normalise(src, k):
                        dve.wait_ge(S["rstd"], k)
                        for j in range(LC):
                            last = dve.tensor_scalar(nrm[:, j, :], src(j), mv3[:, j, 0:1], lnv3[:, j:j + 1],
                                                     ALU.subtract, ALU.mult)
                        last.then_inc(S["normed"], 1)

                    with dve.Fori(0, NB) as b:
                        tok = lambda j: ps_a[:, j // 2, (j % 2) * D:(j % 2 + 1) * D]
                        stats_of([tok(j) for j in range(LC)], "x_tok", b + 1, "stats", "mv", 3 * b + 1)
                        normalise(tok, 3 * b + 1)
                        stats_of([x1[:, j, :] for j in range(LC)], "x1_ready", b + 1, "stats", "mv", 3 * b + 2)
                        normalise(lambda j: x1[:, j, :], 3 * b + 2)
                        dve.wait_ge(S["f_log"], b + 1)
                        dve.wait_ge(S["f_relu"], b + 1)
                        dve.tensor_tensor(fa[:], fa[:], fr_[:], ALU.add).then_inc(S["f_sum"], 1)
                        dve.wait_ge(S["f_sum"], b + 1)
                        dve.tensor_tensor_scan(ncs[:], ones[:], fa[:], 0.0, ALU.mult, ALU.add).then_inc(S["cs_ready"], 1)
                        dve.wait_ge(S["cs_ready"], b + 1)
                        dve.tensor_tensor(ga[:], ga[:], ncs[:], ALU.add).then_inc(S["ga_ready"], 1)
                        dve.wait_ge(S["ga_ready"], b + 1)
                        dve.tensor_tensor_scan(gm[:], ga[:], ga[:], -3.0e38, ALU.max, ALU.max).then_inc(S["gm_ready"], 1)
                        dve.wait_ge(S["gm_ready"], b + 1)
                        dve.tensor_tensor(ge[:], ncs[:], gm[:], ALU.subtract).then_inc(S["ge_diff"], 1)
                        dve.wait_ge(S["ae_ready"], b + 1)
                        for h in range(NH):
                            dve.wait_ge(S["m_bc"], b * NH + h + 1)
                            if h >= 2:
                                dve.wait_ge(S["av"], b * NH + h - 1)
                            for i in range(LC):
                                dve.tensor_scalar(dm[:, h % 2, i, i * P:L], ps_s[:, 0, i * P:L], ae[:, i, h:h + 1],
                                                  0.0, ALU.add, ALU.min).then_inc(S["d_arg"], 1)
                            for i in range(LC):
                                n_ = (b * NH + h) * LC + i + 1
                                dve.wait_ge(S["qk"], n_)
                                dve.wait_ge(S["d_masked"], n_)
                                blk = dm[:, h % 2, i, i * P:L]
                                dve.scalar_tensor_tensor(blk, ps_s[:, 1 + i % 3, i * P:L], DH ** -0.5, blk,
                                                         ALU.mult, ALU.mult).then_inc(S["c_ready"], 1)
                        row_sum = osb[:, :, :, DH]
                        dve.wait_ge(S["o_evac"], (b + 1) * LC)
                        dve.scalar_tensor_tensor(den[:], row_sum, -1.0, ae[:, :, NH:2 * NH], ALU.mult,
                                                 ALU.max).then_inc(S["h_neg"], 1)
                        dve.wait_ge(S["h_neg"], b + 1)
                        dve.tensor_tensor(den[:], row_sum, den[:], ALU.max).then_inc(S["h_den"], 1)
                        stats_of([osb[:, j, h, 0:DH] for j in range(LC) for h in range(NH)], "o_evac", (b + 1) * LC,
                                 "h_stats", "h_mv", b + 1)
                        dve.wait_ge(S["h_den"], b + 1)
                        dve.tensor_scalar(den[:], den[:], EPS_MLSTM, None, ALU.add).then_inc(S["h_rec"], 1)
                        dve.wait_ge(S["h_rec"], 3 * b + 1)
                        dve.reciprocal(den[:], den[:]).then_inc(S["h_rec"], 1)
                        dve.wait_ge(S["h_rec"], 3 * b + 2)
                        dve.tensor_tensor(kk[:], den[:], den[:], ALU.mult).then_inc(S["h_rec"], 1)
                        dve.wait_ge(S["h_rec"], 3 * b + 3)
                        dve.wait_ge(S["h_mv"], b + 1)
                        dve.tensor_tensor(kk[:], kk[:], mv3[:, :, 1].rearrange("p (j h) -> p j h", h=NH),
                                          ALU.mult).then_inc(S["h_t2"], 1)
                        dve.wait_ge(S["h_rs"], b + 1)
                        dve.tensor_tensor(kk[:], kk[:], den[:], ALU.mult).then_inc(S["h_k"], 1)
                        dve.wait_ge(S["h_scaled"], b + 1)
                        dve.tensor_tensor(x2[:], t_a[:], x1[:], ALU.add).then_inc(S["x2_ready"], 1)
                        stats_of([x2[:, j, :] for j in range(LC)], "x2_ready", b + 1, "stats", "mv", 3 * b + 3)
                        normalise(lambda j: x2[:, j, :], 3 * b + 3)
                        for c in range(HC):
                            n_ = b * HC + c + 1
                            dve.wait_ge(S["gl_ready"], n_)
                            dve.tensor_scalar(gs[:, c % 2, :], gl[:, c % 2, :], SIG_MIN, None, ALU.max).then_inc(S["g_cl"], 1)
                            dve.wait_ge(S["g_silu"], n_)
                            dve.wait_ge(S["ffn_u"], n_)
                            dve.tensor_tensor(hid[:, c, :], gs[:, c % 2, :], ps_s[:, 2 + c % 2, :], ALU.mult).then_inc(S["hid_ready"], 1)
                        dve.wait_ge(S["out_free"], 16 * (b + 1))
                        for j in range(LC):
                            dve.wait_ge(S["down"], b * LC + 2 * (j // 2) + 2)
                            dve.tensor_tensor(o_sb[:, j, :], x2[:, j, :], ps_b[:, j // 2, (j % 2) * D:(j % 2 + 1) * D],
                                              ALU.add).then_inc(S["out_ready"], 1)


_INS = ['x', 'ctx_1024', 'L0_attn_rms_w', 'L0_attn_W_in', 'L0_attn_conv_w', 'L0_attn_conv_b', 'L0_attn_W_x',
        'L0_attn_W_dt', 'L0_attn_b_dt', 'L0_attn_A_log', 'L0_attn_Dp', 'L0_attn_W_out', 'L0_attn_ln_w',
        'L0_attn_ln_b', 'L0_xattn_igate_kernel', 'L0_xattn_igate_bias', 'L0_xattn_fgate_kernel',
        'L0_xattn_fgate_bias', 'L0_xattn_outnorm_scale', 'L0_ffn_w_gate', 'L0_ffn_w_up', 'L0_ffn_w_down']


def kernel(**inputs):
    import numpy as _np
    import concourse.bacc as _bacc
    from concourse import mybir as _mybir
    from concourse.bass_utils import run_bass_kernel_spmd as _run

    nc = _bacc.Bacc("TRN2", target_bir_lowering=False, num_devices=1)
    arrays, args = {}, []
    for name in _INS:
        a = _np.ascontiguousarray(inputs[name])
        arrays[f"in_{name}_dram"] = a
        args.append(nc.dram_tensor(f"in_{name}_dram", a.shape, _mybir.dt.from_np(a.dtype), kind="ExternalInput").ap())
    shape = inputs['x'].shape
    args.append(nc.dram_tensor("out_0_dram", shape, _mybir.dt.float32, kind="ExternalOutput").ap())
    build(nc, *args)
    r = _run(nc, [arrays], core_ids=[0])
    return r.results[0]["out_0_dram"]
```

```python
def build(nc, x, ctx_1024, rms_w, W_in, conv_w, conv_b, W_x, W_dt, b_dt, A_log, Dp, W_out, ln_w, ln_b,
          igate_kernel, igate_bias, fgate_kernel, fgate_bias, outnorm_scale, w_gate, w_up, w_down, out):
    import concourse.bass as bass
    from concourse import mybir
    from contextlib import ExitStack

    F32 = mybir.dt.float32
    I32 = mybir.dt.int32
    ACT = mybir.ActivationFunctionType
    ALU = mybir.AluOpType
    ds = bass.ds

    P = 128
    NB, L, D = x.shape
    ED, KC = conv_w.shape
    R = W_dt.shape[0]
    N = A_log.shape[1]
    NH = igate_bias.shape[0]
    DH = D // NH
    HID = w_gate.shape[0]
    DC, EC, LC, HC = D // P, ED // P, L // P, HID // P
    DEPTH = 6
    STAGES = DEPTH * NB
    EPS, EPS_MLSTM, FFN_SCALE = 1e-5, 1e-6, 1.0 / 127.0
    SIG_MIN = -40.0
    DBC = R + 2 * N

    SLOTS = [
        [("ms", 0)],
        [("xs", 0), ("xs", 1)],
        [("cv", 0)],
        [("xs", 2), ("y", 0), ("y", 1)],
        [("cv", 1)],
        [("xs", 3), ("y", 2), ("y", 3)],
        [("cv", 2)],
        [("cv", 3)],
        [("o", 0)],
        [("bc", 0)],
        [("o", 1), ("dl", 0)],
        [("dl", 1), ("cl", 0)],
        [("dl", 2), ("z", 0)],
        [("dl", 3), ("dx", 0), ("z", 1)],
        [("dx", 1), ("dx", 2), ("z", 2)],
        [("dx", 3), ("z", 3)],
    ]
    V_CLAMP_AT, V_SIG_AT, XC_AT = (2, 4, 6, 7), (3, 5, 7, 8), (3, 5, 7, 8)
    Z_CLAMP_AT, Z_SIG_AT, GATE_AT = (3, 3, 8, 8), (4, 6, 9, 10), (5, 7, 10, 11)
    YG_AT, DELTA_AT, U_AT, RESIDUAL_AT = (1, 1, 2, 2), (11, 12, 13, 14), 0, 11
    BACK = ("y", "o")

    def steps(n, back, front):
        return [k for k in SLOTS[n] if (back if k[0] in BACK else front)]

    N_BACK = sum(k[0] in BACK for s in SLOTS for k in s)
    N_FRONT = sum(len(s) for s in SLOTS) - N_BACK
    N_ALL = N_BACK + N_FRONT

    NHB = 3

    def hb_of(n):
        return n % NHB if n < N - 1 else 1

    def hb_age(n):
        m = n - 1
        while hb_of(m % N) != hb_of(n):
            m -= 1
        return n - m

    top = ExitStack()
    with top:
        def sem(name):
            return top.enter_context(nc.semaphore(name))

        def sb(stack, name, shape, dt=F32):
            return stack.enter_context(nc.sbuf_tensor(name, shape, dt))

        def pb(stack, name, shape):
            return stack.enter_context(nc.psum_tensor(name, shape, F32))

        xT = sb(top, "xT", [P, NB, DC, L])
        ident = sb(top, "ident", [P, P])
        eps = sb(top, "eps", [P, 2])

        mamba = ExitStack()
        with mamba:
            w_in = sb(mamba, "w_in", [P, DC, 2 * ED])
            w_x = sb(mamba, "w_x", [P, EC, DBC])
            w_dt = sb(mamba, "w_dt", [R, ED])
            w_out = sb(mamba, "w_out", [P, EC, D])
            conv_diag = sb(mamba, "conv_diag", [P, EC, KC, P])
            d_diag = sb(mamba, "d_diag", [P, EC, P])
            mean_mat = sb(mamba, "mean_mat", [P, P])
            neg_a = sb(mamba, "neg_a", [P, EC, N])
            cb = sb(mamba, "cb", [P, EC])
            bdt = sb(mamba, "bdt", [P, EC])

            w_loaded, x_loaded = sem("w_loaded"), sem("x_loaded")
            const_set, weights_set, a_exp = sem("const_set"), sem("weights_set"), sem("a_exp")
            ln_stats, ln_mv, ln_log, ln_rstd, ln_out = (sem("ln_stats"), sem("ln_mv"), sem("ln_log"),
                                                        sem("ln_rstd"), sem("ln_out"))
            ln_tr = sem("ln_tr")
            x_ready = sem("x_ready")

            with ExitStack() as s1:
                x_nat = sb(s1, "x_nat", [P, NB, LC, D])
                rmsw = sb(s1, "rmsw", [P, DC])
                cw = sb(s1, "cw", [P, EC, KC])
                dcol = sb(s1, "dcol", [P, EC])
                stats = sb(s1, "stats", [P, LC, 6])
                mv = sb(s1, "mv", [P, LC, 2])
                lnv = sb(s1, "lnv", [P, LC])
                xn = sb(s1, "xn", [P, LC, D])
                carrier1 = sb(s1, "carrier1", [P, 1])
                pt = pb(s1, "pt", [P, DC, L])
                N_LOADS = 10
                with nc.Block() as block:
                    @block.sync
                    def _(sp):
                        sp.dma_start(x_nat[:, 0], x[0].rearrange("(j p) d -> p j d", p=P)).then_inc(x_loaded, 16)
                        sp.dma_start(x_nat[:, 1:NB], x[1:NB].rearrange("b (j p) d -> p b j d", p=P)).then_inc(x_loaded, 16)
                        sp.dma_start(w_in[:], W_in.rearrange("(k p) e -> p k e", p=P)).then_inc(w_loaded, 16)
                        sp.dma_start(w_x[:], W_x.rearrange("(c p) m -> p c m", p=P)).then_inc(w_loaded, 16)
                        sp.dma_start(w_dt[:], W_dt).then_inc(w_loaded, 16)
                        sp.dma_start(w_out[:], W_out.rearrange("(c p) d -> p c d", p=P)).then_inc(w_loaded, 16)

                    @block.gpsimd
                    def _(pool):
                        pool.memset(ident[:], 0.0).then_inc(const_set, 1)
                        pool.wait_ge(const_set, 1)
                        pool.affine_select(out=ident[:], in_=ident[:], compare_op=ALU.not_equal, fill=1.0,
                                           base=0, pattern=[[-1, P]], channel_multiplier=1).then_inc(const_set, 1)
                        pool.memset(mean_mat[:], 1.0 / D).then_inc(weights_set, 1)
                        pool.memset(eps[:, 0:1], EPS).then_inc(const_set, 1)
                        pool.memset(eps[:, 1:2], EPS_MLSTM).then_inc(const_set, 1)
                        pool.wait_ge(const_set, 2)
                        pool.wait_ge(w_loaded, 16 * N_LOADS)
                        for c in range(EC):
                            for k in range(KC):
                                pool.tensor_scalar(conv_diag[:, c, k, :], ident[:], cw[:, c, k:k + 1], None,
                                                   ALU.mult).then_inc(weights_set, 1)
                            pool.tensor_scalar(d_diag[:, c, :], ident[:], dcol[:, c:c + 1], None,
                                               ALU.mult).then_inc(weights_set, 1)
                        for k in range(DC):
                            pool.tensor_scalar(w_in[:, k, :], w_in[:, k, :], rmsw[:, k:k + 1], None,
                                               ALU.mult).then_inc(weights_set, 1)
                        pool.wait_ge(a_exp, 1)
                        pool.tensor_scalar(neg_a[:], neg_a[:], -1.0, None, ALU.mult).then_inc(weights_set, 1)

                    @block.scalar
                    def _(act):
                        act.dma_start(cw[:], conv_w.rearrange("(c p) k -> p c k", p=P)).then_inc(w_loaded, 16)
                        act.dma_start(neg_a[:], A_log.rearrange("(c p) n -> p c n", p=P)).then_inc(w_loaded, 16)
                        for dst, src in ((rmsw, rms_w), (cb, conv_b), (bdt, b_dt), (dcol, Dp)):
                            act.dma_start(dst[:], src.rearrange("(c p) -> p c", p=P),
                                          allow_slow_non_contiguous=True).then_inc(w_loaded, 16)
                        act.preload_act_table_set("natural_log_exp_and_others")
                        act.wait_ge(w_loaded, 16 * N_LOADS)
                        act.activation(neg_a[:], neg_a[:], ACT.Exp).then_inc(a_exp, 1)
                        act.wait_ge(const_set, 4)
                        with act.Fori(0, NB) as b:
                            act.wait_ge(ln_mv, b + 1)
                            act.activation(lnv[:], mv[:, :, 1], ACT.Ln, bias=eps[:, 0:1]).then_inc(ln_log, 1)
                            act.wait_ge(ln_log, b + 1)
                            act.activation(lnv[:], lnv[:], ACT.Exp, scale=-0.5).then_inc(ln_rstd, 1)
                            act.wait_ge(ln_tr, b + 1)
                            act.activation(xT[:, ds(b, 1), :, :], pt[:], ACT.Copy).then_inc(x_ready, 1)

                    @block.vector
                    def _(dve):
                        dve.wait_ge(x_loaded, 32)
                        with dve.Fori(0, NB) as b:
                            for j in range(LC):
                                dve.bn_stats(stats[:, j, :], x_nat[:, ds(b, 1), j, :]).then_inc(ln_stats, 1)
                            dve.wait_ge(ln_stats, (b + 1) * LC)
                            dve.memset(carrier1[:], 0.0)
                            for j in range(LC):
                                last = dve.bn_aggr(mv[:, j, :], stats[:, j, :])
                            last.then_inc(ln_mv, 1)
                            dve.wait_ge(ln_rstd, b + 1)
                            for j in range(LC):
                                last = dve.tensor_scalar(xn[:, j, :], x_nat[:, ds(b, 1), j, :], mv[:, j, 0:1],
                                                         lnv[:, j:j + 1], ALU.subtract, ALU.mult)
                            last.then_inc(ln_out, 1)
                            dve.wait_ge(ln_tr, b + 1)

                    @block.tensor
                    def _(pe):
                        pe.wait_ge(const_set, 2)
                        with pe.Fori(0, NB) as b:
                            pe.wait_ge(ln_out, b + 1)
                            for k in range(DC):
                                for j in range(LC):
                                    last = pe.transpose(pt[:, k, j * P:(j + 1) * P], xn[:, j, k * P:(k + 1) * P],
                                                        ident[:])
                            last.then_inc(ln_tr, 1)
                            pe.wait_ge(x_ready, b + 1)

            with ExitStack() as s2:
                sq = sb(s2, "sq", [P, DC, L])
                rstd = sb(s2, "rstd", [P, L])
                u = sb(s2, "u", [P, DC, L])
                PAD = KC - 1
                xs = sb(s2, "xs", [P, 2, L + PAD])
                xc = sb(s2, "xc", [P, EC, L])
                sg = sb(s2, "sg", [P, 2, L])
                dbc = sb(s2, "dbc", [DBC, 2, L])
                c_tok = sb(s2, "c_tok", [P, 2, LC, N])
                delta = sb(s2, "delta", [P, 2, EC, L])
                dx = sb(s2, "dx", [P, 2, EC, L])
                pos = sb(s2, "pos", [P, 2, L])
                zl = sb(s2, "zl", [P, LC, ED])
                g = sb(s2, "g", [P, LC, ED])
                acc = sb(s2, "acc", [P, 2, LC, ED])
                da = sb(s2, "da", [P, 2, EC, L])
                hb = sb(s2, "hb", [P, NHB, EC, L])
                b_all = sb(s2, "b_all", [P, 2, L])
                ht = pb(s2, "ht", [P, LC, ED])
                bb = pb(s2, "bb", [P, 2, L])
                fr = pb(s2, "fr", [P, 2, L])

                pads = sem("pads")
                front_full, front_free = sem("front_full"), sem("front_free")
                sq_ready, rms_log, rstd_ready, u_ready = (sem("sq_ready"), sem("rms_log"), sem("rstd_ready"),
                                                          sem("u_ready"))
                v_ready, v_clamped, v_exp, v_log, v_sig, xc_ready = (
                    sem("v_ready"), sem("v_clamped"), sem("v_exp"), sem("v_log"), sem("v_sig"), sem("xc_ready"))
                z_ready, z_clamped, z_exp, z_log, z_sig, g_ready = (
                    sem("z_ready"), sem("z_clamped"), sem("z_exp"), sem("z_log"), sem("z_sig"), sem("g_ready"))
                p_abs, p_pos, p_exp, p_log, delta_ready, dx_ready = (
                    sem("p_abs"), sem("p_pos"), sem("p_exp"), sem("p_log"), sem("delta_ready"), sem("dx_ready"))
                xs_ready, dbc_ready, c_ready, acc_set = sem("xs_ready"), sem("dbc_ready"), sem("c_ready"), sem("acc_set")
                yg_ready, yt_ready, o_ready = sem("yg_ready"), sem("yt_ready"), sem("o_ready")
                b_bcast, b_ready = sem("b_bcast"), sem("b_ready")
                da_ready, dbx_ready, scanned, h_tr, y_added = (sem("da_ready"), sem("dbx_ready"), sem("scanned"),
                                                               sem("h_tr"), sem("y_added"))

                class Stage:

                    def __init__(self, s, par, base, phase):
                        self.s, self.par, self.base, self.phase = s, par, base, phase

                    def bank(self, k):
                        return (self.phase + k) % 2

                def emit_act_step(act, st, k, kind, i):
                    s, nx = st.s, st.s + 1
                    q = 1 - st.par
                    bank = fr[:, st.bank(k), :]
                    act.wait_ge(front_full, st.base + k + 1)
                    if kind == "z":
                        if not st.is_prelude:
                            act.wait_ge(g_ready, LC * s + i + 1)
                        act.activation(zl[:, i, :], bank, ACT.Copy).then_inc(front_free, 1)
                    elif kind == "ms":
                        act.activation(rstd[:], bank, ACT.Ln, bias=eps[:, 0:1]).then_inc(front_free, 1)
                        act.wait_ge(front_free, st.base + k + 1)
                        act.activation(rstd[:], rstd[:], ACT.Exp, scale=-0.5).then_inc(rstd_ready, 1)
                    elif kind == "xs":
                        act.activation(xs[:, i % 2, PAD:], bank, ACT.Copy).then_inc(front_free, 1)
                    elif kind == "cv":
                        if i == 0 and not st.is_prelude:
                            act.wait_ge(dx_ready, EC * nx)
                        act.activation(xc[:, i, :], bank, ACT.Identity, bias=cb[:, i:i + 1]).then_inc(front_free, 1)
                    elif kind == "y":
                        act.activation(dx[:, q, i, :], bank, ACT.Copy).then_inc(front_free, 1)
                    elif kind == "o":
                        act.activation(sq[:, i, :], bank, ACT.Copy).then_inc(front_free, 1)
                    elif kind == "bc":
                        act.activation(dbc[:, q, :], fr[0:DBC, st.bank(k), :], ACT.Copy).then_inc(front_free, 1)
                    elif kind == "cl":
                        if not (st.is_prelude or st.is_first):
                            act.wait_ge(y_added, LC * N * s)
                        act.activation(c_tok[:, q], bank[:, 0:LC * N].rearrange("p (j n) -> p j n", n=N),
                                       ACT.Copy).then_inc(front_free, 1)
                    elif kind == "dx":
                        act.activation(acc[:, q, i, :], bank, ACT.Copy).then_inc(front_free, 1)
                    elif kind == "dl":
                        act.activation(delta[:, q, i, :], bank, ACT.Abs, bias=bdt[:, i:i + 1]).then_inc(p_abs, 1)
                        if i < 2:
                            if not st.is_prelude:
                                act.wait_ge(delta_ready, EC * nx)
                        else:
                            act.wait_ge(delta_ready, EC * nx + i - 1)
                        act.activation(pos[:, i % 2, :], bank, ACT.Relu, bias=bdt[:, i:i + 1]).then_inc(front_free, 1)
                        act.wait_ge(p_abs, EC * nx + i + 1)
                        act.activation(delta[:, q, i, :], delta[:, q, i, :], ACT.Exp, scale=-1.0).then_inc(p_exp, 1)
                        act.wait_ge(p_exp, EC * nx + i + 1)
                        act.activation(delta[:, q, i, :], delta[:, q, i, :], ACT.Ln, bias=1.0).then_inc(p_log, 1)

                def emit_act_sigmoid(act, buf, clamped, e, l, sig, count):
                    act.wait_ge(clamped, count)
                    act.activation(buf, buf, ACT.Exp, scale=-1.0).then_inc(e, 1)
                    act.wait_ge(e, count)
                    act.activation(buf, buf, ACT.Ln, bias=1.0).then_inc(l, 1)
                    act.wait_ge(l, count)
                    act.activation(buf, buf, ACT.Exp, scale=-1.0).then_inc(sig, 1)

                def emit_act_squares(act, nx, b):
                    act.wait_ge(x_ready, nx + 1)
                    act.wait_ge(x_ready, nx + (NB - 2))
                    act.activation(sq[:], xT[:, ds(b, 1), :, :], ACT.Square).then_inc(sq_ready, 1)

                def emit_act_decay(act, s, par, n, warm):
                    if n == 0:
                        act.wait_ge(delta_ready, EC * s + EC)
                    if warm:
                        act.wait_ge(scanned, N * s + n - 1)
                    for c in range(EC):
                        last = act.activation(da[:, n % 2, c, 1:L], delta[:, par, c, 1:L], ACT.Exp,
                                              scale=neg_a[:, c, n:n + 1])
                    last.then_inc(da_ready, 1)

                def emit_act_b(act, s, n, warm):
                    act.wait_ge(b_bcast, N * s + n + 1)
                    if warm:
                        act.wait_ge(dbx_ready, N * s + n - 1)
                    act.activation(b_all[:, n % 2, :], bb[:, n % 2, :], ACT.Copy).then_inc(b_ready, 1)

                def act_stage(act, st, back, gate, front, scan, next_scan, first=False):
                    s, k = st.s, 0
                    for n in range(N):
                        if n == 0 and front:
                            emit_act_squares(act, s + 1, (s + 1) % NB)
                        if scan:
                            if n + 1 < N:
                                emit_act_decay(act, s, st.par, n + 1, not first or n + 1 >= 2)
                            elif next_scan:
                                emit_act_decay(act, s + 1, 1 - st.par, 0, True)
                        for kind, i in steps(n, back, front):
                            emit_act_step(act, st, k, kind, i)
                            k += 1
                        if scan:
                            if n + 2 < N:
                                emit_act_b(act, s, n + 2, True)
                            elif next_scan:
                                emit_act_b(act, s + 1, n + 2 - N, True)
                        for i in range(EC):
                            if front and n == V_SIG_AT[i]:
                                emit_act_sigmoid(act, sg[:, i % 2, :], v_clamped, v_exp, v_log, v_sig,
                                                 EC * (s + 1) + i + 1)
                            if gate and n == Z_SIG_AT[i]:
                                emit_act_sigmoid(act, g[:, i, :], z_clamped, z_exp, z_log, z_sig, LC * s + i + 1)

                def emit_pe_step(pe, st, k, kind, i):
                    s, nx = st.s, st.s + 1
                    q = 1 - st.par
                    b_ = st.bank(k)
                    bank = fr[:, b_, :]
                    if not (st.is_prelude and k < 2):
                        pe.wait_ge(front_free, st.base + k - 1)

                    if kind == "z":
                        pe.wait_ge(u_ready, nx + 1)
                        for d in range(DC):
                            last = pe.matmul(bank, u[:, d, i * P:(i + 1) * P], w_in[:, d, ED:2 * ED],
                                             start=d == 0, stop=d == DC - 1)
                    elif kind == "ms":
                        pe.wait_ge(sq_ready, nx + 1)
                        for d in range(DC):
                            last = pe.matmul(bank, mean_mat[:], sq[:, d, :], start=d == 0, stop=d == DC - 1)
                    elif kind == "xs":
                        pe.wait_ge(u_ready, nx + 1)
                        for d in range(DC):
                            last = pe.matmul(bank, w_in[:, d, i * P:(i + 1) * P], u[:, d, :],
                                             start=d == 0, stop=d == DC - 1)
                    elif kind == "cv":
                        pe.wait_ge(front_free, st.base + xs_step(st, i) + 1)
                        for t in range(KC):
                            last = pe.matmul(bank, conv_diag[:, i, t, :], xs[:, i % 2, t:t + L],
                                             start=t == 0, stop=t == KC - 1)
                    elif kind == "y":
                        pe.wait_ge(yg_ready, LC * s)
                        for j in range(LC):
                            last = pe.transpose(bank[:, j * P:(j + 1) * P], acc[:, q, j, i * P:(i + 1) * P], ident[:])
                    elif kind == "o":
                        pe.wait_ge(front_free, st.base + k_of(st, "y", EC - 1) + 1)
                        for c in range(EC):
                            last = pe.matmul(bank, w_out[:, c, i * P:(i + 1) * P], dx[:, q, c, :],
                                             start=c == 0, stop=c == EC - 1)
                    elif kind == "bc":
                        pe.wait_ge(xc_ready, EC * nx + EC)
                        for c in range(EC):
                            last = pe.matmul(fr[0:DBC, b_, :], w_x[:, c, :], xc[:, c, :], start=c == 0, stop=c == EC - 1)
                    elif kind == "dl":
                        pe.wait_ge(front_free, st.base + k_of(st, "bc", 0) + 1)
                        last = pe.matmul(bank, w_dt[:, i * P:(i + 1) * P], dbc[0:R, q, :], start=True, stop=True)
                    elif kind == "cl":
                        for j in range(LC):
                            for c in range(EC):
                                last = pe.matmul(bank[:, j * N:(j + 1) * N], xc[:, c, j * P:(j + 1) * P],
                                                 w_x[:, c, R + N:DBC], start=c == 0, stop=c == EC - 1)
                    elif kind == "dx":
                        for c in range(EC):
                            last = pe.matmul(bank[:, c * P:(c + 1) * P], xc[:, c, i * P:(i + 1) * P],
                                             d_diag[:, c, :], start=True, stop=True)
                    last.then_inc(front_full, 1)

                def k_of(st, kind, i):
                    return st.order.index((kind, i))

                def xs_step(st, i):
                    return k_of(st, "xs", i)

                def emit_pe_b(pe, s, par, n, warm):
                    if warm:
                        pe.wait_ge(b_ready, N * s + n - 1)
                    pe.matmul(bb[:, n % 2, :], ident[R:R + N, R + n:R + n + 1].broadcast_to([N, P]),
                              dbc[R:R + N, par, :], start=True, stop=True).then_inc(b_bcast, 1)

                def emit_pe_transposes(pe, s, n, warm):
                    pe.wait_ge(scanned, N * s + n + 1)
                    for j in range(LC):
                        if warm:
                            pe.wait_ge(y_added, LC * (N * s + n - 1) + j + 1)
                        for c in range(EC):
                            last = pe.transpose(ht[:, j, c * P:(c + 1) * P], hb[:, hb_of(n), c, j * P:(j + 1) * P],
                                                ident[:])
                        last.then_inc(h_tr, 1)

                def pe_stage(pe, st, back, gate, front, scan, next_scan, first=False):
                    s, k = st.s, 0
                    for n in range(N):
                        for kind, i in steps(n, back, front):
                            emit_pe_step(pe, st, k, kind, i)
                            k += 1
                        if scan:
                            if n + 2 < N:
                                emit_pe_b(pe, s, st.par, n + 2, True)
                            elif next_scan:
                                emit_pe_b(pe, s + 1, 1 - st.par, n + 2 - N, True)
                            emit_pe_transposes(pe, s, n, not first or n > 0)

                def emit_pool_dbx(pool, s, par, n, warm):
                    pool.wait_ge(b_ready, N * s + n + 1)
                    if n == 0:
                        pool.wait_ge(dx_ready, EC * s + EC)
                    if warm:
                        pool.wait_ge(h_tr, LC * (N * s + n - hb_age(n) + 1))
                    pool.tensor_tensor(hb[:, hb_of(n)], dx[:, par],
                                       b_all[:, n % 2:n % 2 + 1, :].broadcast_to([P, EC, L]),
                                       ALU.mult).then_inc(dbx_ready, 1)

                def emit_pool_rms(pool, nx, b):
                    pool.wait_ge(rstd_ready, nx + 1)
                    pool.tensor_tensor(u[:], xT[:, ds(b, 1), :, :], rstd[:].unsqueeze(1).broadcast_to([P, DC, L]),
                                       ALU.mult).then_inc(u_ready, 1)

                def emit_pool_xc(pool, nx, i):
                    pool.wait_ge(v_sig, EC * nx + i + 1)
                    pool.tensor_tensor(xc[:, i, :], xc[:, i, :], sg[:, i % 2, :], ALU.mult).then_inc(xc_ready, 1)

                def emit_pool_delta(pool, nx, q, i):
                    pool.wait_ge(p_log, EC * nx + i + 1)
                    pool.tensor_tensor(delta[:, q, i, :], delta[:, q, i, :], pos[:, i % 2, :],
                                       ALU.add).then_inc(delta_ready, 1)
                    pool.wait_ge(delta_ready, EC * nx + i + 1)
                    pool.tensor_tensor(dx[:, q, i, :], delta[:, q, i, :], xc[:, i, :], ALU.mult).then_inc(dx_ready, 1)

                def emit_pool_gate(pool, s, i):
                    pool.wait_ge(z_sig, LC * s + i + 1)
                    pool.tensor_tensor(g[:, i, :], g[:, i, :], zl[:, i, :], ALU.mult).then_inc(g_ready, 1)

                def emit_pool_yg(pool, s, q, j):
                    pool.wait_ge(y_added, LC * N * s - LC + j + 1)
                    pool.wait_ge(g_ready, LC * (s - 1) + j + 1)
                    pool.tensor_tensor(acc[:, q, j, :], acc[:, q, j, :], g[:, j, :], ALU.mult).then_inc(yg_ready, 1)

                def pool_stage(pool, st, back, gate, front, scan, next_scan, first=False):
                    s, q = st.s, 1 - st.par
                    for n in range(N):
                        if scan:
                            if n + 1 < N:
                                emit_pool_dbx(pool, s, st.par, n + 1, not first or n + 1 >= NHB)
                            elif next_scan:
                                emit_pool_dbx(pool, s + 1, q, 0, True)
                        if front and n == U_AT:
                            if not st.is_prelude:
                                pool.wait_ge(front_free, st.base)
                            emit_pool_rms(pool, s + 1, (s + 1) % NB)
                        for i in range(EC):
                            if front and n == XC_AT[i]:
                                emit_pool_xc(pool, s + 1, i)
                            if back and n == YG_AT[i]:
                                emit_pool_yg(pool, s, q, i)
                            if gate and n == GATE_AT[i]:
                                emit_pool_gate(pool, s, i)
                            if front and n == DELTA_AT[i]:
                                if i == 0 and back:
                                    pool.wait_ge(front_free, st.base + k_of(st, "o", DC - 1) + 1)
                                emit_pool_delta(pool, s + 1, q, i)

                def emit_dve_scan(dve, s, n):
                    dve.wait_ge(da_ready, N * s + n + 1)
                    dve.wait_ge(dbx_ready, N * s + n + 1)
                    h = hb[:, hb_of(n)].rearrange("p c l -> p (c l)")
                    dve.tensor_tensor_scan(h, da[:, n % 2].rearrange("p c l -> p (c l)"), h, 0.0,
                                           ALU.mult, ALU.add).then_inc(scanned, 1)

                def emit_dve_y(dve, s, par, n, st=None):
                    for j in range(LC):
                        dve.wait_ge(h_tr, LC * (N * s + n) + j + 1)
                        if n > 0:
                            dve.wait_ge(y_added, LC * (N * s + n - 1) + j + 1)
                        dve.scalar_tensor_tensor(acc[:, par, j, :], ht[:, j, :], c_tok[:, par, j, n:n + 1],
                                                 acc[:, par, j, :], ALU.mult, ALU.add).then_inc(y_added, 1)

                def emit_dve_residual(dve, st, s, b):
                    dve.wait_ge(front_free, st.base + k_of(st, "o", DC - 1) + 1)
                    dve.scalar_tensor_tensor(xT[:, ds(b, 1), :, :].rearrange("p b k l -> p (b k l)"),
                                             xT[:, ds(b, 1), :, :].rearrange("p b k l -> p (b k l)"), 2.0,
                                             sq[:].rearrange("p k l -> p (k l)"), ALU.mult, ALU.add).then_inc(x_ready, 1)

                def emit_dve_clamp_v(dve, st, nx, i):
                    dve.wait_ge(front_free, st.base + k_of(st, "cv", i) + 1)
                    if i >= 2:
                        dve.wait_ge(xc_ready, EC * nx + i - 1)
                    dve.tensor_scalar(sg[:, i % 2, :], xc[:, i, :], SIG_MIN, None, ALU.max).then_inc(v_clamped, 1)

                def emit_dve_clamp_z(dve, st, s, i):
                    dve.wait_ge(front_free, st.base)
                    dve.tensor_scalar(g[:, i, :], zl[:, i, :], SIG_MIN, None, ALU.max).then_inc(z_clamped, 1)

                def dve_stage(dve, st, back, gate, front, scan, next_scan, first=False, acc_base=None):
                    s = st.s
                    for n in range(N):
                        if scan:
                            emit_dve_scan(dve, s, n)
                            if n == 0:
                                if back:
                                    emit_dve_y(dve, s - 1, 1 - st.par, N - 1)
                            else:
                                if n == 1:
                                    dve.wait_ge(front_free, st.base)
                                emit_dve_y(dve, s, st.par, n - 1)
                        for i in range(EC):
                            if front and n == V_CLAMP_AT[i]:
                                emit_dve_clamp_v(dve, st, s + 1, i)
                            if gate and n == Z_CLAMP_AT[i]:
                                if i == 0 and back:
                                    dve.wait_ge(yg_ready, LC * s)
                                emit_dve_clamp_z(dve, st, s, i)
                        if back and n == RESIDUAL_AT:
                            emit_dve_residual(dve, st, s, (s - 1 + NB) % NB)

                def make(s, par, base, phase, back, gate, front):
                    st = Stage(s, par, base, phase % 2)
                    st.order = [k for n in range(N) for k in steps(n, back, front)]
                    st.is_prelude, st.is_first = front and not gate, gate and front and not back
                    return st

                PAIRS = (STAGES - 2) // 2
                BASE1 = 2 * N_FRONT

                def drive(eng, stage_fn, prelude, flush):
                    st = make(-1, 1, 0, 0, False, False, True)
                    stage_fn(eng, st, False, False, True, False, False, first=True)
                    prelude(eng)
                    st = make(0, 0, N_FRONT, N_FRONT, False, True, True)
                    stage_fn(eng, st, False, True, True, True, True, first=True)
                    with eng.Fori(0, PAIRS) as t:
                        for half in (0, 1):
                            st = make(t * 2 + (1 + half), (1 + half) % 2, t * (2 * N_ALL) + (BASE1 + half * N_ALL),
                                      BASE1 + half * N_ALL, True, True, True)
                            stage_fn(eng, st, True, True, True, True, True)
                    last = STAGES - 1
                    base = BASE1 + (STAGES - 2) * N_ALL
                    st = make(last, last % 2, base, base, True, True, False)
                    stage_fn(eng, st, True, True, False, True, False)
                    flush(eng)
                    base += N_BACK
                    st = make(STAGES, STAGES % 2, base, base, True, False, False)
                    stage_fn(eng, st, True, False, False, False, False)

                nothing = lambda eng: None

                with nc.Block() as block:
                    @block.scalar
                    def _(act):
                        act.wait_ge(pads, 2)

                        def prelude(act):
                            emit_act_decay(act, 0, 0, 0, False)
                            emit_act_b(act, 0, 0, False)
                            emit_act_b(act, 0, 1, False)
                        drive(act, act_stage, prelude, nothing)

                    @block.tensor
                    def _(pe):
                        def prelude(pe):
                            pe.wait_ge(front_free, N_FRONT)
                            emit_pe_b(pe, 0, 0, 0, False)
                            emit_pe_b(pe, 0, 0, 1, False)
                        drive(pe, pe_stage, prelude, nothing)

                    @block.gpsimd
                    def _(pool):
                        def prelude(pool):
                            emit_pool_dbx(pool, 0, 0, 0, False)
                        drive(pool, pool_stage, prelude, nothing)

                    @block.vector
                    def _(dve):
                        dve.memset(da[:], 0.0).then_inc(pads, 1)
                        dve.memset(xs[:], 0.0).then_inc(pads, 1)
                        drive(dve, dve_stage, nothing,
                              lambda dve: emit_dve_y(dve, STAGES - 1, (STAGES - 1) % 2, N - 1))

        with ExitStack() as s3:
            GK = 3 * DC
            lnw = sb(s3, "lnw", [P, D])
            lnb = sb(s3, "lnb", [P, D])
            onorm = sb(s3, "onorm", [P, D])
            igk = sb(s3, "igk", [P, GK, NH])
            fgk = sb(s3, "fgk", [P, GK, NH])
            gate_bias = sb(s3, "gate_bias", [NH, 3])
            ones = sb(s3, "ones", [NH, L])
            neg_sel = sb(s3, "neg_sel", [NH, NH])
            wg = sb(s3, "wg", [P, DC, HID])
            wu = sb(s3, "wu", [P, DC, HID])
            wd = sb(s3, "wd", [P, HC, D])
            w_int = sb(s3, "w_int", [P, HC * D], I32)
            w_f = sb(s3, "w_f", [P, HC * D])
            xin = sb(s3, "xin", [P, LC, D])
            cx = sb(s3, "cx", [P, LC, D])
            xm = sb(s3, "xm", [P, DC, L])
            t_a = sb(s3, "t_a", [P, LC, D])
            x1 = sb(s3, "x1", [P, LC, D])
            x2 = sb(s3, "x2", [P, LC, D])
            nrm = sb(s3, "nrm", [P, LC, D])
            qt = sb(s3, "qt", [P, DC, L])
            ct = sb(s3, "ct", [P, DC, L])
            x2t = sb(s3, "x2t", [P, DC, L])
            v1 = sb(s3, "v1", [P, LC, NH, DH + 1])
            stats3 = sb(s3, "stats3", [P, 4 * LC, 6])
            mv3 = sb(s3, "mv3", [P, 4 * LC, 2])
            lnv3 = sb(s3, "lnv3", [P, 4 * LC])
            carrier = sb(s3, "carrier", [P, 1])
            carrier_p = sb(s3, "carrier_p", [P, 1])
            fa = sb(s3, "fa", [NH, L])
            fr_ = sb(s3, "fr_", [NH, L])
            ncs = sb(s3, "ncs", [NH, L])
            ga = sb(s3, "ga", [NH, L])
            gm = sb(s3, "gm", [NH, L])
            ge = sb(s3, "ge", [NH, L])
            ae = sb(s3, "ae", [P, LC, 2 * NH])
            dm = sb(s3, "dm", [P, 2, LC, L])
            osb = sb(s3, "osb", [P, LC, NH, DH + 1])
            den = sb(s3, "den", [P, LC, NH])
            kk = sb(s3, "kk", [P, LC, NH])
            gl = sb(s3, "gl", [P, 2, L])
            gs = sb(s3, "gs", [P, 2, L])
            hid = sb(s3, "hid", [P, HC, L])
            o_sb = sb(s3, "o_sb", [P, LC, D])
            ps_a = pb(s3, "ps_a", [P, 2, L])
            ps_b = pb(s3, "ps_b", [P, 2, L])
            ps_s = pb(s3, "ps_s", [P, 4, L])

            S = {k: sem("e_" + k) for k in (
                "consts", "w_in", "w_scaled", "w_tr", "w_evac", "x_in", "c_in", "out_free", "out_ready", "set", "act_set",
                "xm_ready", "x_tok", "stats", "mv", "log", "rstd", "normed", "lnm_w", "lnm_b", "x1_ready",
                "c_tr", "c_t_ready", "v_ready", "q_tr", "q_t_ready", "gates", "f_abs", "f_relu", "f_exp", "f_log",
                "i_ready", "f_sum", "cs_ready", "ga_ready", "gm_ready", "ge_diff", "ge_ready", "ae_tr", "ae_ready",
                "m_bc", "d_arg", "qk", "d_exp", "d_masked", "c_ready", "av", "h_stats", "h_mv", "h_neg", "h_den", "h_rec", "o_evac",
                "h_t1", "h_t2", "h_log", "h_rs", "h_k", "h_sub", "h_mul", "h_scaled", "x2_ready", "x2_tr",
                "x2t_ready", "ffn_g", "ffn_u", "gl_ready", "g_cl", "g_exp", "g_log", "g_sig", "g_silu", "hid_ready",
                "down")}

            def three(ap, k):
                return ap.rearrange("p (k f) -> p k f", k=k)

            oh = [ps_a[:, 0], ps_a[:, 1], ps_b[:, 0], ps_b[:, 1]]

            def oh_heads(j):
                return oh[j][:, 0:NH * (DH + 1)].rearrange("p (h d) -> p h d", h=NH)

            N_CONST = 7
            GATE_BANK, UP_BANK = 2, 3

            def down_half(j):
                return ps_s[:, GATE_BANK + j // 2, (j % 2) * D:(j % 2 + 1) * D]

            def pipelined(eng, entry):
                entry(0, None)
                with eng.Fori(1, NB) as b:
                    entry(b, b - 1)
                entry(None, NB - 1)

            with nc.Block() as block:
                @block.sync
                def _(sp):
                    for dst, src in ((lnw, ln_w), (lnb, ln_b), (onorm, outnorm_scale)):
                        sp.dma_start(dst[:], src.partition_broadcast(P)).then_inc(S["consts"], 16)
                    sp.dma_start(igk[:], igate_kernel.rearrange("(k p) h -> p k h", p=P)).then_inc(S["consts"], 16)
                    sp.dma_start(fgk[:], fgate_kernel.rearrange("(k p) h -> p k h", p=P)).then_inc(S["consts"], 16)
                    sp.dma_start(gate_bias[:, 0:1], igate_bias.rearrange("(h a) -> h a", a=1),
                                 allow_slow_non_contiguous=True).then_inc(S["consts"], 16)
                    sp.dma_start(gate_bias[:, 1:2], fgate_bias.rearrange("(h a) -> h a", a=1),
                                 allow_slow_non_contiguous=True).then_inc(S["consts"], 16)
                    sp.sem_inc(S["out_free"], 16)
                    for m, w in enumerate((w_gate, w_up)):
                        if m:
                            sp.wait_ge(S["w_scaled"], m)
                        sp.dma_start(three(w_int[:], HC), w.rearrange("(c p) d -> p c d", p=P)).then_inc(S["w_in"], 16)
                    sp.wait_ge(S["w_scaled"], 2)
                    sp.dma_start(three(w_int[:], DC), w_down.rearrange("(k p) h -> p k h", p=P)).then_inc(S["w_in"], 16)

                    def load(b):
                        sp.dma_start(xin[:], x[ds(b, 1)].rearrange("b (j p) d -> p (b j) d", p=P)).then_inc(S["x_in"], 16)
                        sp.dma_start(cx[:], ctx_1024[ds(b, 1)].rearrange("b (j p) d -> p (b j) d", p=P)).then_inc(S["c_in"], 16)

                    def store(b):
                        sp.wait_ge(S["out_ready"], (b + 1) * LC)
                        sp.dma_start(out[ds(b, 1)].rearrange("b (j p) d -> p (b j) d", p=P), o_sb[:]).then_inc(S["out_free"], 16)

                    load(0)
                    with sp.Fori(0, NB - 1) as b:
                        sp.wait_ge(S["x1_ready"], b + 1)
                        sp.wait_ge(S["c_t_ready"], b + 1)
                        sp.wait_ge(S["v_ready"], b + 1)
                        load(b + 1)
                        store(b)
                    store(NB - 1)
                    sp.wait_ge(S["out_free"], 16 * (NB + 1))

                @block.scalar
                def _(act):
                    def evac(out_, in_, full, count, done):
                        act.wait_ge(S[full], count)
                        act.activation(out_, in_, ACT.Copy).then_inc(S[done], 1)

                    def rsqrt(out_, in_, ready, count, log, done, e, lead=1.0):
                        act.wait_ge(S[ready], count)
                        act.activation(out_, in_, ACT.Ln, bias=e).then_inc(S[log], 1)
                        act.wait_ge(S[log], count)
                        act.activation(out_, out_, ACT.Exp, scale=-0.5).then_inc(S[done], 1)

                    act.wait_ge(S["consts"], 16 * N_CONST)
                    act.activation(gate_bias[:, 2:3], gate_bias[:, 1:2], ACT.Copy, scale=-1.0).then_inc(S["act_set"], 1)
                    act.activation(neg_sel[:], ident[0:NH, 0:NH], ACT.Copy, scale=-1.0).then_inc(S["act_set"], 1)
                    act.wait_ge(S["act_set"], 2)
                    for m, w in enumerate((wg, wu)):
                        for k in range(DC):
                            act.wait_ge(S["w_tr"], m * DC + k + 1)
                            act.activation(w[:, k, 0:L], ps_s[:, 2 * k, :], ACT.Copy)
                            act.activation(w[:, k, L:HID], ps_s[:, 2 * k + 1, 0:HID - L], ACT.Copy).then_inc(S["w_evac"], 1)
                    act.wait_ge(S["w_tr"], 2 * DC + 1)
                    act.activation(wd[:, 0:4, :], ps_s[:, 0:2, :].rearrange("p a l -> p (a l)").rearrange("p (c d) -> p c d", d=D), ACT.Copy)
                    act.activation(wd[:, 4:6, :], three(ps_s[:, 2, :], 2), ACT.Copy).then_inc(S["w_evac"], 1)
                    def ffn_chunk(f, c):
                        n_ = f * HC + c + 1
                        if c >= 2:
                            act.wait_ge(S["g_silu"], n_ - 2)
                        evac(gl[:, c % 2, :], ps_s[:, GATE_BANK, :], "ffn_g", n_, "gl_ready")
                        buf = gs[:, c % 2, :]
                        act.wait_ge(S["g_cl"], n_)
                        act.activation(buf, buf, ACT.Exp, scale=-1.0).then_inc(S["g_exp"], 1)
                        act.wait_ge(S["g_exp"], n_)
                        act.activation(buf, buf, ACT.Ln, bias=1.0).then_inc(S["g_log"], 1)
                        act.wait_ge(S["g_log"], n_)
                        act.activation(buf, buf, ACT.Exp, scale=-1.0).then_inc(S["g_sig"], 1)

                    def entry(b, f):
                        def ffn(*chunks):
                            if f is not None:
                                for c in chunks:
                                    ffn_chunk(f, c)

                        if b is None:
                            ffn(*range(HC))
                            return
                        act.activation(xm[:], xT[:, ds(b, 1), :, :], ACT.Copy).then_inc(S["xm_ready"], 1)
                        act.wait_ge(S["set"], 2)
                        act.wait_ge(S["c_in"], 16 * (b + 1))
                        for i in range(LC):
                            last = act.activation(v1[:, i, :, 0:DH], cx[:, i, :].rearrange("p (h d) -> p h d", h=NH), ACT.Copy)
                        last.then_inc(S["v_ready"], 1)
                        ffn(0)
                        rsqrt(lnv3[:, 0:LC], mv3[:, 0:LC, 1], "mv", 3 * b + 1, "log", "rstd", eps[:, 0:1])
                        evac(ct[:], ps_b[:], "c_tr", b + 1, "c_t_ready")
                        ffn(1, 2)
                        rsqrt(lnv3[:, 0:LC], mv3[:, 0:LC, 1], "mv", 3 * b + 2, "log", "rstd", eps[:, 0:1])
                        evac(qt[:], ps_a[:], "q_tr", b + 1, "q_t_ready")
                        ffn(3)
                        act.wait_ge(S["gates"], b + 1)
                        act.activation(ga[:], ps_s[0:NH, 0, :], ACT.Identity, bias=gate_bias[:, 0:1]).then_inc(S["i_ready"], 1)
                        act.activation(fa[:], ps_s[0:NH, 1, :], ACT.Abs, bias=gate_bias[:, 1:2]).then_inc(S["f_abs"], 1)
                        act.activation(fr_[:], ps_s[0:NH, 1, :], ACT.Relu, scale=-1.0, bias=gate_bias[:, 2:3]).then_inc(S["f_relu"], 1)
                        act.wait_ge(S["f_abs"], b + 1)
                        act.activation(fa[:], fa[:], ACT.Exp, scale=-1.0).then_inc(S["f_exp"], 1)
                        act.wait_ge(S["f_exp"], b + 1)
                        act.activation(fa[:], fa[:], ACT.Ln, bias=1.0).then_inc(S["f_log"], 1)
                        ffn(4, 5)
                        act.wait_ge(S["ge_diff"], b + 1)
                        act.activation(ge[:], ge[:], ACT.Exp).then_inc(S["ge_ready"], 1)
                        evac(ae[:], ps_s[:, 0, 0:LC * 2 * NH].rearrange("p (j g) -> p j g", j=LC), "ae_tr", b + 1, "ae_ready")
                        for h in range(NH):
                            for i in range(LC):
                                dlog = dm[:, h % 2, i, i * P:L]
                                act.wait_ge(S["d_arg"], (b * NH + h) * LC + i + 1)
                                act.activation(dlog, dlog, ACT.Exp).then_inc(S["d_exp"], 1)
                        act.wait_ge(S["av"], (b + 1) * NH)
                        for j in range(LC):
                            act.activation(osb[:, j], oh_heads(j), ACT.Copy).then_inc(S["o_evac"], 1)
                        rsqrt(kk[:], kk[:], "h_t2", b + 1, "h_log", "h_rs", eps[:, 1:2])
                        rsqrt(lnv3[:, 0:LC], mv3[:, 0:LC, 1], "mv", 3 * b + 3, "log", "rstd", eps[:, 0:1])
                        evac(x2t[:], ps_a[:], "x2_tr", b + 1, "x2t_ready")

                    act.wait_ge(S["w_evac"], 2 * DC + 1)
                    pipelined(act, entry)

                @block.tensor
                def _(pe):
                    for m, w in enumerate((wg, wu)):
                        pe.wait_ge(S["w_scaled"], m + 1)
                        if m:
                            pe.wait_ge(S["w_evac"], m * DC)
                        wf = three(w_f[:], HC)
                        for k in range(DC):
                            for c in range(HC):
                                dst = ps_s[:, 2 * k + c // 4, (c % 4) * P:(c % 4 + 1) * P]
                                last = pe.transpose(dst, wf[:, c, k * P:(k + 1) * P], ident[:])
                            last.then_inc(S["w_tr"], 1)
                    pe.wait_ge(S["w_scaled"], 3)
                    pe.wait_ge(S["w_evac"], 2 * DC)
                    wf = three(w_f[:], DC)
                    for c in range(HC):
                        for k in range(DC):
                            at = c * D + k * P
                            last = pe.transpose(ps_s[:, at // L, at % L:at % L + P], wf[:, k, c * P:(c + 1) * P], ident[:])
                    last.then_inc(S["w_tr"], 1)

                    def to_channels(dst, src, done):
                        for k in range(DC):
                            for j in range(LC):
                                last = pe.transpose(dst[:, k, j * P:(j + 1) * P], src[:, j, k * P:(k + 1) * P], ident[:])
                        last.then_inc(S[done], 1)

                    def ffn_chunk(f, c):
                        if c >= 1:
                            pe.wait_ge(S["gl_ready"], f * HC + c)
                        for w, bank, done in ((wg, GATE_BANK, "ffn_g"), (wu, UP_BANK, "ffn_u")):
                            if w is wu and c >= 1:
                                pe.wait_ge(S["hid_ready"], f * HC + c)
                            for k in range(DC):
                                last = pe.matmul(ps_s[:, bank, :], w[:, k, c * P:(c + 1) * P], x2t[:, k, :],
                                                 start=k == 0, stop=k == DC - 1)
                            last.then_inc(S[done], 1)

                    def ffn_down(f):
                        pe.wait_ge(S["hid_ready"], (f + 1) * HC)
                        for j in range(LC):
                            for c in range(HC):
                                last = pe.matmul(down_half(j), hid[:, c, j * P:(j + 1) * P], wd[:, c, :],
                                                 start=c == 0, stop=c == HC - 1)
                            last.then_inc(S["down"], 1)

                    def entry(b, f):
                        def ffn(*chunks):
                            if f is not None:
                                for c in chunks:
                                    ffn_chunk(f, c)

                        if b is None:
                            pe.wait_ge(S["x2t_ready"], f + 1)
                            ffn(*range(HC))
                            ffn_down(f)
                            return
                        pe.wait_ge(S["xm_ready"], b + 1)
                        for j in range(LC):
                            for k in range(DC):
                                last = pe.transpose(ps_a[:, j // 2, (j % 2) * D + k * P:(j % 2) * D + (k + 1) * P],
                                                    xm[:, k, j * P:(j + 1) * P], ident[:])
                        last.then_inc(S["x_tok"], 1)
                        ffn(0)
                        pe.wait_ge(S["c_in"], 16 * (b + 1))
                        pe.wait_ge(S["normed"], 3 * b + 1)
                        to_channels(ps_b, cx, "c_tr")
                        ffn(1, 2)
                        pe.wait_ge(S["normed"], 3 * b + 2)
                        to_channels(ps_a, nrm, "q_tr")
                        ffn(3)
                        pe.wait_ge(S["q_t_ready"], b + 1)
                        pe.wait_ge(S["c_t_ready"], b + 1)
                        for m, w in enumerate((igk, fgk)):
                            for k in range(GK):
                                src = qt[:, k, :] if k < DC else ct[:, k % DC, :]
                                last = pe.matmul(ps_s[0:NH, m, :], w[:, k, :], src, start=k == 0, stop=k == GK - 1)
                        last.then_inc(S["gates"], 1)
                        ffn(4, 5)
                        if f is not None:
                            ffn_down(f)
                        pe.wait_ge(S["ga_ready"], b + 1)
                        pe.wait_ge(S["ge_ready"], b + 1)
                        for j in range(LC):
                            for m, src in enumerate((ga, ge)):
                                last = pe.matmul(ps_s[:, 0, (2 * j + m) * NH:(2 * j + m + 1) * NH],
                                                 src[:, j * P:(j + 1) * P], ident[0:NH, 0:NH], start=True, stop=True)
                        last.then_inc(S["ae_tr"], 1)
                        pe.wait_ge(S["v_ready"], b + 1)
                        pe.wait_ge(S["ae_ready"], b + 1)
                        if f is not None:
                            pe.wait_ge(S["out_ready"], (f + 1) * LC)

                        def attend(h):
                            pe.wait_ge(S["c_ready"], (b * NH + h + 1) * LC)
                            for j in range(LC):
                                for i in range(j + 1):
                                    last = pe.matmul(oh[j][:, h * (DH + 1):(h + 1) * (DH + 1)],
                                                     dm[:, h % 2, i, j * P:(j + 1) * P], v1[:, i, h, :],
                                                     start=i == 0, stop=i == j)
                            last.then_inc(S["av"], 1)

                        for h in range(NH):
                            at = (h % 2) * DH
                            if h:
                                pe.wait_ge(S["d_arg"], (b * NH + h) * LC)
                            pe.matmul(ps_s[:, 0, :], neg_sel[:, h:h + 1].broadcast_to([NH, P]), gm[:],
                                      start=True, stop=True).then_inc(S["m_bc"], 1)
                            for i in range(LC):
                                if i == 0 and h:
                                    pe.wait_ge(S["c_ready"], (b * NH + h) * LC)
                                if i == 3:
                                    pe.wait_ge(S["c_ready"], (b * NH + h) * LC + 1)
                                pe.matmul(ps_s[:, 1 + i % 3, i * P:L], ct[at:at + DH, h // 2, i * P:(i + 1) * P],
                                          qt[at:at + DH, h // 2, i * P:L], start=True, stop=True).then_inc(S["qk"], 1)
                            if h:
                                attend(h - 1)
                        attend(NH - 1)
                        pe.wait_ge(S["normed"], 3 * b + 3)
                        to_channels(ps_a, nrm, "x2_tr")

                    pe.wait_ge(S["w_evac"], 2 * DC + 1)
                    pipelined(pe, entry)

                @block.gpsimd
                def _(pool):
                    pool.memset(ones[:], 1.0).then_inc(S["set"], 1)
                    pool.memset(v1[:], 1.0).then_inc(S["set"], 1)
                    pool.wait_ge(S["set"], 2)
                    def bc(w, reps):
                        return w[:].unsqueeze(1).broadcast_to([P, reps, D])

                    def entry(b, f):
                        def ffn(*chunks):
                            if f is not None:
                                for c in chunks:
                                    pool.wait_ge(S["g_sig"], f * HC + c + 1)
                                    pool.tensor_tensor(gs[:, c % 2, :], gs[:, c % 2, :], gl[:, c % 2, :],
                                                       ALU.mult).then_inc(S["g_silu"], 1)

                        if b is None:
                            ffn(*range(HC))
                            return
                        ffn(0)
                        pool.wait_ge(S["normed"], 3 * b + 1)
                        pool.tensor_tensor(t_a[:], nrm[:], bc(lnw, LC), ALU.mult).then_inc(S["lnm_w"], 1)
                        pool.wait_ge(S["lnm_w"], b + 1)
                        pool.tensor_tensor(t_a[:], t_a[:], bc(lnb, LC), ALU.add).then_inc(S["lnm_b"], 1)
                        pool.wait_ge(S["lnm_b"], b + 1)
                        pool.wait_ge(S["x_in"], 16 * (b + 1))
                        pool.tensor_tensor(x1[:], t_a[:], xin[:], ALU.add).then_inc(S["x1_ready"], 1)
                        ffn(*range(1, HC))
                        for h in range(NH):
                            pool.wait_ge(S["d_exp"], (b * NH + h + 1) * LC)
                            pool.tensor_tensor(carrier_p[:], eps[:, 0:1], eps[:, 0:1], ALU.add)
                            for i in range(LC):
                                diag = dm[:, h % 2, i, i * P:(i + 1) * P]
                                pool.affine_select(out=diag, in_=diag, compare_op=ALU.is_ge, fill=0.0, base=0,
                                                   pattern=[[1, P]], channel_multiplier=-1).then_inc(S["d_masked"], 1)
                        flat = osb[:].rearrange("p j h d -> p (j h) d")[:, :, 0:DH]
                        pool.wait_ge(S["o_evac"], (b + 1) * LC)
                        pool.wait_ge(S["h_mv"], b + 1)
                        pool.tensor_tensor(flat, flat, mv3[:, :, 0:1].broadcast_to([P, LC * NH, DH]),
                                           ALU.subtract).then_inc(S["h_sub"], 1)
                        pool.wait_ge(S["h_sub"], b + 1)
                        pool.wait_ge(S["h_k"], b + 1)
                        pool.tensor_tensor(flat, flat, kk[:].rearrange("p j h -> p (j h)").unsqueeze(2)
                                           .broadcast_to([P, LC * NH, DH]), ALU.mult).then_inc(S["h_mul"], 1)
                        pool.wait_ge(S["h_mul"], b + 1)
                        pool.tensor_tensor(t_a[:].rearrange("p j (h d) -> p j h d", h=NH), osb[:, :, :, 0:DH],
                                           onorm[:].rearrange("p (h d) -> p h d", h=NH).unsqueeze(1)
                                           .broadcast_to([P, LC, NH, DH]), ALU.mult).then_inc(S["h_scaled"], 1)

                    pipelined(pool, entry)

                @block.vector
                def _(dve):
                    for m in range(3):
                        dve.wait_ge(S["w_in"], 16 * (m + 1))
                        if m:
                            dve.wait_ge(S["w_tr"], m * DC)
                        dve.tensor_scalar(w_f[:], w_int[:], FFN_SCALE, None, ALU.mult).then_inc(S["w_scaled"], 1)

                    def stats_of(parts, wait, count, stat, done, times):
                        dve.wait_ge(S[wait], count)
                        for m, part in enumerate(parts):
                            dve.bn_stats(stats3[:, m, :], part).then_inc(S[stat], 1)
                        dve.wait_ge(S[stat], times * len(parts))
                        dve.memset(carrier[:], 0.0)
                        for m in range(len(parts)):
                            last = dve.bn_aggr(mv3[:, m, :], stats3[:, m, :])
                        last.then_inc(S[done], 1)

                    def normalise(src, k):
                        dve.wait_ge(S["rstd"], k)
                        for j in range(LC):
                            last = dve.tensor_scalar(nrm[:, j, :], src(j), mv3[:, j, 0:1], lnv3[:, j:j + 1],
                                                     ALU.subtract, ALU.mult)
                        last.then_inc(S["normed"], 1)

                    def clamp(f, c):
                        n_ = f * HC + c + 1
                        dve.wait_ge(S["gl_ready"], n_)
                        dve.tensor_scalar(gs[:, c % 2, :], gl[:, c % 2, :], SIG_MIN, None, ALU.max).then_inc(S["g_cl"], 1)

                    def hidden(f, c):
                        n_ = f * HC + c + 1
                        dve.wait_ge(S["g_silu"], n_)
                        dve.wait_ge(S["ffn_u"], n_)
                        dve.tensor_tensor(hid[:, c, :], gs[:, c % 2, :], ps_s[:, UP_BANK, :], ALU.mult).then_inc(S["hid_ready"], 1)

                    def output(f):
                        dve.wait_ge(S["out_free"], 16 * (f + 1))
                        for j in range(LC):
                            dve.wait_ge(S["down"], f * LC + 2 * (j // 2) + 2)
                            dve.tensor_tensor(o_sb[:, j, :], x2[:, j, :], down_half(j), ALU.add).then_inc(S["out_ready"], 1)

                    def tok(j):
                        return ps_a[:, j // 2, (j % 2) * D:(j % 2 + 1) * D]

                    def entry(b, f):
                        def ffn(step, c):
                            if f is not None:
                                step(f, c)

                        if b is None:
                            for c in range(HC):
                                clamp(f, c)
                                hidden(f, c)
                            output(f)
                            return
                        stats_of([tok(j) for j in range(LC)], "x_tok", b + 1, "stats", "mv", 3 * b + 1)
                        ffn(clamp, 0)
                        normalise(tok, 3 * b + 1)
                        ffn(hidden, 0)
                        ffn(clamp, 1)
                        stats_of([x1[:, j, :] for j in range(LC)], "x1_ready", b + 1, "stats", "mv", 3 * b + 2)
                        ffn(hidden, 1)
                        ffn(clamp, 2)
                        normalise(lambda j: x1[:, j, :], 3 * b + 2)
                        ffn(hidden, 2)
                        ffn(clamp, 3)
                        ffn(hidden, 3)
                        dve.wait_ge(S["f_log"], b + 1)
                        dve.wait_ge(S["f_relu"], b + 1)
                        dve.tensor_tensor(fa[:], fa[:], fr_[:], ALU.add).then_inc(S["f_sum"], 1)
                        dve.wait_ge(S["f_sum"], b + 1)
                        dve.tensor_tensor_scan(ncs[:], ones[:], fa[:], 0.0, ALU.mult, ALU.add).then_inc(S["cs_ready"], 1)
                        dve.wait_ge(S["cs_ready"], b + 1)
                        dve.tensor_tensor(ga[:], ga[:], ncs[:], ALU.add).then_inc(S["ga_ready"], 1)
                        ffn(clamp, 4)
                        dve.wait_ge(S["ga_ready"], b + 1)
                        dve.tensor_tensor_scan(gm[:], ga[:], ga[:], -3.0e38, ALU.max, ALU.max).then_inc(S["gm_ready"], 1)
                        dve.wait_ge(S["gm_ready"], b + 1)
                        dve.tensor_tensor(ge[:], ncs[:], gm[:], ALU.subtract).then_inc(S["ge_diff"], 1)
                        ffn(hidden, 4)
                        ffn(clamp, 5)
                        ffn(hidden, 5)
                        if f is not None:
                            output(f)
                        dve.wait_ge(S["ae_ready"], b + 1)
                        for h in range(NH):
                            dve.wait_ge(S["m_bc"], b * NH + h + 1)
                            if h >= 2:
                                dve.wait_ge(S["av"], b * NH + h - 1)
                            for i in range(LC):
                                dve.tensor_scalar(dm[:, h % 2, i, i * P:L], ps_s[:, 0, i * P:L], ae[:, i, h:h + 1],
                                                  0.0, ALU.add, ALU.min).then_inc(S["d_arg"], 1)
                            for i in range(LC):
                                n_ = (b * NH + h) * LC + i + 1
                                dve.wait_ge(S["qk"], n_)
                                dve.wait_ge(S["d_masked"], n_)
                                c_blk = dm[:, h % 2, i, i * P:L]
                                dve.scalar_tensor_tensor(c_blk, ps_s[:, 1 + i % 3, i * P:L], DH ** -0.5, c_blk,
                                                         ALU.mult, ALU.mult).then_inc(S["c_ready"], 1)
                        row_sum = osb[:, :, :, DH]
                        dve.wait_ge(S["o_evac"], (b + 1) * LC)
                        dve.scalar_tensor_tensor(den[:], row_sum, -1.0, ae[:, :, NH:2 * NH], ALU.mult,
                                                 ALU.max).then_inc(S["h_neg"], 1)
                        dve.wait_ge(S["h_neg"], b + 1)
                        dve.tensor_tensor(den[:], row_sum, den[:], ALU.max).then_inc(S["h_den"], 1)
                        stats_of([osb[:, j, h, 0:DH] for j in range(LC) for h in range(NH)], "o_evac", (b + 1) * LC,
                                 "h_stats", "h_mv", b + 1)
                        dve.wait_ge(S["h_den"], b + 1)
                        dve.tensor_scalar(den[:], den[:], EPS_MLSTM, None, ALU.add).then_inc(S["h_rec"], 1)
                        dve.wait_ge(S["h_rec"], 3 * b + 1)
                        dve.reciprocal(den[:], den[:]).then_inc(S["h_rec"], 1)
                        dve.wait_ge(S["h_rec"], 3 * b + 2)
                        dve.tensor_tensor(kk[:], den[:], den[:], ALU.mult).then_inc(S["h_rec"], 1)
                        dve.wait_ge(S["h_rec"], 3 * b + 3)
                        dve.wait_ge(S["h_mv"], b + 1)
                        dve.tensor_tensor(kk[:], kk[:], mv3[:, :, 1].rearrange("p (j h) -> p j h", h=NH),
                                          ALU.mult).then_inc(S["h_t2"], 1)
                        dve.wait_ge(S["h_rs"], b + 1)
                        dve.tensor_tensor(kk[:], kk[:], den[:], ALU.mult).then_inc(S["h_k"], 1)
                        dve.wait_ge(S["h_scaled"], b + 1)
                        dve.tensor_tensor(x2[:], t_a[:], x1[:], ALU.add).then_inc(S["x2_ready"], 1)
                        stats_of([x2[:, j, :] for j in range(LC)], "x2_ready", b + 1, "stats", "mv", 3 * b + 3)
                        normalise(lambda j: x2[:, j, :], 3 * b + 3)

                    pipelined(dve, entry)


_INS = ['x', 'ctx_1024', 'L0_attn_rms_w', 'L0_attn_W_in', 'L0_attn_conv_w', 'L0_attn_conv_b', 'L0_attn_W_x',
        'L0_attn_W_dt', 'L0_attn_b_dt', 'L0_attn_A_log', 'L0_attn_Dp', 'L0_attn_W_out', 'L0_attn_ln_w',
        'L0_attn_ln_b', 'L0_xattn_igate_kernel', 'L0_xattn_igate_bias', 'L0_xattn_fgate_kernel',
        'L0_xattn_fgate_bias', 'L0_xattn_outnorm_scale', 'L0_ffn_w_gate', 'L0_ffn_w_up', 'L0_ffn_w_down']


def kernel(**inputs):
    import numpy as _np
    import concourse.bacc as _bacc
    from concourse import mybir as _mybir
    from concourse.bass_utils import run_bass_kernel_spmd as _run

    nc = _bacc.Bacc("TRN2", target_bir_lowering=False, num_devices=1)
    arrays, args = {}, []
    for name in _INS:
        a = _np.ascontiguousarray(inputs[name])
        arrays[f"in_{name}_dram"] = a
        args.append(nc.dram_tensor(f"in_{name}_dram", a.shape, _mybir.dt.from_np(a.dtype), kind="ExternalInput").ap())
    shape = inputs['x'].shape
    args.append(nc.dram_tensor("out_0_dram", shape, _mybir.dt.float32, kind="ExternalOutput").ap())
    build(nc, *args)
    r = _run(nc, [arrays], core_ids=[0])
    return r.results[0]["out_0_dram"]
```

```python
def build(nc, x, ctx_1024, rms_w, W_in, conv_w, conv_b, W_x, W_dt, b_dt, A_log, Dp, W_out, ln_w, ln_b,
          igate_kernel, igate_bias, fgate_kernel, fgate_bias, outnorm_scale, w_gate, w_up, w_down, out):
    import concourse.bass as bass
    from concourse import mybir
    from contextlib import ExitStack

    F32 = mybir.dt.float32
    I32 = mybir.dt.int32
    BF16 = mybir.dt.bfloat16
    ACT = mybir.ActivationFunctionType
    ALU = mybir.AluOpType
    ds = bass.ds

    P = 128
    NB, L, D = x.shape
    ED, KC = conv_w.shape
    R = W_dt.shape[0]
    N = A_log.shape[1]
    NH = igate_bias.shape[0]
    DH = D // NH
    HID = w_gate.shape[0]
    DC, EC, LC, HC = D // P, ED // P, L // P, HID // P
    DEPTH = 6
    STAGES = DEPTH * NB
    EPS, EPS_MLSTM, FFN_SCALE = 1e-5, 1e-6, 1.0 / 127.0
    SIG_MIN = -40.0
    DBC = R + 2 * N

    STEP_AT = {
        ("xs", 0): 3, ("xs", 1): 4, ("cv", 0): 6, ("xs", 2): 10, ("y", 0): 10, ("y", 1): 13, ("cv", 1): 15,
        ("xs", 3): 15, ("y", 2): 16, ("y", 3): 19, ("cv", 2): 21, ("cv", 3): 25, ("o", 0): 29,
        ("bc", 0): 33, ("o", 1): 37, ("dl", 0): 41, ("z", 0): 43, ("dl", 1): 44, ("cl", 0): 46,
        ("dl", 2): 47, ("z", 1): 48, ("dl", 3): 51, ("ms", 0): 52, ("dx", 0): 54, ("z", 2): 56,
        ("dx", 1): 57, ("dx", 2): 59, ("dx", 3): 60, ("z", 3): 61}
    V_CLAMP_AT = (11, 19, 25, 31)
    V_SIG_AT = (12, 20, 28, 32)
    XC_AT = (18, 22, 28, 32)
    Z_CLAMP_AT = (15, 19, 31, 33)
    Z_SIG_AT = (16, 24, 35, 38)
    GATE_AT = (20, 25, 40, 44)
    YG_AT = (4, 4, 5, 8)
    DELTA_AT = (47, 48, 55, 59)
    U_AT = 56
    RESIDUAL_AT = 44
    SPLIT_AT = (38, 46)
    MID_AT = 41
    B_BEHIND = 3
    SQUARES_AT = 49
    B_HI, B_MID, B_LO = R, 32, 0
    BACK = ("y", "o")
    AHEAD = 3

    PIECES = {"xs": DC, "cv": KC, "bc": EC, "o": EC, "z": DC, "ms": DC}

    def schedule(back, front, scan, next_scan):
        done, order = 0, []
        due = [(LC * n + B_BEHIND, ("b", n + AHEAD)) for n in range(N) if (scan if n + AHEAD < N else next_scan)]
        for step, start in list(STEP_AT.items()) + [(None, LC * N - 1)]:
            while due and due[0][0] <= max(start, done):
                done = max(done, due[0][0])
                order.append((done, due.pop(0)[1], 0))
            if step and (back if step[0] in BACK else front):
                for piece in range(PIECES.get(step[0], 1)):
                    done = max(done, start + piece)
                    order.append((done, step, piece))
        assert done < LC * N
        return order

    def is_last(step, piece):
        return piece == PIECES.get(step[0], 1) - 1

    N_BACK = sum(k[0] in BACK for k in STEP_AT)
    N_FRONT = len(STEP_AT) - N_BACK
    N_ALL = N_BACK + N_FRONT + N

    DBX_ON_DVE = (13,)
    DBX_BEFORE = 2
    NBB = 4
    NHB = 4
    TR_LAG, Y_LAG = LC, LC + 1

    top = ExitStack()
    with top:
        def sem(name):
            return top.enter_context(nc.semaphore(name))

        def sb(stack, name, shape, dt=F32):
            return stack.enter_context(nc.sbuf_tensor(name, shape, dt))

        def pb(stack, name, shape):
            return stack.enter_context(nc.psum_tensor(name, shape, F32))

        xT = sb(top, "xT", [P, NB, DC, L])
        ident = sb(top, "ident", [P, P])
        eps = sb(top, "eps", [P, 2])

        mamba = ExitStack()
        with mamba:
            w_in = sb(mamba, "w_in", [P, DC, 2 * ED])
            w_x = sb(mamba, "w_x", [P, EC, DBC])
            w_dt = sb(mamba, "w_dt", [R, ED])
            w_out = sb(mamba, "w_out", [P, EC, D])
            conv_diag = sb(mamba, "conv_diag", [P, EC, KC, P])
            d_diag = sb(mamba, "d_diag", [P, EC, P])
            mean_mat = sb(mamba, "mean_mat", [P, P])
            neg_a = sb(mamba, "neg_a", [P, EC, N])
            cb = sb(mamba, "cb", [P, EC])
            bdt = sb(mamba, "bdt", [P, EC])

            w_loaded = sem("w_loaded")
            x_loaded = [sem(f"x_loaded_{b}") for b in range(NB)]
            const_set, weights_set, a_exp = sem("const_set"), sem("weights_set"), sem("a_exp")
            ln_stats, ln_mv, ln_log, ln_rstd, ln_out = (sem("ln_stats"), sem("ln_mv"), sem("ln_log"),
                                                        sem("ln_rstd"), sem("ln_out"))
            ln_tr = sem("ln_tr")
            x_ready = sem("x_ready")

            with ExitStack() as s1:
                x_nat = sb(s1, "x_nat", [P, NB, LC, D])
                rmsw = sb(s1, "rmsw", [P, DC])
                cw = sb(s1, "cw", [P, EC, KC])
                dcol = sb(s1, "dcol", [P, EC])
                stats = sb(s1, "stats", [P, NB, LC, 6])
                mv = sb(s1, "mv", [P, NB, LC, 2])
                lnv = sb(s1, "lnv", [P, NB, LC])
                xn = sb(s1, "xn", [P, 2, LC, D])
                pt = pb(s1, "pt", [P, 2, DC, L])
                N_LOADS = 10
                with nc.Block() as block:
                    @block.sync
                    def _(sp):
                        sp.dma_start(w_in[:], W_in.rearrange("(k p) e -> p k e", p=P)).then_inc(w_loaded, 16)
                        sp.dma_start(w_x[:], W_x.rearrange("(c p) m -> p c m", p=P)).then_inc(w_loaded, 16)
                        sp.dma_start(w_dt[:], W_dt).then_inc(w_loaded, 16)
                        sp.dma_start(w_out[:], W_out.rearrange("(c p) d -> p c d", p=P)).then_inc(w_loaded, 16)
                        for b in range(NB):
                            sp.dma_start(x_nat[:, b], x[b].rearrange("(j p) d -> p j d", p=P)).then_inc(x_loaded[b], 16)

                    @block.gpsimd
                    def _(pool):
                        pool.memset(ident[:], 0.0).then_inc(const_set, 1)
                        pool.wait_ge(const_set, 1)
                        pool.affine_select(out=ident[:], in_=ident[:], compare_op=ALU.not_equal, fill=1.0,
                                           base=0, pattern=[[-1, P]], channel_multiplier=1).then_inc(const_set, 1)
                        pool.memset(mean_mat[:], 1.0 / D).then_inc(weights_set, 1)
                        pool.memset(eps[:, 0:1], EPS).then_inc(const_set, 1)
                        pool.memset(eps[:, 1:2], EPS_MLSTM).then_inc(const_set, 1)
                        pool.wait_ge(const_set, 2)
                        pool.wait_ge(w_loaded, 16 * N_LOADS)
                        for c in range(EC):
                            for k in range(KC):
                                pool.tensor_scalar(conv_diag[:, c, k, :], ident[:], cw[:, c, k:k + 1], None,
                                                   ALU.mult).then_inc(weights_set, 1)
                            pool.tensor_scalar(d_diag[:, c, :], ident[:], dcol[:, c:c + 1], None,
                                               ALU.mult).then_inc(weights_set, 1)
                        for k in range(DC):
                            pool.tensor_scalar(w_in[:, k, :], w_in[:, k, :], rmsw[:, k:k + 1], None,
                                               ALU.mult).then_inc(weights_set, 1)
                        pool.wait_ge(a_exp, 1)
                        pool.tensor_scalar(neg_a[:], neg_a[:], -1.0, None, ALU.mult).then_inc(weights_set, 1)

                    @block.scalar
                    def _(act):
                        act.dma_start(cw[:], conv_w.rearrange("(c p) k -> p c k", p=P)).then_inc(w_loaded, 16)
                        act.dma_start(neg_a[:], A_log.rearrange("(c p) n -> p c n", p=P)).then_inc(w_loaded, 16)
                        for dst, src in ((rmsw, rms_w), (cb, conv_b), (bdt, b_dt), (dcol, Dp)):
                            act.dma_start(dst[:], src.rearrange("(c p) -> p c", p=P),
                                          allow_slow_non_contiguous=True).then_inc(w_loaded, 16)
                        act.preload_act_table_set("natural_log_exp_and_others")
                        act.wait_ge(w_loaded, 16 * N_LOADS)
                        act.activation(neg_a[:], neg_a[:], ACT.Exp).then_inc(a_exp, 1)
                        act.wait_ge(const_set, 4)
                        act.wait_ge(ln_mv, 1)
                        act.activation(lnv[:], mv[:, :, :, 1], ACT.Ln, bias=eps[:, 0:1]).then_inc(ln_log, 1)
                        act.wait_ge(ln_log, 1)
                        act.activation(lnv[:], lnv[:], ACT.Exp, scale=-0.5).then_inc(ln_rstd, 1)
                        with act.Fori(0, NB) as b:
                            act.wait_ge(ln_tr, b + 1)
                            act.activation(xT[:, ds(b, 1), :, :], pt[:, ds(b % 2, 1)], ACT.Copy).then_inc(x_ready, 1)

                    @block.vector
                    def _(dve):
                        for b in range(NB):
                            dve.wait_ge(x_loaded[b], 16)
                            for j in range(LC):
                                dve.bn_stats(stats[:, b, j, :], x_nat[:, b, j, :]).then_inc(ln_stats, 1)
                        dve.wait_ge(ln_stats, NB * LC)
                        for b in range(NB):
                            for j in range(LC):
                                last = dve.bn_aggr(mv[:, b, j, :], stats[:, b, j, :])
                        last.then_inc(ln_mv, 1)

                        def normalise(b, buffer, warm):
                            if warm:
                                dve.wait_ge(ln_tr, b - 1)
                            for j in range(LC):
                                last = dve.tensor_scalar(xn[:, buffer, j, :], x_nat[:, ds(b, 1), j, :], mv[:, ds(b, 1), j, 0:1],
                                                         lnv[:, ds(b, 1), j:j + 1], ALU.subtract, ALU.mult)
                            last.then_inc(ln_out, 1)

                        dve.wait_ge(ln_rstd, 1)
                        for b in (0, 1):
                            normalise(b, slice(b, b + 1), False)
                        with dve.Fori(2, NB) as b:
                            normalise(b, ds(b % 2, 1), True)

                    @block.tensor
                    def _(pe):
                        def transposes(b, buffer, warm):
                            pe.wait_ge(ln_out, b + 1)
                            if warm:
                                pe.wait_ge(x_ready, b - 1)
                            for k in range(DC):
                                for j in range(LC):
                                    last = pe.transpose(pt[:, buffer, k, j * P:(j + 1) * P],
                                                        xn[:, buffer, j, k * P:(k + 1) * P], ident[:])
                            last.then_inc(ln_tr, 1)

                        pe.wait_ge(const_set, 2)
                        for b in (0, 1):
                            transposes(b, b, False)
                        with pe.Fori(1, NB // 2) as pair:
                            for buffer in (0, 1):
                                transposes(pair * 2 + buffer, buffer, True)

            with ExitStack() as s2:
                sq = sb(s2, "sq", [P, DC, L])
                rstd = sb(s2, "rstd", [P, L])
                u = sb(s2, "u", [P, 2, DC, L])
                PAD = KC - 1
                xs = sb(s2, "xs", [P, 2, L + PAD])
                xc = sb(s2, "xc", [P, EC, L])
                sg = sb(s2, "sg", [P, 2, L])
                dbc = sb(s2, "dbc", [DBC, 2, L])
                c_tok = sb(s2, "c_tok", [P, 2, LC, N])
                delta = sb(s2, "delta", [P, 2, EC, L])
                dx = sb(s2, "dx", [P, 2, EC, L])
                pos = sb(s2, "pos", [P, 2, L])
                zl = sb(s2, "zl", [P, LC, ED])
                g = sb(s2, "g", [P, LC, ED])
                acc = sb(s2, "acc", [P, 2, LC, ED])
                hb = sb(s2, "hb", [P, NHB, EC, L])
                b_parts = sb(s2, "b_parts", [R + N, 2, L], BF16)
                b_rest = sb(s2, "b_rest", [R + N, L])
                b_pick = sb(s2, "b_pick", [R + N, N], BF16)
                b_all = sb(s2, "b_all", [P, NBB, L])
                da = pb(s2, "da", [P, EC, L])
                ht = pb(s2, "ht", [P, 2, ED])
                fr = pb(s2, "fr", [P, 2, L])

                pads = sem("pads")
                front_full, front_free = sem("front_full"), sem("front_free")
                sq_ready, rms_log, rstd_ready, u_ready = (sem("sq_ready"), sem("rms_log"), sem("rstd_ready"),
                                                          sem("u_ready"))
                v_ready, v_clamped, v_exp, v_log, v_sig, xc_ready = (
                    sem("v_ready"), sem("v_clamped"), sem("v_exp"), sem("v_log"), sem("v_sig"), sem("xc_ready"))
                z_ready, z_clamped, z_exp, z_log, z_sig, g_ready = (
                    sem("z_ready"), sem("z_clamped"), sem("z_exp"), sem("z_log"), sem("z_sig"), sem("g_ready"))
                p_abs, p_pos, p_exp, p_log, delta_ready, dx_ready = (
                    sem("p_abs"), sem("p_pos"), sem("p_exp"), sem("p_log"), sem("delta_ready"), sem("dx_ready"))
                xs_ready, dbc_ready, c_ready, acc_set = sem("xs_ready"), sem("dbc_ready"), sem("c_ready"), sem("acc_set")
                b_low, b_mid = sem("b_low"), sem("b_mid")
                yg_ready, yt_ready, o_ready = sem("yg_ready"), sem("yt_ready"), sem("o_ready")
                da_ready, scanned, h_tr, y_added = sem("da_ready"), sem("scanned"), sem("h_tr"), sem("y_added")
                dbx_by_pool, dbx_by_dve = sem("dbx_by_pool"), sem("dbx_by_dve")

                def dbx_done(s, n):
                    s, n = (s, n) if n >= 0 else (s - 1, n + N)
                    by_dve = sum(m < n for m in DBX_ON_DVE)
                    if n in DBX_ON_DVE:
                        return dbx_by_dve, len(DBX_ON_DVE) * s + by_dve + 1
                    return dbx_by_pool, (N - len(DBX_ON_DVE)) * s + n - by_dve + 1

                class Stage:

                    def __init__(self, s, par, base, phase):
                        self.s, self.par, self.base, self.phase = s, par, base, phase

                    def bank(self, k):
                        return (self.phase + k) % 2

                def emit_act_step(act, st, k, kind, i):
                    s, nx = st.s, st.s + 1
                    q = 1 - st.par
                    bank = fr[:, st.bank(k), :]
                    act.wait_ge(front_full, st.base + k + 1)
                    if kind == "z":
                        if not st.is_prelude:
                            act.wait_ge(g_ready, LC * s + i + 1)
                        act.activation(zl[:, i, :], bank, ACT.Copy).then_inc(front_free, 1)
                    elif kind == "ms":
                        if not st.is_opening:
                            act.wait_ge(u_ready, s + 2)
                        act.activation(rstd[:], bank, ACT.Ln, bias=eps[:, 0:1]).then_inc(front_free, 1)
                        act.wait_ge(front_free, st.base + k + 1)
                        act.activation(rstd[:], rstd[:], ACT.Exp, scale=-0.5).then_inc(rstd_ready, 1)
                    elif kind == "xs":
                        act.activation(xs[:, i % 2, PAD:], bank, ACT.Copy).then_inc(front_free, 1)
                    elif kind == "cv":
                        if i == 0 and not st.is_prelude:
                            act.wait_ge(dx_ready, EC * nx)
                        act.activation(xc[:, i, :], bank, ACT.Identity, bias=cb[:, i:i + 1]).then_inc(front_free, 1)
                    elif kind == "y":
                        act.activation(dx[:, q, i, :], bank, ACT.Copy).then_inc(front_free, 1)
                    elif kind == "o":
                        act.activation(sq[:, i, :], bank, ACT.Copy).then_inc(front_free, 1)
                    elif kind == "bc":
                        act.activation(b_parts[B_HI:B_HI + N, q, :], fr[R:R + N, st.bank(k), :], ACT.Copy)
                        act.activation(dbc[:, q, :], fr[0:DBC, st.bank(k), :], ACT.Copy).then_inc(front_free, 1)
                    elif kind == "cl":
                        if not (st.is_prelude or st.is_first):
                            act.wait_ge(y_added, LC * N * s)
                        act.activation(c_tok[:, q], bank[:, 0:LC * N].rearrange("p (j n) -> p j n", n=N),
                                       ACT.Copy).then_inc(front_free, 1)
                    elif kind == "dx":
                        act.activation(acc[:, q, i, :], bank, ACT.Copy).then_inc(front_free, 1)
                    elif kind == "b":
                        if not (st.is_prelude or st.is_first and i < NBB):
                            act.wait_ge(*dbx_done(s, i - NBB))
                        act.activation(b_all[:, i % NBB, :], bank, ACT.Copy).then_inc(front_free, 1)
                    elif kind == "dl":
                        act.activation(delta[:, q, i, :], bank, ACT.Abs, bias=bdt[:, i:i + 1]).then_inc(p_abs, 1)
                        if i < 2:
                            if not st.is_prelude:
                                act.wait_ge(delta_ready, EC * nx)
                        else:
                            act.wait_ge(delta_ready, EC * nx + i - 1)
                        act.activation(pos[:, i % 2, :], bank, ACT.Relu, bias=bdt[:, i:i + 1]).then_inc(front_free, 1)

                def emit_act_softplus(act, nx, q, i, part):
                    if part == 0:
                        act.wait_ge(p_abs, EC * nx + i + 1)
                        act.activation(delta[:, q, i, :], delta[:, q, i, :], ACT.Exp, scale=-1.0).then_inc(p_exp, 1)
                    else:
                        act.wait_ge(p_exp, EC * nx + i + 1)
                        act.activation(delta[:, q, i, :], delta[:, q, i, :], ACT.Ln, bias=1.0).then_inc(p_log, 1)

                def emit_act_sigmoid(act, buf, clamped, e, l, sig, count, part):
                    if part == 0:
                        act.wait_ge(clamped, count)
                        act.activation(buf, buf, ACT.Exp, scale=-1.0).then_inc(e, 1)
                    elif part == 1:
                        act.wait_ge(e, count)
                        act.activation(buf, buf, ACT.Ln, bias=1.0).then_inc(l, 1)
                    else:
                        act.wait_ge(l, count)
                        act.activation(buf, buf, ACT.Exp, scale=-1.0).then_inc(sig, 1)

                def emit_act_squares(act, m, b):
                    act.wait_ge(x_ready, m + 1)
                    act.wait_ge(x_ready, m + (NB - 2))
                    act.activation(sq[:], xT[:, ds(b, 1), :, :], ACT.Square).then_inc(sq_ready, 1)

                def emit_act_decay(act, s, par, n, c, warm):
                    if n == 0:
                        act.wait_ge(delta_ready, EC * s + c + 1)
                    if warm:
                        act.wait_ge(scanned, EC * (N * s + n - 1) + c + 1)
                    act.activation(da[:, c, :], delta[:, par, c, :], ACT.Exp, scale=neg_a[:, c, n:n + 1]).then_inc(da_ready, 1)

                def emit_act_b_mid(act, nx, q):
                    act.wait_ge(b_low, 2 * nx + 1)
                    act.activation(b_parts[B_MID:B_MID + N, q, :], b_rest[B_MID:B_MID + N, :], ACT.Copy).then_inc(b_mid, 1)

                def act_stage(act, st, back, gate, front, scan, next_scan):
                    s, k = st.s, 0
                    for at in range(LC * N):
                        if front and at == SQUARES_AT:
                            emit_act_squares(act, s + 2, (s + 2) % NB)
                        n, c = at // EC, at % EC
                        if scan and n + 1 < N:
                            emit_act_decay(act, s, st.par, n + 1, c, True)
                        elif next_scan and n + 1 == N:
                            emit_act_decay(act, s + 1, 1 - st.par, 0, c, True)
                        for when, (kind, i), piece in st.schedule:
                            if when == at and is_last((kind, i), piece):
                                emit_act_step(act, st, k, kind, i)
                                k += 1
                            for part in (0, 1):
                                if kind == "dl" and when + 1 + part == at:
                                    emit_act_softplus(act, s + 1, 1 - st.par, i, part)
                        if front and at == MID_AT:
                            emit_act_b_mid(act, s + 1, 1 - st.par)
                        for i in range(EC):
                            for part in range(3):
                                if front and at == V_SIG_AT[i] + part:
                                    emit_act_sigmoid(act, sg[:, i % 2, :], v_clamped, v_exp, v_log, v_sig,
                                                     EC * (s + 1) + i + 1, part)
                                if gate and at == Z_SIG_AT[i] + part:
                                    emit_act_sigmoid(act, g[:, i, :], z_clamped, z_exp, z_log, z_sig,
                                                     LC * s + i + 1, part)

                def emit_pe_step(pe, st, k, kind, i, piece):
                    s, nx = st.s, st.s + 1
                    q = 1 - st.par
                    bank = fr[:, st.bank(k), :]
                    start, stop = piece == 0, is_last((kind, i), piece)
                    if start and not (st.is_opening or st.is_prelude and k == 0):
                        pe.wait_ge(front_free, st.base + k - 1)

                    if kind == "z":
                        if start:
                            pe.wait_ge(u_ready, nx + 1)
                        last = pe.matmul(bank, u[:, q, piece, i * P:(i + 1) * P], w_in[:, piece, ED:2 * ED],
                                         start=start, stop=stop)
                    elif kind == "ms":
                        if start:
                            pe.wait_ge(sq_ready, s + 3)
                        last = pe.matmul(bank, mean_mat[:], sq[:, piece, :], start=start, stop=stop)
                    elif kind == "xs":
                        if start:
                            pe.wait_ge(u_ready, nx + 1)
                        last = pe.matmul(bank, w_in[:, piece, i * P:(i + 1) * P], u[:, q, piece, :], start=start, stop=stop)
                    elif kind == "cv":
                        if start:
                            pe.wait_ge(front_free, st.base + xs_step(st, i) + 1)
                        last = pe.matmul(bank, conv_diag[:, i, piece, :], xs[:, i % 2, piece:piece + L],
                                         start=start, stop=stop)
                    elif kind == "y":
                        pe.wait_ge(yg_ready, LC * s)
                        for j in range(LC):
                            last = pe.transpose(bank[:, j * P:(j + 1) * P], acc[:, q, j, i * P:(i + 1) * P], ident[:])
                    elif kind == "o":
                        pe.wait_ge(front_free, st.base + k_of(st, "y", piece) + 1)
                        last = pe.matmul(bank, w_out[:, piece, i * P:(i + 1) * P], dx[:, q, piece, :], start=start, stop=stop)
                    elif kind == "bc":
                        pe.wait_ge(xc_ready, EC * nx + piece + 1)
                        last = pe.matmul(fr[0:DBC, st.bank(k), :], w_x[:, piece, :], xc[:, piece, :], start=start, stop=stop)
                    elif kind == "dl":
                        pe.wait_ge(front_free, st.base + k_of(st, "bc", 0) + 1)
                        last = pe.matmul(bank, w_dt[:, i * P:(i + 1) * P], dbc[0:R, q, :], start=True, stop=True)
                    elif kind == "cl":
                        for j in range(LC):
                            for c in range(EC):
                                last = pe.matmul(bank[:, j * N:(j + 1) * N], xc[:, c, j * P:(j + 1) * P],
                                                 w_x[:, c, R + N:DBC], start=c == 0, stop=c == EC - 1)
                    elif kind == "dx":
                        for c in range(EC):
                            last = pe.matmul(bank[:, c * P:(c + 1) * P], xc[:, c, i * P:(i + 1) * P],
                                             d_diag[:, c, :], start=True, stop=True)
                    elif kind == "b":
                        if i >= N:
                            pe.wait_ge(b_low, 2 * nx + 2)
                        n, rows = i % N, b_parts[:, st.par if i < N else q, :]
                        last = pe.matmul(bank, b_pick[:, n:n + 1].broadcast_to([R + N, P]), rows, start=True, stop=True)
                    if stop:
                        last.then_inc(front_full, 1)

                def k_of(st, kind, i):
                    return st.order.index((kind, i))

                def xs_step(st, i):
                    return k_of(st, "xs", i)

                def lagged(st, quarter, back):
                    if quarter >= 0:
                        return st.s, st.par, quarter // LC, quarter % LC
                    if back:
                        return st.s - 1, 1 - st.par, N + quarter // LC, quarter % LC
                    return None

                def emit_pe_transposes(pe, s, n, j, warm):
                    at = LC * (N * s + n) + j
                    pe.wait_ge(scanned, EC * (N * s + n) + EC)
                    if warm:
                        pe.wait_ge(y_added, at - 1)
                    for c in range(EC):
                        last = pe.transpose(ht[:, j % 2, c * P:(c + 1) * P], hb[:, n % NHB, c, j * P:(j + 1) * P],
                                            ident[:])
                    last.then_inc(h_tr, 1)

                def pe_stage(pe, st, back, gate, front, scan, next_scan):
                    k = 0
                    for at in range(LC * N):
                        due = lagged(st, at - TR_LAG, back)
                        if scan and due:
                            emit_pe_transposes(pe, due[0], due[2], due[3], not (st.is_first and at - TR_LAG < 2))
                        for when, (kind, i), piece in st.schedule:
                            if when == at:
                                emit_pe_step(pe, st, k, kind, i, piece)
                                k += is_last((kind, i), piece)

                def emit_dbx(eng, s, par, n, b_at, warm):
                    eng.wait_ge(front_free, b_at)
                    if n == 0 or n in DBX_ON_DVE:
                        eng.wait_ge(dx_ready, EC * s + EC)
                    if warm:
                        eng.wait_ge(h_tr, LC * (N * s + n - NHB + 1))
                    eng.tensor_tensor(hb[:, n % NHB], dx[:, par],
                                      b_all[:, n % NBB:n % NBB + 1, :].broadcast_to([P, EC, L]),
                                      ALU.mult).then_inc(dbx_done(s, n)[0], 1)

                def emit_pool_rms(pool, m, par, b):
                    pool.wait_ge(rstd_ready, m + 1)
                    pool.tensor_tensor(u[:, par], xT[:, ds(b, 1), :, :], rstd[:].unsqueeze(1).broadcast_to([P, DC, L]),
                                       ALU.mult).then_inc(u_ready, 1)

                def emit_pool_xc(pool, nx, i):
                    pool.wait_ge(v_sig, EC * nx + i + 1)
                    pool.tensor_tensor(xc[:, i, :], xc[:, i, :], sg[:, i % 2, :], ALU.mult).then_inc(xc_ready, 1)

                def emit_pool_delta(pool, nx, q, i):
                    pool.wait_ge(p_log, EC * nx + i + 1)
                    pool.tensor_tensor(delta[:, q, i, :], delta[:, q, i, :], pos[:, i % 2, :],
                                       ALU.add).then_inc(delta_ready, 1)
                    pool.wait_ge(delta_ready, EC * nx + i + 1)
                    pool.tensor_tensor(dx[:, q, i, :], delta[:, q, i, :], xc[:, i, :], ALU.mult).then_inc(dx_ready, 1)

                def emit_pool_gate(pool, s, i):
                    pool.wait_ge(z_sig, LC * s + i + 1)
                    pool.tensor_tensor(g[:, i, :], g[:, i, :], zl[:, i, :], ALU.mult).then_inc(g_ready, 1)

                def emit_pool_yg(pool, s, q, j):
                    pool.wait_ge(y_added, LC * N * s - LC + j + 1)
                    pool.wait_ge(g_ready, LC * (s - 1) + j + 1)
                    pool.tensor_tensor(acc[:, q, j, :], acc[:, q, j, :], g[:, j, :], ALU.mult).then_inc(yg_ready, 1)

                def pool_stage(pool, st, back, gate, front, scan, next_scan):
                    s, q = st.s, 1 - st.par
                    for at in range(LC * N):
                        n = at // LC
                        if scan and at % LC == 0:
                            if n + 1 < AHEAD:
                                emit_dbx(pool, s, st.par, n + 1, st.base, not st.is_first)
                            elif n + 1 in DBX_ON_DVE:
                                pass
                            elif n + 1 < N:
                                emit_dbx(pool, s, st.par, n + 1, st.base + k_of(st, "b", n + 1) + 1,
                                              not st.is_first or n + 1 >= NHB)
                            elif next_scan:
                                emit_dbx(pool, s + 1, q, 0, st.base + k_of(st, "b", N) + 1, True)
                        if front and at == U_AT:
                            pool.wait_ge(front_free, st.base)
                            emit_pool_rms(pool, s + 2, st.par, (s + 2) % NB)
                        for i in range(EC):
                            if front and at == XC_AT[i]:
                                emit_pool_xc(pool, s + 1, i)
                            if back and at == YG_AT[i]:
                                emit_pool_yg(pool, s, q, i)
                            if gate and at == GATE_AT[i]:
                                emit_pool_gate(pool, s, i)
                            if front and at == DELTA_AT[i]:
                                if i == 0 and back:
                                    pool.wait_ge(front_free, st.base + k_of(st, "o", DC - 1) + 1)
                                emit_pool_delta(pool, s + 1, q, i)

                def emit_dve_scan(dve, s, n, c):
                    dve.wait_ge(da_ready, EC * (N * s + n) + c + 1)
                    if c == 0:
                        dve.wait_ge(*dbx_done(s, n))
                    h = hb[:, n % NHB, c, :]
                    dve.tensor_tensor_scan(h, da[:, c, :], h, 0.0, ALU.mult, ALU.add).then_inc(scanned, 1)

                def emit_dve_y(dve, s, par, n, j):
                    dve.wait_ge(h_tr, LC * (N * s + n) + j + 1)
                    if n > 0:
                        dve.wait_ge(y_added, LC * (N * s + n - 1) + j + 1)
                    dve.scalar_tensor_tensor(acc[:, par, j, :], ht[:, j % 2, :], c_tok[:, par, j, n:n + 1],
                                             acc[:, par, j, :], ALU.mult, ALU.add).then_inc(y_added, 1)

                def emit_dve_residual(dve, st, s, b):
                    dve.wait_ge(front_free, st.base + k_of(st, "o", DC - 1) + 1)
                    dve.scalar_tensor_tensor(xT[:, ds(b, 1), :, :].rearrange("p b k l -> p (b k l)"),
                                             xT[:, ds(b, 1), :, :].rearrange("p b k l -> p (b k l)"), 2.0,
                                             sq[:].rearrange("p k l -> p (k l)"), ALU.mult, ALU.add).then_inc(x_ready, 1)

                def emit_dve_b_split(dve, st, nx, q, part):
                    if part == 0:
                        dve.wait_ge(front_free, st.base + k_of(st, "bc", 0) + 1)
                        dve.tensor_tensor(b_rest[B_MID:B_MID + N, :], dbc[R:R + N, q, :], b_parts[B_HI:B_HI + N, q, :],
                                          ALU.subtract).then_inc(b_low, 1)
                    else:
                        dve.wait_ge(b_mid, nx + 1)
                        dve.tensor_tensor(b_parts[B_LO:B_LO + N, q, :], b_rest[B_MID:B_MID + N, :],
                                          b_parts[B_MID:B_MID + N, q, :], ALU.subtract).then_inc(b_low, 1)

                def emit_dve_clamp_v(dve, st, nx, i):
                    dve.wait_ge(front_free, st.base + k_of(st, "cv", i) + 1)
                    if i >= 2:
                        dve.wait_ge(xc_ready, EC * nx + i - 1)
                    dve.tensor_scalar(sg[:, i % 2, :], xc[:, i, :], SIG_MIN, None, ALU.max).then_inc(v_clamped, 1)

                def emit_dve_clamp_z(dve, st, s, i):
                    dve.wait_ge(front_free, st.base)
                    dve.tensor_scalar(g[:, i, :], zl[:, i, :], SIG_MIN, None, ALU.max).then_inc(z_clamped, 1)

                def dve_stage(dve, st, back, gate, front, scan, next_scan):
                    s = st.s
                    for at in range(LC * N):
                        due = lagged(st, at - Y_LAG, back)
                        n = (at + DBX_BEFORE) // LC
                        if scan and (at + DBX_BEFORE) % LC == 0 and n in DBX_ON_DVE:
                            emit_dbx(dve, s, st.par, n, st.base + k_of(st, "b", n) + 1, True)
                        if scan:
                            emit_dve_scan(dve, s, at // EC, at % EC)
                            if at == Y_LAG:
                                dve.wait_ge(front_free, st.base)
                            if due:
                                emit_dve_y(dve, due[0], due[1], due[2], due[3])
                        for i in range(EC):
                            if front and at == V_CLAMP_AT[i]:
                                emit_dve_clamp_v(dve, st, s + 1, i)
                            if gate and at == Z_CLAMP_AT[i]:
                                if i == 0 and back:
                                    dve.wait_ge(yg_ready, LC * s)
                                emit_dve_clamp_z(dve, st, s, i)
                        for part in (0, 1):
                            if front and at == SPLIT_AT[part]:
                                emit_dve_b_split(dve, st, s + 1, 1 - st.par, part)
                        if back and at == RESIDUAL_AT:
                            emit_dve_residual(dve, st, s, (s - 1 + NB) % NB)

                def make(s, par, base, phase, back, gate, front, scan, next_scan):
                    st = Stage(s, par, base, phase % 2)
                    st.schedule = schedule(back, front, scan, next_scan)
                    st.order = [step for _, step, piece in st.schedule if piece == 0]
                    st.is_prelude, st.is_first = front and not gate, gate and front and not back
                    st.is_opening = False
                    return st

                PAIRS = (STAGES - 2) // 2
                BASE0 = 1 + N_FRONT + AHEAD
                BASE1 = BASE0 + N_FRONT + N

                def drive(eng, stage_fn, opening, prelude, flush):
                    st = Stage(-2, 0, 0, 0)
                    st.is_opening, st.is_prelude = True, False
                    opening(eng, st)
                    kind = (False, False, True, False, False)
                    st = make(-1, 1, 1, 1, *kind)
                    stage_fn(eng, st, *kind)
                    prelude(eng, st)
                    kind = (False, True, True, True, True)
                    stage_fn(eng, make(0, 0, BASE0, BASE0, *kind), *kind)
                    kind = (True, True, True, True, True)
                    with eng.Fori(0, PAIRS) as t:
                        for half in (0, 1):
                            st = make(t * 2 + (1 + half), (1 + half) % 2, t * (2 * N_ALL) + (BASE1 + half * N_ALL),
                                      BASE1 + half * N_ALL, *kind)
                            stage_fn(eng, st, *kind)
                    last = STAGES - 1
                    base = BASE1 + (STAGES - 2) * N_ALL
                    kind = (True, True, False, True, False)
                    stage_fn(eng, make(last, last % 2, base, base, *kind), *kind)
                    flush(eng)
                    base += N_BACK + N - AHEAD
                    kind = (True, False, False, False, False)
                    stage_fn(eng, make(STAGES, STAGES % 2, base, base, *kind), *kind)

                def nothing(*_):
                    pass

                LAST, LAST_PAR = STAGES - 1, (STAGES - 1) % 2

                with nc.Block() as block:
                    @block.scalar
                    def _(act):
                        act.wait_ge(pads, 4)

                        def opening(act, st):
                            emit_act_squares(act, 0, 0)
                            emit_act_step(act, st, 0, "ms", 0)

                        def prelude(act, st):
                            for c in range(EC):
                                emit_act_decay(act, 0, 0, 0, c, False)
                            for i in range(AHEAD):
                                emit_act_step(act, st, N_FRONT + i, "b", N + i)
                        drive(act, act_stage, opening, prelude, nothing)

                    @block.tensor
                    def _(pe):
                        def opening(pe, st):
                            for piece in range(PIECES["ms"]):
                                emit_pe_step(pe, st, 0, "ms", 0, piece)

                        def prelude(pe, st):
                            for i in range(AHEAD):
                                emit_pe_step(pe, st, N_FRONT + i, "b", N + i, 0)

                        def flush(pe):
                            for quarter in range(LC * N - TR_LAG, LC * N):
                                emit_pe_transposes(pe, LAST, quarter // LC, quarter % LC, True)
                        drive(pe, pe_stage, opening, prelude, flush)

                    @block.gpsimd
                    def _(pool):
                        def opening(pool, st):
                            emit_pool_rms(pool, 0, 0, 0)

                        def prelude(pool, st):
                            emit_dbx(pool, 0, 0, 0, 1 + N_FRONT + 1, False)
                        drive(pool, pool_stage, opening, prelude, nothing)

                    @block.vector
                    def _(dve):
                        dve.memset(xs[:], 0.0).then_inc(pads, 1)
                        dve.memset(b_parts[:], 0.0).then_inc(pads, 1)
                        dve.tensor_tensor(b_pick[:], ident[0:R + N, B_HI:B_HI + N], ident[0:R + N, B_MID:B_MID + N],
                                          ALU.add).then_inc(pads, 1)
                        dve.wait_ge(pads, 3)
                        dve.tensor_tensor(b_pick[:], b_pick[:], ident[0:R + N, B_LO:B_LO + N], ALU.add).then_inc(pads, 1)

                        def flush(dve):
                            for quarter in range(LC * N - Y_LAG, LC * N):
                                emit_dve_y(dve, LAST, LAST_PAR, quarter // LC, quarter % LC)
                        drive(dve, dve_stage, nothing, nothing, flush)

        with ExitStack() as s3:
            GK = 3 * DC
            lnw = sb(s3, "lnw", [P, D])
            lnb = sb(s3, "lnb", [P, D])
            onorm = sb(s3, "onorm", [P, D])
            gate_w = sb(s3, "gate_w", [P, GK, 32 + NH])
            gate_bias = sb(s3, "gate_bias", [32 + NH, 3])
            ones = sb(s3, "ones", [NH, L])
            neg_sel = sb(s3, "neg_sel", [NH, NH])
            wg = sb(s3, "wg", [P, DC, HID])
            wu = sb(s3, "wu", [P, DC, HID])
            wd = sb(s3, "wd", [P, HC, D])
            w_int = sb(s3, "w_int", [P, HC * D], I32)
            w_f = sb(s3, "w_f", [P, HC * D])
            xin = sb(s3, "xin", [P, LC, D])
            cx = sb(s3, "cx", [P, LC, D])
            xm = sb(s3, "xm", [P, DC, L])
            t_a = sb(s3, "t_a", [P, LC, D])
            x1 = sb(s3, "x1", [P, LC, D])
            x2 = sb(s3, "x2", [P, LC, D])
            nrm = sb(s3, "nrm", [P, LC, D])
            qt = sb(s3, "qt", [P, DC, L])
            ct = sb(s3, "ct", [P, DC, L])
            x2t = sb(s3, "x2t", [P, DC, L])
            v1 = sb(s3, "v1", [P, LC, NH, DH + 1])
            stats3 = sb(s3, "stats3", [P, 4 * LC, 6])
            mv3 = sb(s3, "mv3", [P, 4 * LC, 2])
            lnv3 = sb(s3, "lnv3", [P, 4 * LC])
            carrier = sb(s3, "carrier", [P, 1])
            carrier_p = sb(s3, "carrier_p", [P, 1])
            fa = sb(s3, "fa", [32 + NH, L])
            fr_ = sb(s3, "fr_", [32 + NH, L])
            fs = sb(s3, "fs", [NH, L])
            ncs = sb(s3, "ncs", [NH, L])
            ga = sb(s3, "ga", [NH, L])
            gm = sb(s3, "gm", [NH, L])
            ge = sb(s3, "ge", [NH, L])
            ae = sb(s3, "ae", [P, LC, 2 * NH])
            dm = sb(s3, "dm", [P, 2, LC, L])
            osb = sb(s3, "osb", [P, LC, NH, DH + 1])
            den = sb(s3, "den", [P, LC, NH])
            kk = sb(s3, "kk", [P, LC, NH])
            gl = sb(s3, "gl", [P, 2, L])
            gs = sb(s3, "gs", [P, 2, L])
            hid = sb(s3, "hid", [P, HC, L])
            o_sb = sb(s3, "o_sb", [P, LC, D])
            ps_a = pb(s3, "ps_a", [P, 2, L])
            ps_b = pb(s3, "ps_b", [P, 2, L])
            ps_s = pb(s3, "ps_s", [P, 4, L])

            S = {k: sem("e_" + k) for k in (
                "consts", "w_in", "w_scaled", "w_tr", "w_evac", "x_in", "c_in", "out_free", "out_ready", "set", "act_set",
                "xm_ready", "x_tok", "stats", "mv", "log", "rstd", "normed", "lnm_w", "lnm_b", "x1_ready",
                "c_tr", "c_t_ready", "v_ready", "q_tr", "q_t_ready", "gates", "f_abs", "f_relu", "f_exp", "f_log",
                "i_ready", "f_sum", "cs_ready", "ga_ready", "gm_ready", "ge_diff", "ge_ready", "ae_tr", "ae_ready",
                "m_bc", "d_arg", "qk", "d_exp", "d_masked", "c_ready", "av", "h_stats", "h_mv", "h_neg", "h_den", "h_rec", "o_evac",
                "h_t2", "h_log", "h_rs", "h_k", "h_sub", "h_mul", "h_scaled", "x2_ready", "x2_tr",
                "x2t_ready", "ffn_g", "ffn_u", "gl_ready", "g_cl", "g_exp", "g_log", "g_sig", "g_silu", "hid_ready",
                "down", "o_base")}

            def three(ap, k):
                return ap.rearrange("p (k f) -> p k f", k=k)

            oh = [ps_a[:, 0], ps_a[:, 1], ps_b[:, 0], ps_b[:, 1]]

            def oh_heads(j):
                return oh[j][:, 0:NH * (DH + 1)].rearrange("p (h d) -> p h d", h=NH)

            N_CONST = 7
            GATE_BANK, UP_BANK = (2, 0), (3, 1)
            F_AT = 32

            def down_half(j):
                return ps_s[:, 2 + j // 2, (j % 2) * D:(j % 2 + 1) * D]

            def pipelined(eng, entry):
                entry(0, None)
                with eng.Fori(1, NB) as b:
                    entry(b, b - 1)
                entry(None, NB - 1)

            with nc.Block() as block:
                @block.sync
                def _(sp):
                    for dst, src in ((lnw, ln_w), (lnb, ln_b), (onorm, outnorm_scale)):
                        sp.dma_start(dst[:], src.partition_broadcast(P)).then_inc(S["consts"], 16)
                    sp.wait_ge(S["set"], 3)
                    for at, src in ((0, igate_kernel), (F_AT, fgate_kernel)):
                        sp.dma_start(gate_w[:, :, at:at + NH], src.rearrange("(k p) h -> p k h", p=P)).then_inc(S["consts"], 16)
                    sp.dma_start(gate_bias[0:NH, 0:1], igate_bias.rearrange("(h a) -> h a", a=1),
                                 allow_slow_non_contiguous=True).then_inc(S["consts"], 16)
                    sp.dma_start(gate_bias[F_AT:F_AT + NH, 1:2], fgate_bias.rearrange("(h a) -> h a", a=1),
                                 allow_slow_non_contiguous=True).then_inc(S["consts"], 16)
                    sp.sem_inc(S["out_free"], 16)
                    for m, w in enumerate((w_gate, w_up)):
                        if m:
                            sp.wait_ge(S["w_scaled"], m)
                        sp.dma_start(three(w_int[:], HC), w.rearrange("(c p) d -> p c d", p=P)).then_inc(S["w_in"], 16)
                    sp.wait_ge(S["w_scaled"], 2)
                    sp.dma_start(three(w_int[:], DC), w_down.rearrange("(k p) h -> p k h", p=P)).then_inc(S["w_in"], 16)

                    def load(b):
                        sp.dma_start(xin[:], x[ds(b, 1)].rearrange("b (j p) d -> p (b j) d", p=P)).then_inc(S["x_in"], 16)
                        sp.dma_start(cx[:], ctx_1024[ds(b, 1)].rearrange("b (j p) d -> p (b j) d", p=P)).then_inc(S["c_in"], 16)

                    def store(b):
                        sp.wait_ge(S["out_ready"], (b + 1) * LC)
                        sp.dma_start(out[ds(b, 1)].rearrange("b (j p) d -> p (b j) d", p=P), o_sb[:]).then_inc(S["out_free"], 16)

                    load(0)
                    with sp.Fori(0, NB - 1) as b:
                        sp.wait_ge(S["x1_ready"], b + 1)
                        sp.wait_ge(S["c_t_ready"], b + 1)
                        sp.wait_ge(S["v_ready"], b + 1)
                        load(b + 1)
                        store(b)
                    store(NB - 1)
                    sp.wait_ge(S["out_free"], 16 * (NB + 1))

                @block.scalar
                def _(act):
                    def evac(out_, in_, full, count, done):
                        act.wait_ge(S[full], count)
                        act.activation(out_, in_, ACT.Copy).then_inc(S[done], 1)

                    def rsqrt(out_, in_, ready, count, log, done, e):
                        act.wait_ge(S[ready], count)
                        act.activation(out_, in_, ACT.Ln, bias=e).then_inc(S[log], 1)
                        act.wait_ge(S[log], count)
                        act.activation(out_, out_, ACT.Exp, scale=-0.5).then_inc(S[done], 1)

                    act.wait_ge(S["consts"], 16 * N_CONST)
                    act.activation(gate_bias[F_AT:F_AT + NH, 2:3], gate_bias[F_AT:F_AT + NH, 1:2], ACT.Copy, scale=-1.0).then_inc(S["act_set"], 1)
                    act.activation(neg_sel[:], ident[0:NH, 0:NH], ACT.Copy, scale=-1.0).then_inc(S["act_set"], 1)
                    act.wait_ge(S["act_set"], 2)
                    for m, w in enumerate((wg, wu)):
                        for k in range(DC):
                            act.wait_ge(S["w_tr"], m * DC + k + 1)
                            act.activation(w[:, k, 0:L], ps_s[:, 2 * k, :], ACT.Copy)
                            act.activation(w[:, k, L:HID], ps_s[:, 2 * k + 1, 0:HID - L], ACT.Copy).then_inc(S["w_evac"], 1)
                    act.wait_ge(S["w_tr"], 2 * DC + 1)
                    act.activation(wd[:, 0:4, :], ps_s[:, 0:2, :].rearrange("p a l -> p (a l)").rearrange("p (c d) -> p c d", d=D), ACT.Copy)
                    act.activation(wd[:, 4:6, :], three(ps_s[:, 2, :], 2), ACT.Copy).then_inc(S["w_evac"], 1)
                    def ffn_gate(f, c):
                        n_ = f * HC + c + 1
                        if c >= 2:
                            act.wait_ge(S["g_silu"], n_ - 2)
                        evac(gl[:, c % 2, :], ps_s[:, GATE_BANK[c % 2], :], "ffn_g", n_, "gl_ready")

                    def ffn_sigmoid(f, c):
                        n_ = f * HC + c + 1
                        buf = gs[:, c % 2, :]
                        act.wait_ge(S["g_cl"], n_)
                        act.activation(buf, buf, ACT.Exp, scale=-1.0).then_inc(S["g_exp"], 1)
                        act.wait_ge(S["g_exp"], n_)
                        act.activation(buf, buf, ACT.Ln, bias=1.0).then_inc(S["g_log"], 1)
                        act.wait_ge(S["g_log"], n_)
                        act.activation(buf, buf, ACT.Exp, scale=-1.0).then_inc(S["g_sig"], 1)

                    def entry(b, f):
                        def gates(c):
                            if f is not None:
                                ffn_gate(f, c)

                        def sigmoids(c):
                            if f is not None:
                                ffn_sigmoid(f, c)

                        def keep_x2():
                            act.wait_ge(S["out_free"], 16 * (f + 1))
                            act.activation(o_sb[:], x2[:], ACT.Copy).then_inc(S["o_base"], 1)

                        if b is None:
                            keep_x2()
                            gates(0)
                            for c in range(HC):
                                if c + 1 < HC:
                                    gates(c + 1)
                                sigmoids(c)
                            return
                        act.activation(xm[:], xT[:, ds(b, 1), :, :], ACT.Copy).then_inc(S["xm_ready"], 1)
                        act.wait_ge(S["set"], 3)
                        act.wait_ge(S["c_in"], 16 * (b + 1))
                        for i in range(LC):
                            last = act.activation(v1[:, i, :, 0:DH], cx[:, i, :].rearrange("p (h d) -> p h d", h=NH), ACT.Copy)
                        last.then_inc(S["v_ready"], 1)
                        evac(ct[:], ps_b[:], "c_tr", b + 1, "c_t_ready")
                        gates(0)
                        rsqrt(lnv3[:, 0:LC], mv3[:, 0:LC, 1], "mv", 3 * b + 1, "log", "rstd", eps[:, 0:1])
                        gates(1)
                        sigmoids(0)
                        sigmoids(1)
                        gates(2)
                        rsqrt(lnv3[:, 0:LC], mv3[:, 0:LC, 1], "mv", 3 * b + 2, "log", "rstd", eps[:, 0:1])
                        gates(3)
                        sigmoids(2)
                        sigmoids(3)
                        evac(qt[:], ps_a[:], "q_tr", b + 1, "q_t_ready")
                        act.wait_ge(S["gates"], b + 1)
                        fg = slice(F_AT, F_AT + NH)
                        act.activation(fa[fg], ps_s[fg, 0, :], ACT.Abs, bias=gate_bias[fg, 1:2]).then_inc(S["f_abs"], 1)
                        act.wait_ge(S["f_abs"], b + 1)
                        act.activation(fa[fg], fa[fg], ACT.Exp, scale=-1.0).then_inc(S["f_exp"], 1)
                        act.activation(fr_[fg], ps_s[fg, 0, :], ACT.Relu, scale=-1.0, bias=gate_bias[fg, 2:3]).then_inc(S["f_relu"], 1)
                        act.wait_ge(S["f_exp"], b + 1)
                        act.activation(fa[fg], fa[fg], ACT.Ln, bias=1.0).then_inc(S["f_log"], 1)
                        act.activation(ga[:], ps_s[0:NH, 0, :], ACT.Identity, bias=gate_bias[0:NH, 0:1]).then_inc(S["i_ready"], 1)
                        gates(4)
                        sigmoids(4)
                        act.wait_ge(S["ge_diff"], b + 1)
                        act.activation(ge[:], ge[:], ACT.Exp).then_inc(S["ge_ready"], 1)
                        evac(ae[:], ps_s[:, 0, 0:LC * 2 * NH].rearrange("p (j g) -> p j g", j=LC), "ae_tr", b + 1, "ae_ready")
                        if f is not None:
                            keep_x2()
                        for h in range(NH):
                            for i in range(LC):
                                dlog = dm[:, h % 2, i, i * P:L]
                                act.wait_ge(S["d_arg"], (b * NH + h) * LC + i + 1)
                                act.activation(dlog, dlog, ACT.Exp).then_inc(S["d_exp"], 1)
                        gates(5)
                        sigmoids(5)
                        act.wait_ge(S["av"], (b + 1) * NH)
                        for j in range(LC):
                            act.activation(osb[:, j], oh_heads(j), ACT.Copy).then_inc(S["o_evac"], 1)
                        rsqrt(kk[:], kk[:], "h_t2", b + 1, "h_log", "h_rs", eps[:, 1:2])
                        rsqrt(lnv3[:, 0:LC], mv3[:, 0:LC, 1], "mv", 3 * b + 3, "log", "rstd", eps[:, 0:1])
                        evac(x2t[:], ps_a[:], "x2_tr", b + 1, "x2t_ready")

                    act.wait_ge(S["w_evac"], 2 * DC + 1)
                    pipelined(act, entry)

                @block.tensor
                def _(pe):
                    for m, w in enumerate((wg, wu)):
                        pe.wait_ge(S["w_scaled"], m + 1)
                        if m:
                            pe.wait_ge(S["w_evac"], m * DC)
                        wf = three(w_f[:], HC)
                        for k in range(DC):
                            for c in range(HC):
                                dst = ps_s[:, 2 * k + c // 4, (c % 4) * P:(c % 4 + 1) * P]
                                last = pe.transpose(dst, wf[:, c, k * P:(k + 1) * P], ident[:])
                            last.then_inc(S["w_tr"], 1)
                    pe.wait_ge(S["w_scaled"], 3)
                    pe.wait_ge(S["w_evac"], 2 * DC)
                    wf = three(w_f[:], DC)
                    for c in range(HC):
                        for k in range(DC):
                            at = c * D + k * P
                            last = pe.transpose(ps_s[:, at // L, at % L:at % L + P], wf[:, k, c * P:(c + 1) * P], ident[:])
                    last.then_inc(S["w_tr"], 1)

                    def to_channels(dst, src, done):
                        for k in range(DC):
                            for j in range(LC):
                                last = pe.transpose(dst[:, k, j * P:(j + 1) * P], src[:, j, k * P:(k + 1) * P], ident[:])
                        last.then_inc(S[done], 1)

                    def ffn_chunk(f, c):
                        for w, banks, read, done in ((wg, GATE_BANK, "gl_ready", "ffn_g"), (wu, UP_BANK, "hid_ready", "ffn_u")):
                            if c >= 2:
                                pe.wait_ge(S[read], f * HC + c - 1)
                            for k in range(DC):
                                last = pe.matmul(ps_s[:, banks[c % 2], :], w[:, k, c * P:(c + 1) * P], x2t[:, k, :],
                                                 start=k == 0, stop=k == DC - 1)
                            last.then_inc(S[done], 1)

                    def ffn_down(f):
                        pe.wait_ge(S["hid_ready"], (f + 1) * HC)
                        for j in range(LC):
                            for c in range(HC):
                                last = pe.matmul(down_half(j), hid[:, c, j * P:(j + 1) * P], wd[:, c, :],
                                                 start=c == 0, stop=c == HC - 1)
                            last.then_inc(S["down"], 1)

                    def entry(b, f):
                        def ffn(*chunks):
                            if f is not None:
                                for c in chunks:
                                    ffn_chunk(f, c)

                        if b is None:
                            pe.wait_ge(S["x2t_ready"], f + 1)
                            ffn(*range(HC))
                            ffn_down(f)
                            return
                        pe.wait_ge(S["xm_ready"], b + 1)
                        for j in range(LC):
                            for k in range(DC):
                                last = pe.transpose(ps_a[:, j // 2, (j % 2) * D + k * P:(j % 2) * D + (k + 1) * P],
                                                    xm[:, k, j * P:(j + 1) * P], ident[:])
                        last.then_inc(S["x_tok"], 1)
                        pe.wait_ge(S["c_in"], 16 * (b + 1))
                        to_channels(ps_b, cx, "c_tr")
                        ffn(0, 1, 2, 3)
                        pe.wait_ge(S["c_t_ready"], b + 1)
                        if f is not None:
                            pe.wait_ge(S["gl_ready"], f * HC + 4)
                        for k in range(DC, GK):
                            pe.matmul(ps_s[0:F_AT + NH, 0, :], gate_w[:, k, :], ct[:, k % DC, :], start=k == DC, stop=False)
                        pe.wait_ge(S["normed"], 3 * b + 2)
                        to_channels(ps_a, nrm, "q_tr")
                        pe.wait_ge(S["q_t_ready"], b + 1)
                        for k in range(DC):
                            last = pe.matmul(ps_s[0:F_AT + NH, 0, :], gate_w[:, k, :], qt[:, k, :], start=False, stop=k == DC - 1)
                        last.then_inc(S["gates"], 1)
                        ffn(4)
                        pe.wait_ge(S["ga_ready"], b + 1)
                        pe.wait_ge(S["ge_ready"], b + 1)
                        for j in range(LC):
                            for m, src in enumerate((ga, ge)):
                                last = pe.matmul(ps_s[:, 0, (2 * j + m) * NH:(2 * j + m + 1) * NH],
                                                 src[:, j * P:(j + 1) * P], ident[0:NH, 0:NH], start=True, stop=True)
                        last.then_inc(S["ae_tr"], 1)
                        pe.wait_ge(S["v_ready"], b + 1)
                        pe.wait_ge(S["ae_ready"], b + 1)
                        if f is not None:
                            pe.wait_ge(S["gl_ready"], f * HC + 5)
                            pe.wait_ge(S["hid_ready"], f * HC + 5)

                        def attend(h):
                            pe.wait_ge(S["c_ready"], (b * NH + h + 1) * LC)
                            for j in range(LC):
                                for i in range(j + 1):
                                    last = pe.matmul(oh[j][:, h * (DH + 1):(h + 1) * (DH + 1)],
                                                     dm[:, h % 2, i, j * P:(j + 1) * P], v1[:, i, h, :],
                                                     start=i == 0, stop=i == j)
                            last.then_inc(S["av"], 1)

                        for h in range(NH):
                            at = (h % 2) * DH
                            if h:
                                pe.wait_ge(S["d_arg"], (b * NH + h) * LC)
                            pe.matmul(ps_s[:, 0, :], neg_sel[:, h:h + 1].broadcast_to([NH, P]), gm[:],
                                      start=True, stop=True).then_inc(S["m_bc"], 1)
                            for i in range(LC):
                                if i == 0 and h:
                                    pe.wait_ge(S["c_ready"], (b * NH + h) * LC)
                                if i == 3:
                                    pe.wait_ge(S["c_ready"], (b * NH + h) * LC + 1)
                                pe.matmul(ps_s[:, 1 + i % 3, i * P:L], ct[at:at + DH, h // 2, i * P:(i + 1) * P],
                                          qt[at:at + DH, h // 2, i * P:L], start=True, stop=True).then_inc(S["qk"], 1)
                            if h:
                                attend(h - 1)
                        if f is not None:
                            pe.wait_ge(S["c_ready"], (b + 1) * NH * LC)
                        ffn(5)
                        attend(NH - 1)
                        if f is not None:
                            ffn_down(f)
                        pe.wait_ge(S["normed"], 3 * b + 3)
                        to_channels(ps_a, nrm, "x2_tr")
                        if f is not None:
                            pe.wait_ge(S["out_ready"], (f + 1) * LC)

                    pe.wait_ge(S["w_evac"], 2 * DC + 1)
                    pipelined(pe, entry)

                @block.gpsimd
                def _(pool):
                    pool.memset(ones[:], 1.0).then_inc(S["set"], 1)
                    pool.memset(v1[:], 1.0).then_inc(S["set"], 1)
                    pool.memset(gate_w[:], 0.0).then_inc(S["set"], 1)
                    def entry(b, f):
                        def ffn(*chunks):
                            if f is not None:
                                for c in chunks:
                                    pool.wait_ge(S["g_sig"], f * HC + c + 1)
                                    pool.tensor_tensor(gs[:, c % 2, :], gs[:, c % 2, :], gl[:, c % 2, :],
                                                       ALU.mult).then_inc(S["g_silu"], 1)

                        if b is None:
                            ffn(*range(HC))
                            return
                        ffn(*range(HC - 1))
                        for h in range(NH):
                            pool.wait_ge(S["d_exp"], (b * NH + h + 1) * LC)
                            pool.tensor_tensor(carrier_p[:], eps[:, 0:1], eps[:, 0:1], ALU.add)
                            for i in range(LC):
                                diag = dm[:, h % 2, i, i * P:(i + 1) * P]
                                pool.affine_select(out=diag, in_=diag, compare_op=ALU.is_ge, fill=0.0, base=0,
                                                   pattern=[[1, P]], channel_multiplier=-1).then_inc(S["d_masked"], 1)
                        ffn(HC - 1)

                    pipelined(pool, entry)

                @block.vector
                def _(dve):
                    for m in range(3):
                        dve.wait_ge(S["w_in"], 16 * (m + 1))
                        if m:
                            dve.wait_ge(S["w_tr"], m * DC)
                        dve.tensor_scalar(w_f[:], w_int[:], FFN_SCALE, None, ALU.mult).then_inc(S["w_scaled"], 1)

                    def per_token(w):
                        return w[:].unsqueeze(1).broadcast_to([P, LC, D])

                    def stats_of(parts, wait, count, stat, done, times):
                        dve.wait_ge(S[wait], count)
                        for m, part in enumerate(parts):
                            dve.bn_stats(stats3[:, m, :], part).then_inc(S[stat], 1)
                        dve.wait_ge(S[stat], times * len(parts))
                        dve.memset(carrier[:], 0.0)
                        for m in range(len(parts)):
                            last = dve.bn_aggr(mv3[:, m, :], stats3[:, m, :])
                        last.then_inc(S[done], 1)

                    def normalise(src, k):
                        dve.wait_ge(S["rstd"], k)
                        for j in range(LC):
                            last = dve.tensor_scalar(nrm[:, j, :], src(j), mv3[:, j, 0:1], lnv3[:, j:j + 1],
                                                     ALU.subtract, ALU.mult)
                        last.then_inc(S["normed"], 1)

                    def clamp(f, c):
                        n_ = f * HC + c + 1
                        dve.wait_ge(S["gl_ready"], n_)
                        if c >= 2:
                            dve.wait_ge(S["hid_ready"], n_ - 2)
                        dve.tensor_scalar(gs[:, c % 2, :], gl[:, c % 2, :], SIG_MIN, None, ALU.max).then_inc(S["g_cl"], 1)

                    def hidden(f, c):
                        n_ = f * HC + c + 1
                        dve.wait_ge(S["g_silu"], n_)
                        dve.wait_ge(S["ffn_u"], n_)
                        dve.tensor_tensor(hid[:, c, :], gs[:, c % 2, :], ps_s[:, UP_BANK[c % 2], :], ALU.mult).then_inc(S["hid_ready"], 1)

                    def output(f):
                        dve.wait_ge(S["o_base"], f + 1)
                        for j in range(LC):
                            dve.wait_ge(S["down"], f * LC + 2 * (j // 2) + 2)
                            dve.tensor_tensor(o_sb[:, j, :], o_sb[:, j, :], down_half(j), ALU.add).then_inc(S["out_ready"], 1)

                    def tok(j):
                        return ps_a[:, j // 2, (j % 2) * D:(j % 2 + 1) * D]

                    def entry(b, f):
                        def ffn(step, c):
                            if f is not None:
                                step(f, c)

                        if b is None:
                            clamp(f, 0)
                            for c in range(HC):
                                if c + 1 < HC:
                                    clamp(f, c + 1)
                                hidden(f, c)
                            output(f)
                            return
                        stats_of([tok(j) for j in range(LC)], "x_tok", b + 1, "stats", "mv", 3 * b + 1)
                        ffn(clamp, 0)
                        normalise(tok, 3 * b + 1)
                        dve.wait_ge(S["normed"], 3 * b + 1)
                        dve.tensor_tensor(t_a[:], nrm[:], per_token(lnw), ALU.mult).then_inc(S["lnm_w"], 1)
                        ffn(clamp, 1)
                        dve.wait_ge(S["lnm_w"], b + 1)
                        dve.tensor_tensor(t_a[:], t_a[:], per_token(lnb), ALU.add).then_inc(S["lnm_b"], 1)
                        dve.wait_ge(S["lnm_b"], b + 1)
                        dve.wait_ge(S["x_in"], 16 * (b + 1))
                        dve.tensor_tensor(x1[:], t_a[:], xin[:], ALU.add).then_inc(S["x1_ready"], 1)
                        stats_of([x1[:, j, :] for j in range(LC)], "x1_ready", b + 1, "stats", "mv", 3 * b + 2)
                        ffn(hidden, 0)
                        ffn(hidden, 1)
                        ffn(clamp, 2)
                        normalise(lambda j: x1[:, j, :], 3 * b + 2)
                        ffn(clamp, 3)
                        ffn(hidden, 2)
                        ffn(hidden, 3)
                        dve.wait_ge(S["f_log"], b + 1)
                        dve.wait_ge(S["f_relu"], b + 1)
                        dve.tensor_tensor(fs[:], fa[F_AT:F_AT + NH], fr_[F_AT:F_AT + NH], ALU.add).then_inc(S["f_sum"], 1)
                        dve.wait_ge(S["f_sum"], b + 1)
                        dve.tensor_tensor_scan(ncs[:], ones[:], fs[:], 0.0, ALU.mult, ALU.add).then_inc(S["cs_ready"], 1)
                        dve.wait_ge(S["cs_ready"], b + 1)
                        dve.wait_ge(S["i_ready"], b + 1)
                        dve.tensor_tensor(ga[:], ga[:], ncs[:], ALU.add).then_inc(S["ga_ready"], 1)
                        ffn(clamp, 4)
                        dve.wait_ge(S["ga_ready"], b + 1)
                        dve.tensor_tensor_scan(gm[:], ga[:], ga[:], -3.0e38, ALU.max, ALU.max).then_inc(S["gm_ready"], 1)
                        dve.wait_ge(S["gm_ready"], b + 1)
                        dve.tensor_tensor(ge[:], ncs[:], gm[:], ALU.subtract).then_inc(S["ge_diff"], 1)
                        ffn(hidden, 4)
                        dve.wait_ge(S["ae_ready"], b + 1)
                        for h in range(NH):
                            dve.wait_ge(S["m_bc"], b * NH + h + 1)
                            if h >= 2:
                                dve.wait_ge(S["av"], b * NH + h - 1)
                            for i in range(LC):
                                dve.tensor_scalar(dm[:, h % 2, i, i * P:L], ps_s[:, 0, i * P:L], ae[:, i, h:h + 1],
                                                  0.0, ALU.add, ALU.min).then_inc(S["d_arg"], 1)
                            for i in range(LC):
                                n_ = (b * NH + h) * LC + i + 1
                                dve.wait_ge(S["qk"], n_)
                                dve.wait_ge(S["d_masked"], n_)
                                c_blk = dm[:, h % 2, i, i * P:L]
                                dve.scalar_tensor_tensor(c_blk, ps_s[:, 1 + i % 3, i * P:L], DH ** -0.5, c_blk,
                                                         ALU.mult, ALU.mult).then_inc(S["c_ready"], 1)
                        ffn(clamp, 5)
                        row_sum = osb[:, :, :, DH]
                        dve.wait_ge(S["o_evac"], (b + 1) * LC)
                        dve.scalar_tensor_tensor(den[:], row_sum, -1.0, ae[:, :, NH:2 * NH], ALU.mult,
                                                 ALU.max).then_inc(S["h_neg"], 1)
                        dve.wait_ge(S["h_neg"], b + 1)
                        dve.tensor_tensor(den[:], row_sum, den[:], ALU.max).then_inc(S["h_den"], 1)
                        ffn(hidden, 5)
                        stats_of([osb[:, j, h, 0:DH] for j in range(LC) for h in range(NH)], "o_evac", (b + 1) * LC,
                                 "h_stats", "h_mv", b + 1)
                        dve.wait_ge(S["h_den"], b + 1)
                        dve.tensor_scalar(den[:], den[:], EPS_MLSTM, None, ALU.add).then_inc(S["h_rec"], 1)
                        dve.wait_ge(S["h_rec"], 3 * b + 1)
                        dve.reciprocal(den[:], den[:]).then_inc(S["h_rec"], 1)
                        dve.wait_ge(S["h_rec"], 3 * b + 2)
                        dve.tensor_tensor(kk[:], den[:], den[:], ALU.mult).then_inc(S["h_rec"], 1)
                        dve.wait_ge(S["h_rec"], 3 * b + 3)
                        dve.wait_ge(S["h_mv"], b + 1)
                        dve.tensor_tensor(kk[:], kk[:], mv3[:, :, 1].rearrange("p (j h) -> p j h", h=NH),
                                          ALU.mult).then_inc(S["h_t2"], 1)
                        flat = osb[:].rearrange("p j h d -> p (j h) d")[:, :, 0:DH]
                        dve.tensor_tensor(flat, flat, mv3[:, :, 0:1].broadcast_to([P, LC * NH, DH]),
                                          ALU.subtract).then_inc(S["h_sub"], 1)
                        dve.wait_ge(S["h_rs"], b + 1)
                        dve.tensor_tensor(kk[:], kk[:], den[:], ALU.mult).then_inc(S["h_k"], 1)
                        dve.wait_ge(S["h_k"], b + 1)
                        dve.wait_ge(S["h_sub"], b + 1)
                        dve.tensor_tensor(flat, flat, kk[:].rearrange("p j h -> p (j h)").unsqueeze(2)
                                          .broadcast_to([P, LC * NH, DH]), ALU.mult).then_inc(S["h_mul"], 1)
                        dve.wait_ge(S["h_mul"], b + 1)
                        dve.tensor_tensor(t_a[:].rearrange("p j (h d) -> p j h d", h=NH), osb[:, :, :, 0:DH],
                                          onorm[:].rearrange("p (h d) -> p h d", h=NH).unsqueeze(1)
                                          .broadcast_to([P, LC, NH, DH]), ALU.mult).then_inc(S["h_scaled"], 1)
                        if f is not None:
                            dve.wait_ge(S["o_base"], f + 1)
                        dve.wait_ge(S["h_scaled"], b + 1)
                        dve.tensor_tensor(x2[:], t_a[:], x1[:], ALU.add).then_inc(S["x2_ready"], 1)
                        stats_of([x2[:, j, :] for j in range(LC)], "x2_ready", b + 1, "stats", "mv", 3 * b + 3)
                        normalise(lambda j: x2[:, j, :], 3 * b + 3)
                        if f is not None:
                            output(f)

                    pipelined(dve, entry)


_INS = ['x', 'ctx_1024', 'L0_attn_rms_w', 'L0_attn_W_in', 'L0_attn_conv_w', 'L0_attn_conv_b', 'L0_attn_W_x',
        'L0_attn_W_dt', 'L0_attn_b_dt', 'L0_attn_A_log', 'L0_attn_Dp', 'L0_attn_W_out', 'L0_attn_ln_w',
        'L0_attn_ln_b', 'L0_xattn_igate_kernel', 'L0_xattn_igate_bias', 'L0_xattn_fgate_kernel',
        'L0_xattn_fgate_bias', 'L0_xattn_outnorm_scale', 'L0_ffn_w_gate', 'L0_ffn_w_up', 'L0_ffn_w_down']


def kernel(**inputs):
    import numpy as _np
    import concourse.bacc as _bacc
    from concourse import mybir as _mybir
    from concourse.bass_utils import run_bass_kernel_spmd as _run

    nc = _bacc.Bacc("TRN2", target_bir_lowering=False, num_devices=1)
    arrays, args = {}, []
    for name in _INS:
        a = _np.ascontiguousarray(inputs[name])
        arrays[f"in_{name}_dram"] = a
        args.append(nc.dram_tensor(f"in_{name}_dram", a.shape, _mybir.dt.from_np(a.dtype), kind="ExternalInput").ap())
    shape = inputs['x'].shape
    args.append(nc.dram_tensor("out_0_dram", shape, _mybir.dt.float32, kind="ExternalOutput").ap())
    build(nc, *args)
    r = _run(nc, [arrays], core_ids=[0])
    return r.results[0]["out_0_dram"]
```
